# Optimizing a Trainium2 kernel written in Bass

```python
import numpy as np
import jax
import jax.numpy as jnp

def _softmax(x, axis=-1):
    return jax.nn.softmax(x, axis=axis)

def _gelu(x):
    return jax.nn.gelu(x, approximate=True)

def _silu(x):
    return jax.nn.silu(x)

def _sigmoid(x):
    return jax.nn.sigmoid(x)

def _layernorm(x, axis=-1, eps=1e-05):
    m = jnp.mean(x, axis=axis, keepdims=True)
    v = jnp.var(x, axis=axis, keepdims=True)
    return (x - m) / jnp.sqrt(v + eps)

def _scatter_add(tgt, idx, src, axis=0):
    return tgt.at[idx].add(src)

def _segment_sum(src, seg, n):
    return jax.ops.segment_sum(src, seg, n)
kernel_name = 'mk_adaln_ffn_d2_seqx_r4_2fdb32'

def setup_inputs(seed: int=0):
    np.random.seed(seed)
    _w = jnp.asarray

    def _rec_inputs():
        import jax
        import jax.numpy as jnp
        _rk = jax.random.key(seed)
        x = -7.109e-05 + 0.9999 * jax.random.normal(jax.random.fold_in(_rk, 1), (64, 64, 512), jnp.float32)
        _lenS = 64 - jax.random.randint(jax.random.fold_in(_rk, 7), (64,), 0, max(1, 64 // 4) + 1, jnp.int32)
        _lenS2 = 64 - jax.random.randint(jax.random.fold_in(_rk, 8), (64,), 0, max(1, 64 // 4) + 1, jnp.int32)
        itok_B_1_198 = jax.random.randint(jax.random.fold_in(_rk, 11), (64,), 1, 199, jnp.int32)
        itok_B_0_6 = jax.random.randint(jax.random.fold_in(_rk, 12), (64,), 0, 7, jnp.int32)
        return (x, itok_B_1_198, itok_B_0_6)
    x, itok_B_1_198, itok_B_0_6 = _rec_inputs()

    def _L0_cond_setup():
        import jax, jax.numpy as jnp
        import numpy as np
        B, C, T = (128, 64, 512)
        S, D = (200, 64)
        key = jax.random.key(seed)
        k1, k2, k3 = jax.random.split(key, 3)
        x = jax.random.normal(k1, (B, C, T), dtype=jnp.float32)
        conditions = jax.random.randint(k2, (B,), 0, S, dtype=jnp.int64)
        weights = jax.random.normal(k3, (S, C, D), dtype=jnp.float32) / jnp.sqrt(jnp.float32(C))
        return {'x': x, 'conditions': conditions, 'weights': weights}
    _L0_cond_all = _L0_cond_setup()
    _L0_cond_in = {k: v for k, v in _L0_cond_all.items() if k in ('weights',)}
    del _L0_cond_all

    def _L0_ffn_setup():
        import jax, jax.numpy as jnp
        import numpy as np
        HIDDEN = 512
        INTER = 2048
        COMPRESSION = 128.9

        def _n_ctrl(out_size, in_size):
            return max(16, int(out_size * in_size / COMPRESSION))

        def _catmull_rom_grid(n_ctrl, n_samples):
            t = np.linspace(0.0, n_ctrl - 1.0, n_samples, dtype=np.float64)
            i = np.clip(np.floor(t).astype(np.int64), 0, n_ctrl - 2)
            f = (t - i).astype(np.float32)
            idx = np.stack([np.clip(i + k, 0, n_ctrl - 1) for k in (-1, 0, 1, 2)], axis=0)
            return (jnp.asarray(idx.astype(np.int32)), jnp.asarray(f))

        def spline_reconstruct(control_points, out_size, in_size):
            n = out_size * in_size
            idx, f = _catmull_rom_grid(control_points.shape[0], n)
            p0, p1, p2, p3 = (control_points[idx[0]], control_points[idx[1]], control_points[idx[2]], control_points[idx[3]])
            f2 = f * f
            f3 = f2 * f
            w = 0.5 * (2.0 * p1 + (p2 - p0) * f + (2.0 * p0 - 5.0 * p1 + 4.0 * p2 - p3) * f2 + (3.0 * p1 - p0 - 3.0 * p2 + p3) * f3)
            return w.reshape(out_size, in_size)
        key = jax.random.key(seed)
        k0, k1, k2, k3 = jax.random.split(key, 4)
        hidden_states = jax.random.normal(k0, (4, 512, HIDDEN), dtype=jnp.float32)
        gate_cp = jax.random.normal(k1, (_n_ctrl(INTER, HIDDEN),), dtype=jnp.float32) * 0.02
        up_cp = jax.random.normal(k2, (_n_ctrl(INTER, HIDDEN),), dtype=jnp.float32) * 0.02
        down_cp = jax.random.normal(k3, (_n_ctrl(HIDDEN, INTER),), dtype=jnp.float32) * 0.02
        return {'hidden_states': hidden_states, 'gate_cp': gate_cp, 'up_cp': up_cp, 'down_cp': down_cp}
    _L0_ffn_all = _L0_ffn_setup()
    _L0_ffn_in = {k: v for k, v in _L0_ffn_all.items() if k in ('gate_cp', 'up_cp', 'down_cp')}
    del _L0_ffn_all

    def _L1_cond_setup():
        import jax, jax.numpy as jnp
        import numpy as np
        B, T, D_IN, D_OUT = (16, 512, 512, 512)
        N_ADAPTERS, RANK = (8, 16)
        key = jax.random.key(seed)
        k_x, k_w, k_a, k_b, k_s, k_idx = jax.random.split(key, 6)
        x = jax.random.normal(k_x, (B, T, D_IN), dtype=jnp.float32)
        W = jax.random.normal(k_w, (D_OUT, D_IN), dtype=jnp.float32) * (1.0 / np.sqrt(D_IN))
        A = jax.random.normal(k_a, (N_ADAPTERS, RANK, D_IN), dtype=jnp.float32) * 0.02
        Bm = jax.random.normal(k_b, (N_ADAPTERS, D_OUT, RANK), dtype=jnp.float32) * 0.02
        scalings = jnp.ones((N_ADAPTERS,), dtype=jnp.float32)
        adapter_idx = jax.random.randint(k_idx, (B,), 0, N_ADAPTERS, dtype=jnp.int32)
        return {'x': x, 'W': W, 'A': A, 'Bm': Bm, 'scalings': scalings, 'adapter_idx': adapter_idx}
    _L1_cond_all = _L1_cond_setup()
    _L1_cond_in = {k: v for k, v in _L1_cond_all.items() if k in ('W', 'A', 'Bm', 'scalings')}
    del _L1_cond_all

    def _L1_ffn_setup():
        import jax, jax.numpy as jnp
        import numpy as np
        B, T, D = (1, 256, 512)
        F_DIM = 352
        E = 8
        TOPK = 2
        key = jax.random.key(seed)
        ks = jax.random.split(key, 5)
        x = jax.random.normal(ks[0], (B, T, D), dtype=jnp.float32)
        gate_w = jax.random.normal(ks[1], (E, D), dtype=jnp.float32) * 0.02
        gate_proj = jax.random.normal(ks[2], (E, F_DIM, D), dtype=jnp.float32) * 0.02
        up_proj = jax.random.normal(ks[3], (E, F_DIM, D), dtype=jnp.float32) * 0.02
        down_proj = jax.random.normal(ks[4], (E, D, F_DIM), dtype=jnp.float32) * 0.02
        return {'x': x, 'gate_w': gate_w, 'gate_proj': gate_proj, 'up_proj': up_proj, 'down_proj': down_proj}
    _L1_ffn_all = _L1_ffn_setup()
    _L1_ffn_in = {k: v for k, v in _L1_ffn_all.items() if k in ('gate_w', 'gate_proj', 'up_proj', 'down_proj')}
    del _L1_ffn_all
    return {'x': x, 'itok_B_1_198': itok_B_1_198, 'itok_B_0_6': itok_B_0_6, 'L0_cond_weights': _L0_cond_in['weights'], 'L0_ffn_gate_cp': _L0_ffn_in['gate_cp'], 'L0_ffn_up_cp': _L0_ffn_in['up_cp'], 'L0_ffn_down_cp': _L0_ffn_in['down_cp'], 'L1_cond_W': _L1_cond_in['W'], 'L1_cond_A': _L1_cond_in['A'], 'L1_cond_Bm': _L1_cond_in['Bm'], 'L1_cond_scalings': _L1_cond_in['scalings'], 'L1_ffn_gate_w': _L1_ffn_in['gate_w'], 'L1_ffn_gate_proj': _L1_ffn_in['gate_proj'], 'L1_ffn_up_proj': _L1_ffn_in['up_proj'], 'L1_ffn_down_proj': _L1_ffn_in['down_proj']}

def reference(x, itok_B_1_198, itok_B_0_6, L0_cond_weights, L0_ffn_gate_cp, L0_ffn_up_cp, L0_ffn_down_cp, L1_cond_W, L1_cond_A, L1_cond_Bm, L1_cond_scalings, L1_ffn_gate_w, L1_ffn_gate_proj, L1_ffn_up_proj, L1_ffn_down_proj):
    import jax
    import jax.numpy as jnp

    def _L0_cond_ref(x, conditions, weights):
        import jax, jax.numpy as jnp
        import numpy as np
        B, C, T = (128, 64, 512)
        S, D = (200, 64)
        w = weights[conditions]
        return jnp.einsum('bct,bcd->bdt', x, w)

    def _L0_ffn_ref(hidden_states, gate_cp, up_cp, down_cp):
        import jax, jax.numpy as jnp
        import numpy as np
        HIDDEN = 512
        INTER = 2048
        COMPRESSION = 128.9

        def _n_ctrl(out_size, in_size):
            return max(16, int(out_size * in_size / COMPRESSION))

        def _catmull_rom_grid(n_ctrl, n_samples):
            t = np.linspace(0.0, n_ctrl - 1.0, n_samples, dtype=np.float64)
            i = np.clip(np.floor(t).astype(np.int64), 0, n_ctrl - 2)
            f = (t - i).astype(np.float32)
            idx = np.stack([np.clip(i + k, 0, n_ctrl - 1) for k in (-1, 0, 1, 2)], axis=0)
            return (jnp.asarray(idx.astype(np.int32)), jnp.asarray(f))

        def spline_reconstruct(control_points, out_size, in_size):
            n = out_size * in_size
            idx, f = _catmull_rom_grid(control_points.shape[0], n)
            p0, p1, p2, p3 = (control_points[idx[0]], control_points[idx[1]], control_points[idx[2]], control_points[idx[3]])
            f2 = f * f
            f3 = f2 * f
            w = 0.5 * (2.0 * p1 + (p2 - p0) * f + (2.0 * p0 - 5.0 * p1 + 4.0 * p2 - p3) * f2 + (3.0 * p1 - p0 - 3.0 * p2 + p3) * f3)
            return w.reshape(out_size, in_size)
        gate_w = spline_reconstruct(gate_cp, INTER, HIDDEN)
        up_w = spline_reconstruct(up_cp, INTER, HIDDEN)
        down_w = spline_reconstruct(down_cp, HIDDEN, INTER)
        gate = jnp.einsum('bsh,ih->bsi', hidden_states, gate_w)
        up = jnp.einsum('bsh,ih->bsi', hidden_states, up_w)
        inter = jax.nn.silu(gate) * up
        return jnp.einsum('bsi,hi->bsh', inter, down_w)

    def _L1_cond_ref(x, W, A, Bm, scalings, adapter_idx):
        import jax, jax.numpy as jnp
        import numpy as np
        B, T, D_IN, D_OUT = (16, 512, 512, 512)
        N_ADAPTERS, RANK = (8, 16)
        H = jnp.einsum('btd,od->bto', x, W)
        A_b = A[adapter_idx]
        B_b = Bm[adapter_idx]
        s_b = scalings[adapter_idx]
        xa = jnp.einsum('btd,brd->btr', x, A_b)
        delta = jnp.einsum('btr,bor->bto', xa, B_b)
        delta = jax.lax.stop_gradient(delta * s_b[:, None, None])
        return H + delta

    def _L1_ffn_ref(x, gate_w, gate_proj, up_proj, down_proj):
        import jax, jax.numpy as jnp
        import numpy as np
        B, T, D = (1, 256, 512)
        F_DIM = 352
        E = 8
        TOPK = 2
        b, t, d = x.shape
        x_flat = x.reshape(-1, d)
        n = x_flat.shape[0]
        router_logits = x_flat @ gate_w.T
        top_w, sel = jax.lax.top_k(router_logits, TOPK)
        top_w = jax.nn.softmax(top_w, axis=-1)
        tok_ids = jnp.arange(n)[:, None]
        tw = jnp.zeros((n, E), dtype=x.dtype).at[tok_ids, sel].add(top_w)
        g = jnp.einsum('nd,efd->enf', x_flat, gate_proj)
        u = jnp.einsum('nd,efd->enf', x_flat, up_proj)
        h = jax.nn.silu(g) * u
        eo = jnp.einsum('enf,edf->end', h, down_proj)
        out = jnp.einsum('end,ne->nd', eo, tw)
        return out.reshape(b, t, d)
    x = x + _L0_ffn_ref(_L0_cond_ref(x, itok_B_1_198, L0_cond_weights), L0_ffn_gate_cp, L0_ffn_up_cp, L0_ffn_down_cp)
    x = x + _L1_ffn_ref(_L1_cond_ref(x, L1_cond_W, L1_cond_A, L1_cond_Bm, L1_cond_scalings, itok_B_0_6), L1_ffn_gate_w, L1_ffn_gate_proj, L1_ffn_up_proj, L1_ffn_down_proj)
    return x

_drawn_inputs = setup_inputs


def setup_inputs(seed=0):
    import zlib

    import numpy as np

    out = dict(_drawn_inputs(seed))
    spreads = {'L1_cond_scalings': (1.0, 0.6)}
    factors = {'L1_cond_A': 8.0, 'L1_cond_Bm': 8.0}
    for name, (base, spread) in spreads.items():
        noise = np.random.default_rng([zlib.crc32(name.encode()), seed]).standard_normal(out[name].shape)
        drawn = base * np.exp(spread * noise) if base else spread * noise
        out[name] = jnp.asarray(drawn.astype(out[name].dtype))
    for name, factor in factors.items():
        out[name] = (out[name] * factor).astype(out[name].dtype)
    return out
```

```python
from contextlib import ExitStack

import numpy as np

import concourse.bass as bass
from concourse import mybir

F32 = mybir.dt.float32
F32R = mybir.dt.float32r
I32 = mybir.dt.int32
U32 = mybir.dt.uint32
U8 = mybir.dt.uint8
ACT = mybir.ActivationFunctionType
ALU = mybir.AluOpType
AX = mybir.AxisListType

P = 128
BATCH, SEQ, D = 64, 64, 512
TOK = BATCH * SEQ
DK = D // P
INTER = 2048
IC = INTER // P
NCP = 8134
CPP = NCP + 10
PAD = 2
TILE = 256
NT = TOK // TILE
SUB = TILE // P
INNER = 4
LTILE = 512
LNT = TOK // LTILE
LSUB = LTILE // P
NSUB = TOK // P

GROUPS = 8
GROUP = INTER // GROUPS
PIECES, POW = 5, 4
KNOTS, KNOT_W, KNOT_GAP, KNOT_STEP = 4, 18, 129, 16
NPOLY = PIECES * POW
NRAW = KNOTS * KNOT_W
NF = NPOLY + NRAW
XW = 520
HALF = 64.0

NA, RANK = 8, 16
NE, FD = 8, 352
FC = 3
FP = FC * P
REM = FD - 2 * P
BLOCKS = 2 * TOK // P + NE - 1
COLS = BLOCKS + 2
TOKP = TOK + P
SLOTS = 3

GH, GL, UH, UL = (i * DK * FD for i in range(4))
DH_, DL_ = 4 * DK * FD, 4 * DK * FD + FC * D
EW = 4 * DK * FD + 2 * FC * D


def spline_constants():
    n = D * INTER
    t = np.linspace(0.0, NCP - 1.0, n, dtype=np.float64)
    iv = np.clip(np.floor(t).astype(np.int64), 0, NCP - 2)
    step = (NCP - 1.0) / (n - 1.0)
    base = 0.5 * np.array([[0, 2, 0, 0], [-1, 0, 1, 0], [2, -5, 4, -1], [-1, 3, -3, 1]], np.float64)

    def cubic(c, s):
        c = np.asarray(c)[..., None]
        return np.stack([base[0] + c * base[1] + c**2 * base[2] + c**3 * base[3],
                         s * (base[1] + 2 * c * base[2] + 3 * c**2 * base[3]),
                         s * s * (base[2] + 3 * c * base[3]),
                         s**3 * base[3] * np.ones_like(c)], -2)

    rt, ri = t.reshape(INTER, D), iv.reshape(INTER, D)
    j0 = ri[:, 0]
    order = np.argsort(j0 - rt[:, 0], kind="stable")
    mom = np.zeros((D, GROUPS, PIECES, POW))
    tabp = np.zeros((INTER, PIECES, POW, 4))
    tabr = np.zeros((INTER, KNOTS, KNOT_W, 5))
    for g in range(GROUPS):
        at = np.arange(g * GROUP, (g + 1) * GROUP)
        r = order[at]
        lo = [KNOT_STEP * g + KNOT_GAP * k for k in range(KNOTS)]
        for p in range(PIECES):
            a, b = ([0] + [x + KNOT_W for x in lo])[p], min((lo + [D])[p], D)
            if b <= a:
                continue
            c = (a + b - 1) / 2
            assert (ri[r, a:b] == (j0[r] + p)[:, None]).all()
            mom[a:b, g, p] = ((np.arange(a, b) - c) / HALF)[:, None] ** np.arange(POW)
            tabp[at, p] = cubic((r * D + c) * step - (j0[r] + p), HALF * step)
        for k in range(KNOTS):
            for w in range(KNOT_W):
                h = lo[k] + w
                if h >= D:
                    continue
                rel = ri[r, h] - j0[r] - k
                assert ((rel == 0) | (rel == 1)).all()
                weight = cubic(rt[r, h] - ri[r, h], 1.0)[:, 0]
                for q in (0, 1):
                    tabr[at[rel == q], k, w, q:q + 4] = weight[rel == q]

    nb = n // P
    b = np.arange(nb)
    jb = iv[b * P]
    jq = np.repeat(jb[::4], 4)
    c4 = b % 4
    tabd = np.zeros((nb, 2, POW, 5))
    for side in range(2):
        weight = cubic((b * P + (P - 1) / 2) * step - jb - side, HALF * step)
        for q in (0, 1):
            s = (jb - jq + 1 - c4) == q
            tabd[s, side, :, q:q + 4] = weight[s]
    assert np.isin(jb - jq + 1 - c4, (0, 1)).all()
    past = (iv.reshape(nb, P) > jb[:, None])
    assert (iv.reshape(nb, P) - jb[:, None] <= 1).all()
    v = ((np.arange(P) - (P - 1) / 2) / HALF)[None] ** np.arange(POW)[:, None]
    vh = np.rint(v * 2**11) / 2**11
    vl = v - vh
    pw = np.zeros((4, 2, 4, POW, 8, P))
    for c in range(4):
        for side in range(2):
            pw[c, side, :, :, 2 * c + side] = np.stack([vh, vl, vh, vl])

    f = lambda a: np.ascontiguousarray(a, dtype=np.float32)
    ints = lambda a: np.ascontiguousarray(a, dtype=np.int32)
    return {
        "c_order": ints(order.reshape(IC, P).T),
        "c_win_gu": ints((j0[order] + PAD - 1).reshape(IC, P).T),
        "c_win_d": ints((jb[::4] + PAD - 2).reshape(16, P).T),
        "c_mom": f(mom.reshape(DK, P, GROUPS * NPOLY).transpose(1, 0, 2)),
        "c_tabp": f(tabp.reshape(IC, P, PIECES, 16).transpose(1, 2, 0, 3).reshape(P, -1)),
        "c_tabr": f(tabr.reshape(IC, P, KNOTS, KNOT_W * 5).transpose(1, 2, 0, 3).reshape(P, -1)),
        "c_tabd": f(tabd.reshape(16, P, 4, 2, 20).transpose(1, 2, 3, 0, 4).reshape(P, -1)),
        "c_pw": f(pw.reshape(P, 8 * P)),
        "c_past": np.ascontiguousarray(past.reshape(16, P, 4, P).transpose(3, 2, 0, 1).reshape(P, -1).astype(np.int32)),
    }


def index_constants():
    p = np.arange(P)
    tok = (np.arange(NSUB)[None] * P + p[:, None]).astype(np.int32)
    small = np.zeros((P, 128), np.float32)
    small[:, 0] = p % 64
    small[:, 1] = p // RANK
    small[:, 8:16] = (p[:, None] // RANK == np.arange(NA))
    small[:, 16:24] = np.arange(NE)
    small[:, 24:24 + COLS] = np.arange(COLS)
    return {"c_tok": tok, "c_small": small,
            "c_no_entry": np.stack([np.repeat((TOK + p)[:, None], COLS, 1), np.zeros((P, COLS))], -1).astype(np.int32)}


def view(ap, offset, dims):
    return bass.AP(tensor=ap.tensor, offset=ap.offset + offset, ap=[list(ap.ap[0])] + [list(d) for d in dims])


def build(nc, io):
    kc = {k: v for k, v in io.items() if k.startswith("c_")}
    dram = lambda n, s, d=F32: nc.dram_tensor(n, s, d, kind="Internal").ap()
    cp_padded = dram("cp_padded", [3, CPP])
    down_natural = dram("down_natural", [INTER, D])
    expert_dram = dram("expert_dram", [NE, P, EW])
    z_dram = dram("z_dram", [TOKP, D])
    table_dram = dram("table_dram", [P * COLS, 2], I32)
    out = io["out"]
    x_flat = io["x"].rearrange("b c h -> (b c) h")
    layer_tiles = out[0:TOK, :].rearrange("(t s p) h -> t p s h", s=LSUB, p=P)
    x_tiles = x_flat.rearrange("(t s p) h -> t p s h", s=SUB, p=P)
    out_tiles = out[0:TOK, :].rearrange("(t s p) h -> t p s h", s=SUB, p=P)
    z_tiles = z_dram[0:TOK, :].rearrange("(t s p) h -> t p s h", s=LSUB, p=P)
    cond_rows = io["cond_w"].rearrange("n c d -> (n c) d")

    top = ExitStack()
    with top:
        def alloc(stack):
            def sb(name, shape, dt=F32):
                return stack.enter_context(nc.sbuf_tensor(name, shape, dt))
            return sb

        def sem(name):
            return top.enter_context(nc.semaphore(name))

        psum = [top.enter_context(nc.psum_tensor(f"bank{i}", [P, 512], F32)) for i in range(8)]
        sb = alloc(top)
        ident = sb("ident", [P, P])
        small = sb("small", [P, 128])
        tok_ids = sb("tok_ids", [P, NSUB], I32)
        logits = sb("logits", [P, NSUB, NE])
        idle = sb("idle", [P, 64])
        ident_set, ident_ready = sem("ident_set"), sem("ident_ready")

        layer = ExitStack()
        sbl = alloc(layer)
        w_hi = sbl("w_hi", [P, DK, D], F32R)
        w_lo = sbl("w_lo", [P, DK, D], F32R)
        a_hi = sbl("a_hi", [P, DK, P], F32R)
        a_lo = sbl("a_lo", [P, DK, P], F32R)
        b_hi = sbl("b_hi", [P, D], F32R)
        b_lo = sbl("b_lo", [P, D], F32R)
        r_hi = sbl("r_hi", [P, DK + 1, NE], F32R)
        r_lo = sbl("r_lo", [P, DK + 1, NE], F32R)
        adapter_scale = sbl("adapter_scale", [P, BATCH])
        main = ExitStack()
        sbm = alloc(main)
        gu_hi = sbm("gu_hi", [NF, 2, INTER], F32R)
        gu_lo = sbm("gu_lo", [NF, 2, INTER], F32R)
        mom = sbm("mom", [P, DK, GROUPS * NPOLY])
        cond_idx = sbm("cond_idx", [P, NSUB + 2 * SUB], I32)
        win_gu = sbm("win_gu", [P, 2, IC, 8])
        win_d = sbm("win_d", [P, 16, 9])
        order_idx = sbm("order_idx", [P, IC], I32)

        expert_weights(nc, io, kc, alloc, sem, psum, ident, ident_set, ident_ready, small, tok_ids,
                       expert_dram, cp_padded, win_gu, win_d, order_idx, table_dram, z_dram, out)
        first_weights(nc, io, kc, alloc, sem, psum, ident, small, mom, gu_hi, gu_lo,
                      w_hi, w_lo, a_hi, a_lo, b_hi, b_lo, r_hi, r_lo, adapter_scale, cond_idx, win_gu)
        down_hi = sbm("down_hi", [P, IC, D], F32R)
        down_lo = sbm("down_lo", [P, IC, D], F32R)
        down_weights(nc, kc, alloc, sem, psum, ident, win_d, order_idx, down_natural, down_hi, down_lo)
        first_ffn(nc, alloc, sem, psum, ident, small, idle, x_tiles, out_tiles, cond_rows, cond_idx, mom,
                  gu_hi, gu_lo, down_hi, down_lo)
        main.close()
        adapted_layer(nc, alloc, sem, psum, ident, layer_tiles, z_tiles, w_hi, w_lo, a_hi, a_lo, b_hi, b_lo,
                      r_hi, r_lo, adapter_scale, logits)
        layer.close()
        experts(nc, alloc, sem, psum, ident, small, idle, tok_ids, logits, expert_dram, table_dram, z_dram, out)


def expert_weights(nc, io, kc, alloc, sem, psum, ident, ident_set, ident_ready, small, tok_ids,
                   expert_dram, cp_padded, win_gu, win_d, order_idx, table_dram, z_dram, out):
    with ExitStack() as scope:
        sb = alloc(scope)
        raw_gu = [[sb(f"raw_{m}{b}", [P, FC, D]) for m in ("gate", "up")] for b in range(2)]
        raw_down = [sb(f"raw_down{b}", [P, DK, FD]) for b in range(2)]
        split = [sb(f"split{b}", [P, EW], F32R) for b in range(2)]
        idx_gu, idx_d = sb("idx_gu", [P, IC], I32), sb("idx_d", [P, 16], I32)
        zeros, no_entry = sb("zeros", [P, D]), sb("no_entry", [P, COLS, 2], I32)
        raw_loaded = [sem(f"raw_loaded{b}") for b in range(2)]
        split_stored = [sem(f"split_stored{b}") for b in range(2)]
        filled = [sem(f"ew_filled{i}") for i in range(4)]
        drained = [sem(f"ew_drained{i}") for i in range(4)]
        high_done = sem("ew_high_done")
        consts_loaded, no_entry_loaded = sem("consts_loaded"), sem("no_entry_loaded")
        cp_stored, win_loaded = sem("cp_stored"), sem("win_loaded")
        zeros_set, padding_stored = sem("zeros_set"), sem("padding_stored")
        USES = 2 * DK + FC
        PER = [len(range(i, USES, 4)) for i in range(4)]
        LAST = (USES - 1) % 4

        def use(u):
            if u < 2 * DK:
                m, c = u // DK, u % DK
                return P, FD, (GH, UH)[m] + c * FD, (GL, UL)[m] + c * FD
            f = u - 2 * DK
            return (P if f < 2 else REM), D, DH_ + f * D, DL_ + f * D

        with nc.Block() as block:
            @block.sync
            def _(sp):
                def load(e, b):
                    for m, name in enumerate(("gate_proj", "up_proj")):
                        src = io[name][bass.ds(e, 1)]
                        sp.dma_start(raw_gu[b][m][:, 0:2, :],
                                     src[:, 0:2 * P, :].rearrange("a (c p) d -> p (a c) d", p=P)).then_inc(raw_loaded[b], 16)
                        sp.dma_start(raw_gu[b][m][0:REM, 2, :],
                                     src[:, 2 * P:FD, :].rearrange("a p d -> p (a d)")).then_inc(raw_loaded[b], 16)
                    sp.dma_start(raw_down[b][:, :, :], io["down_proj"][bass.ds(e, 1)]
                                 .rearrange("a (c p) f -> p (a c) f", p=P)).then_inc(raw_loaded[b], 16)

                def store(e, b):
                    sp.wait_ge(drained[LAST], PER[LAST] * (e + 1) + 1)
                    sp.dma_start(expert_dram[bass.ds(e, 1)].rearrange("a p w -> p (a w)"),
                                 split[b][:, :].bitcast(F32)).then_inc(split_stored[b], 16)

                load(0, 0)
                load(1, 1)
                with sp.Fori(0, NE // 2 - 1) as k:
                    for b in range(2):
                        sp.wait_ge(filled[LAST], PER[LAST] * (2 * k + b + 1))
                        load(2 * k + b + 2, b)
                        store(2 * k + b, b)
                store(NE - 2, 0)
                store(NE - 1, 1)
                for b in range(2):
                    sp.wait_ge(split_stored[b], 16 * NE // 2)

            @block.gpsimd
            def _(pool):
                nc.gpsimd.memset(ident[:, :], 0.0).then_inc(ident_set, 1)
                pool.wait_ge(ident_set, 1)
                nc.gpsimd.affine_select(out=ident[:, :], in_=ident[:, :], compare_op=ALU.not_equal, fill=1.0,
                                        base=0, pattern=[[-1, P]], channel_multiplier=1).then_inc(ident_ready, 1)
                nc.gpsimd.memset(zeros[:, :], 0.0).then_inc(zeros_set, 1)
                pool.wait_ge(consts_loaded, 16 * 5)
                pool.wait_ge(cp_stored, 16 * 3 * (PAD + 3))
                flat = cp_padded.rearrange("m (a b) -> (m a) b", b=1)
                for m in range(2):
                    for q in range(IC):
                        nc.gpsimd.indirect_dma_start(win_gu[:, m, q, :], None, flat,
                                                     bass.IndirectOffsetOnAxis(ap=idx_gu[:, q:q + 1], axis=0),
                                                     element_offset=m * CPP).then_inc(win_loaded, 16)
                for q in range(16):
                    nc.gpsimd.indirect_dma_start(win_d[:, q, :], None, flat,
                                                 bass.IndirectOffsetOnAxis(ap=idx_d[:, q:q + 1], axis=0),
                                                 element_offset=2 * CPP).then_inc(win_loaded, 16)
                pool.wait_ge(win_loaded, 16 * (2 * IC + 16))

            @block.tensor
            def _(pe):
                pe.wait_ge(ident_ready, 1)
                with pe.Fori(0, NE // 2) as k:
                    for b in range(2):
                        e = 2 * k + b
                        pe.wait_ge(raw_loaded[b], 16 * 5 * (k + 1))
                        for u in range(USES):
                            i = u % 4
                            pe.wait_ge(drained[i], e * PER[i] + u // 4 + 1)
                            if u < 2 * DK:
                                m, c = u // DK, u % DK
                                for f in range(FC):
                                    rows = P if f < 2 else REM
                                    ins = nc.tensor.transpose(psum[i][:, f * P:f * P + rows],
                                                              raw_gu[b][m][0:rows, f, c * P:(c + 1) * P], ident[0:rows, 0:rows])
                            else:
                                f = u - 2 * DK
                                rows = P if f < 2 else REM
                                for c in range(DK):
                                    ins = nc.tensor.transpose(psum[i][0:rows, c * P:(c + 1) * P],
                                                              raw_down[b][:, c, f * P:f * P + rows], ident[:, :])
                            ins.then_inc(filled[i], 1)

            @block.scalar
            def _(act):
                act.dma_start(idx_gu[:, :], kc["c_win_gu"]).then_inc(consts_loaded, 16)
                act.dma_start(idx_d[:, :], kc["c_win_d"]).then_inc(consts_loaded, 16)
                act.dma_start(order_idx[:, :], kc["c_order"]).then_inc(consts_loaded, 16)
                act.dma_start(small[:, :], kc["c_small"]).then_inc(consts_loaded, 16)
                act.dma_start(tok_ids[:, :], kc["c_tok"]).then_inc(consts_loaded, 16)
                for m, name in enumerate(("gate_cp", "up_cp", "down_cp")):
                    cp = io[name].rearrange("(a n) -> a n", a=1)
                    to = cp_padded[m:m + 1, :]
                    act.dma_start(to[:, PAD:PAD + NCP], cp).then_inc(cp_stored, 16)
                    for i in range(PAD):
                        act.dma_start(to[:, i:i + 1], cp[:, 0:1]).then_inc(cp_stored, 16)
                    act.dma_start(to[:, PAD + NCP:PAD + NCP + 1], cp[:, NCP - 1:NCP]).then_inc(cp_stored, 16)
                    act.dma_start(to[:, PAD + NCP + 1:CPP], cp[:, 0:CPP - PAD - NCP - 1]).then_inc(cp_stored, 16)
                act.dma_start(no_entry[:, :, :], kc["c_no_entry"]).then_inc(no_entry_loaded, 16)
                act.wait_ge(zeros_set, 1)
                act.dma_start(z_dram[TOK:TOKP, :], zeros[:, :]).then_inc(padding_stored, 16)
                act.dma_start(out[TOK:TOKP, :], zeros[:, :]).then_inc(padding_stored, 16)
                act.wait_ge(no_entry_loaded, 16)
                act.dma_start(table_dram.rearrange("(p c) w -> p (c w)", p=P),
                              no_entry[:, :, :].rearrange("p c w -> p (c w)")).then_inc(padding_stored, 16)

                def high_parts(k, b, first):
                    e = 2 * k + b
                    if not first:
                        act.wait_ge(split_stored[b], 16 * k)
                    for u in range(USES):
                        rows, w, hi, _ = use(u)
                        act.wait_ge(filled[u % 4], e * PER[u % 4] + u // 4 + 1)
                        nc.scalar.activation(split[b][0:rows, hi:hi + w], psum[u % 4][0:rows, 0:w], ACT.Copy).then_inc(high_done, 1)

                for b in range(2):
                    high_parts(0, b, True)
                with act.Fori(1, NE // 2) as k:
                    for b in range(2):
                        high_parts(k, b, False)
                act.wait_ge(padding_stored, 48)

            @block.vector
            def _(dve):
                for i in range(4):
                    nc.vector.nop().then_inc(drained[i], 1)
                for b in range(2):
                    nc.vector.memset(split[b][REM:P, DH_ + 2 * D:DH_ + 3 * D].bitcast(F32), 0.0)
                    nc.vector.memset(split[b][REM:P, DL_ + 2 * D:DL_ + 3 * D].bitcast(F32), 0.0)
                with dve.Fori(0, NE // 2) as k:
                    for b in range(2):
                        e = 2 * k + b
                        for u in range(USES):
                            rows, w, hi, lo = use(u)
                            dve.wait_ge(high_done, e * USES + u + 1)
                            nc.vector.tensor_tensor(split[b][0:rows, lo:lo + w], psum[u % 4][0:rows, 0:w],
                                                    split[b][0:rows, hi:hi + w].bitcast(F32), ALU.subtract).then_inc(drained[u % 4], 1)


def first_weights(nc, io, kc, alloc, sem, psum, ident, small, mom, gu_hi, gu_lo,
                  w_hi, w_lo, a_hi, a_lo, b_hi, b_lo, r_hi, r_lo, adapter_scale, cond_idx, win_gu):
    with ExitStack() as scope:
        sb = alloc(scope)
        tabp = sb("tabp", [P, PIECES, IC, POW, 4])
        tabr = sb("tabr", [P, KNOTS, IC, KNOT_W, 5])
        prod = [sb(f"prod{b}", [P, IC, KNOT_W, 5]) for b in range(2)]
        rows_gu = sb("rows_gu", [P, 2, IC, NF])
        raw_w = sb("raw_w", [P, DK, D])
        raw_a = sb("raw_a", [P, D])
        raw_b = sb("raw_b", [P, DK, NA, RANK])
        raw_r = sb("raw_r", [NE, D])
        r_t = sb("r_t", [P, DK, NE])
        cond_i, cond_f = sb("cond_i", [P, BATCH], I32), sb("cond_f", [P, BATCH])
        adapt_i, adapt_f = sb("adapt_i", [P, BATCH], I32), sb("adapt_f", [P, BATCH])
        idx_f = sb("idx_f", [P, NSUB])
        scale_all, scale_own = sb("scale_all", [P, NA]), sb("scale_own", [P, 1])
        scale_pick = sb("scale_pick", [P, NA])
        tabs_loaded, raw_loaded, ints_loaded = sem("tabs_loaded"), sem("fw_raw_loaded"), sem("ints_loaded")
        step = sem("fw_step")
        NB = 4
        filled = [sem(f"fw_filled{i}") for i in range(NB)]
        drained = [sem(f"fw_drained{i}") for i in range(NB)]
        high_done, rows_done, rt_done = sem("fw_high_done"), sem("rows_done"), sem("rt_done")
        W_USE, A_USE, B_USE, RT_USE, R_USE, GU_USE = 0, DK, DK + 1, DK + 2, DK + 3, DK + 4
        USES = GU_USE + 2 * IC // 4

        def target(u):
            if u < A_USE:
                return w_hi[:, u, :], w_lo[:, u, :], P, D
            if u == A_USE:
                return (a_hi[:, :, :].rearrange("p k r -> p (k r)"), a_lo[:, :, :].rearrange("p k r -> p (k r)"), P, D)
            if u == B_USE:
                return b_hi[:, :], b_lo[:, :], P, D
            if u == R_USE:
                n = (DK + 1) * NE
                return (r_hi[:, :, :].rearrange("p k e -> p (k e)"), r_lo[:, :, :].rearrange("p k e -> p (k e)"), P, n)
            m, q = (u - GU_USE) // 4, (u - GU_USE) % 4
            return gu_hi[:, m, q * D:(q + 1) * D], gu_lo[:, m, q * D:(q + 1) * D], NF, D

        splits = [u for u in range(USES) if u != RT_USE]

        with nc.Block() as block:
            @block.sync
            def _(sp):
                sp.dma_start(raw_w[:, :, :], io["W"].rearrange("(c p) d -> p c d", p=P)).then_inc(raw_loaded, 16)
                sp.dma_start(raw_a[:, :], io["A"].rearrange("n r d -> (n r) d")).then_inc(raw_loaded, 16)
                for c in range(DK):
                    sp.dma_start(raw_b[:, c, :, :], io["Bm"][:, c * P:(c + 1) * P, :].rearrange("n p r -> p n r")).then_inc(raw_loaded, 16)
                sp.dma_start(raw_r[:, :], io["router_w"]).then_inc(raw_loaded, 16)

            @block.gpsimd
            def _(pool):
                pass

            @block.tensor
            def _(pe):
                pe.wait_ge(raw_loaded, 16 * (3 + DK))
                for u in range(USES):
                    i = u % NB
                    pe.wait_ge(drained[i], u // NB + 1)
                    bank = psum[i]
                    if u < A_USE:
                        for c in range(DK):
                            ins = nc.tensor.transpose(bank[:, c * P:(c + 1) * P], raw_w[:, c, u * P:(u + 1) * P], ident[:, :])
                    elif u == A_USE:
                        for c in range(DK):
                            ins = nc.tensor.transpose(bank[:, c * P:(c + 1) * P], raw_a[:, c * P:(c + 1) * P], ident[:, :])
                    elif u == B_USE:
                        for c in range(DK):
                            ins = nc.tensor.transpose(bank[:, c * P:(c + 1) * P],
                                                      raw_b[:, c, :, :].rearrange("p n r -> p (n r)"), ident[:, :])
                    elif u == RT_USE:
                        for c in range(DK):
                            ins = nc.tensor.transpose(bank[:, c * NE:(c + 1) * NE], raw_r[:, c * P:(c + 1) * P], ident[0:NE, 0:NE])
                    elif u == R_USE:
                        pe.wait_ge(rt_done, 1)
                        for k in range(DK):
                            for c in range(DK):
                                nc.tensor.matmul(bank[:, k * NE:(k + 1) * NE], raw_w[:, c, k * P:(k + 1) * P], r_t[:, c, :],
                                                 start=(c == 0), stop=(c == DK - 1))
                        for c in range(DK):
                            ins = nc.tensor.matmul(bank[:, DK * NE:(DK + 1) * NE], raw_b[:, c, :, :].rearrange("p n r -> p (n r)"),
                                                   r_t[:, c, :], start=(c == 0), stop=(c == DK - 1))
                    else:
                        m, q4 = (u - GU_USE) // 4, (u - GU_USE) % 4
                        pe.wait_ge(rows_done, m + 1)
                        for q in range(4):
                            ins = nc.tensor.transpose(bank[0:NF, q * P:(q + 1) * P], rows_gu[:, m, 4 * q4 + q, :], ident[:, :])
                    ins.then_inc(filled[i], 1)

            @block.scalar
            def _(act):
                act.dma_start(tabp[:, :, :, :, :].rearrange("p a b c d -> p (a b c d)"), kc["c_tabp"]).then_inc(tabs_loaded, 16)
                act.dma_start(tabr[:, :, :, :, :].rearrange("p a b c d -> p (a b c d)"), kc["c_tabr"]).then_inc(tabs_loaded, 16)
                act.dma_start(mom[:, :, :].rearrange("p k n -> p (k n)"), kc["c_mom"].rearrange("p k n -> p (k n)")).then_inc(tabs_loaded, 16)
                act.dma_start(cond_i[:, :], io["cond"].rearrange("(a n) -> a n", a=1).to_broadcast([P, BATCH])).then_inc(ints_loaded, 16)
                act.dma_start(adapt_i[:, :], io["adapter"].rearrange("(a n) -> a n", a=1).to_broadcast([P, BATCH])).then_inc(ints_loaded, 16)
                act.dma_start(scale_all[:, :], io["scalings"].rearrange("(a n) -> a n", a=1).to_broadcast([P, NA])).then_inc(ints_loaded, 16)
                for u in range(USES):
                    act.wait_ge(filled[u % NB], u // NB + 1)
                    if u == RT_USE:
                        nc.scalar.activation(r_t[:, :, :].rearrange("p c e -> p (c e)"), psum[u % NB][:, 0:DK * NE], ACT.Copy).then_inc(rt_done, 1)
                        act.wait_ge(rt_done, 1)
                        nc.scalar.nop().then_inc(drained[u % NB], 1)
                        continue
                    hi, _, rows, w = target(u)
                    nc.scalar.activation(hi, psum[u % NB][0:rows, 0:w], ACT.Copy).then_inc(high_done, 1)

            @block.vector
            def _(dve):
                for i in range(NB):
                    nc.vector.nop().then_inc(drained[i], 1)
                count = [0]

                def link(ins):
                    count[0] += 1
                    ins.then_inc(step, 1)
                    dve.wait_ge(step, count[0])

                def low_part(u):
                    hi, lo, rows, w = target(u)
                    dve.wait_ge(high_done, splits.index(u) + 1)
                    nc.vector.tensor_tensor(lo, psum[u % NB][0:rows, 0:w], hi.bitcast(F32), ALU.subtract).then_inc(drained[u % NB], 1)

                for u in range(RT_USE):
                    low_part(u)
                low_part(R_USE)
                dve.wait_ge(ints_loaded, 48)
                link(nc.vector.tensor_copy(cond_f[:, :], cond_i[:, :]))
                for half in range(2):
                    rows = slice(64 * half, 64 * half + 64)
                    last = nc.vector.tensor_scalar(idx_f[rows, :], cond_f[rows, half::2], 64.0, small[rows, 0:1], ALU.mult, ALU.add)
                    link(last)
                link(nc.vector.memset(cond_idx[:, NSUB:], 0))
                link(nc.vector.tensor_copy(cond_idx[:, 0:NSUB], idx_f[:, :]))
                link(nc.vector.tensor_copy(adapt_f[:, :], adapt_i[:, :]))
                link(nc.vector.tensor_tensor(scale_pick[:, :], scale_all[:, :], small[:, 8:8 + NA], ALU.mult))
                link(nc.vector.tensor_reduce(scale_own[:, :], scale_pick[:, :], AX.X, ALU.add))
                link(nc.vector.tensor_scalar(adapter_scale[:, :], adapt_f[:, :], small[:, 1:2], scale_own[:, 0:1], ALU.is_equal, ALU.mult))
                dve.wait_ge(tabs_loaded, 48)
                turn = 0
                for m in range(2):
                    for p in range(PIECES):
                        pr = prod[turn % 2][:, :, 0:POW, 0:4]
                        link(nc.vector.tensor_tensor(pr, tabp[:, p], view(win_gu[:, m], p, [[8, IC], [0, POW], [1, 4]]), ALU.mult))
                        last = nc.vector.tensor_reduce(rows_gu[:, m, :, p * POW:(p + 1) * POW], pr, AX.X, ALU.add)
                        turn += 1
                    for k in range(KNOTS):
                        pr = prod[turn % 2][:, :, :, :]
                        link(nc.vector.tensor_tensor(pr, tabr[:, k], view(win_gu[:, m], k, [[8, IC], [0, KNOT_W], [1, 5]]), ALU.mult))
                        last = nc.vector.tensor_reduce(rows_gu[:, m, :, NPOLY + k * KNOT_W:NPOLY + (k + 1) * KNOT_W], pr, AX.X, ALU.add)
                        turn += 1
                    last.then_inc(rows_done, 1)
                    for q in range(4):
                        if m == 1:
                            low_part(GU_USE + q)
                for q in range(4):
                    low_part(GU_USE + 4 + q)


def down_weights(nc, kc, alloc, sem, psum, ident, win_d, order_idx, down_natural, down_hi, down_lo):
    with ExitStack() as scope:
        sb = alloc(scope)
        tabd = sb("tabd", [P, 4, 2, 16, POW, 5])
        prod = [sb(f"dprod{b}", [P, 16, POW, 5]) for b in range(2)]
        coef = sb("coef", [P, 16, 8, POW])
        parts = sb("parts", [P, 16, 8, 4, POW])
        powers, powers_r = sb("powers", [P, 8, P]), sb("powers_r", [P, 8, P], F32R)
        past = sb("past", [P, 4, 4, 4 * P], U8)
        coef_t = sb("coef_t", [P, 4, 4 * P], F32R)
        dense = sb("dense", [P, IC, D])
        tabs_loaded, past_loaded, step = sem("dw_tabs_loaded"), sem("past_loaded"), sem("dw_step")
        past_ready = sem("past_ready")
        parts_hi, parts_done, powers_done = sem("parts_hi"), sem("parts_done"), sem("powers_done")
        t_filled, t_drained = [sem(f"dt_filled{i}") for i in range(2)], [sem(f"dt_drained{i}") for i in range(2)]
        filled, before, drained = ([sem(f"dw_{n}{i}") for i in range(3)] for n in ("filled", "before", "drained"))
        stored, gathered, high_done, low_done = sem("dense_stored"), sem("dense_gathered"), sem("dw_high_done"), sem("dw_low_done")

        with nc.Block() as block:
            @block.sync
            def _(sp):
                sp.dma_start(tabd[:, :, :, :, :, :].rearrange("p a b c d e -> p (a b c d e)"), kc["c_tabd"]).then_inc(tabs_loaded, 16)
                sp.dma_start(powers[:, :, :].rearrange("p a b -> p (a b)"), kc["c_pw"]).then_inc(tabs_loaded, 16)
                sp.dma_start(dense[:, :, :].rearrange("p a b -> p (a b)").bitcast(I32), kc["c_past"]).then_inc(past_loaded, 16)
                sp.wait_ge(drained[15 % 3], 16 // 3 + 2)
                sp.dma_start(down_natural.rearrange("(j s) h -> s j h", s=P), dense[:, :, :]).then_inc(stored, 16)
                sp.wait_ge(stored, 16)

            @block.gpsimd
            def _(pool):
                pool.wait_ge(stored, 16)
                for q in range(IC):
                    nc.gpsimd.indirect_dma_start(dense[:, q, :], None, down_natural,
                                                 bass.IndirectOffsetOnAxis(ap=order_idx[:, q:q + 1], axis=0)).then_inc(gathered, 16)
                pool.wait_ge(gathered, 16 * IC)

            @block.tensor
            def _(pe):
                pe.wait_ge(parts_done, 1)
                for g in range(4):
                    pe.wait_ge(t_drained[g % 2], g // 2 + 1)
                    for q in range(4):
                        ins = nc.tensor.transpose(psum[6 + g % 2][:, q * P:(q + 1) * P],
                                                  parts[:, 4 * g + q, :, :, :].rearrange("p a b c -> p (a b c)"), ident[:, :])
                    ins.then_inc(t_filled[g % 2], 1)
                pe.wait_ge(powers_done, 1)
                for n in range(16):
                    g, c, i = n // 4, n % 4, n % 3
                    pe.wait_ge(t_drained[g % 2], g // 2 + 2)
                    pe.wait_ge(drained[i], n // 3 + 1)
                    nc.tensor.matmul(psum[2 * i][:, :], powers_r[:, 2 * c, :], coef_t[:, g, :], start=True, stop=True)
                    nc.tensor.matmul(psum[2 * i + 1][:, :], powers_r[:, 2 * c + 1, :], coef_t[:, g, :],
                                     start=True, stop=True).then_inc(filled[i], 1)

            def place(n):
                g, c = n // 4, n % 4
                return view(dense[:, :, :], c * D + g * P, [[32, 4], [1, 32], [4 * D, 4]])

            @block.scalar
            def _(act):
                act.wait_ge(tabs_loaded, 32)
                nc.scalar.activation(powers_r[:, :, :], powers[:, :, :], ACT.Copy).then_inc(powers_done, 1)
                for g in range(4):
                    act.wait_ge(t_filled[g % 2], g // 2 + 1)
                    nc.scalar.activation(coef_t[:, g, :], psum[6 + g % 2][:, :], ACT.Copy).then_inc(t_drained[g % 2], 1)
                act.wait_ge(past_ready, 1)
                for n in range(16):
                    i = n % 3
                    act.wait_ge(filled[i], n // 3 + 1)
                    nc.scalar.activation(place(n), psum[2 * i][:, :].rearrange("p (a b c) -> p a b c", a=4, c=4),
                                         ACT.Copy).then_inc(before[i], 1)
                act.wait_ge(gathered, 16 * IC)
                for q in range(IC):
                    nc.scalar.activation(down_hi[:, q, :], dense[:, q, :], ACT.Copy).then_inc(high_done, 1)

            @block.vector
            def _(dve):
                for i in range(2):
                    nc.vector.nop().then_inc(t_drained[i], 1)
                for i in range(3):
                    nc.vector.nop().then_inc(drained[i], 1)
                count = [0]

                def link(ins):
                    count[0] += 1
                    ins.then_inc(step, 1)
                    dve.wait_ge(step, count[0])

                dve.wait_ge(tabs_loaded, 32)
                for c in range(4):
                    for side in range(2):
                        pr = prod[side][:, :, :, :]
                        link(nc.vector.tensor_tensor(pr, tabd[:, c, side], view(win_d[:, :, :], c + side, [[9, 16], [0, POW], [1, 5]]), ALU.mult))
                        last = nc.vector.tensor_reduce(coef[:, :, 2 * c + side, :], pr, AX.X, ALU.add)
                link(last)
                flat = coef[:, :, :, :].rearrange("p q c m -> p (q c) m")
                to = parts[:, :, :, :, :].rearrange("p q c r m -> p (q c) r m")
                for r in range(2):
                    link(nc.vector.tensor_copy(to[:, :, r, :].bitcast(F32R), flat))
                nc.vector.tensor_tensor(to[:, :, 2, :].bitcast(F32R), flat, to[:, :, 0, :], ALU.subtract)
                nc.vector.tensor_tensor(to[:, :, 3, :].bitcast(F32R), flat, to[:, :, 0, :], ALU.subtract).then_inc(parts_done, 1)
                dve.wait_ge(past_loaded, 16)
                nc.vector.tensor_copy(past[:, :, :, :].rearrange("p a b c -> p (a b c)"),
                                      dense[:, :, :].rearrange("p a b -> p (a b)").bitcast(I32)).then_inc(past_ready, 1)
                dve.wait_ge(past_ready, 1)
                for n in range(16):
                    i = n % 3
                    dve.wait_ge(before[i], n // 3 + 1)
                    nc.vector.copy_predicated(place(n), past[:, n % 4, n // 4, :].rearrange("p (a b c) -> p a b c", a=4, c=4),
                                              psum[2 * i + 1][:, :].rearrange("p (a b c) -> p a b c", a=4, c=4)).then_inc(drained[i], 1)
                for q in range(IC):
                    dve.wait_ge(high_done, q + 1)
                    last = nc.vector.tensor_tensor(down_lo[:, q, :], dense[:, q, :], down_hi[:, q, :].bitcast(F32), ALU.subtract)
                last.then_inc(low_done, 1)
                dve.wait_ge(low_done, 1)


def first_ffn(nc, alloc, sem, psum, ident, small, idle, x_tiles, out_tiles, cond_rows, cond_idx, mom,
              gu_hi, gu_lo, down_hi, down_lo):
    with ExitStack() as scope:
        sb = alloc(scope)
        x_in = sb("x_in", [P, SUB, XW])
        x_res = sb("x_res", [P, SUB, D])
        x_t = sb("x_t", [P, D])
        cond_now = sb("cond_now", [P, SUB], I32)
        cond_w = sb("cond_w", [P, SUB, SEQ])
        pair_hi, pair_lo = sb("pair_hi", [P, SUB, P], F32R), sb("pair_lo", [P, SUB, P], F32R)
        feat_hi, feat_lo = sb("feat_hi", [P, SUB, GROUPS, NF], F32R), sb("feat_lo", [P, SUB, GROUPS, NF], F32R)
        f_hi, f_lo = sb("f_hi", [NF, GROUPS, TILE], F32R), sb("f_lo", [NF, GROUPS, TILE], F32R)
        silu = [sb(f"silu{b}", [P, TILE]) for b in range(2)]
        inner = [sb(f"inner{b}", [P, TILE]) for b in range(INNER)]
        in_hi, in_lo = sb("in_hi", [P, IC, TILE], F32R), sb("in_lo", [P, IC, TILE], F32R)

        GATE, UP, OUT, PREP = [0, 1], [2, 3], [4, 5], 6
        FEAT = [GATE[0], UP[0], GATE[1], UP[1]]
        filled = [sem(f"filled{i}") for i in range(7)]
        drained = [sem(f"drained{i}") for i in range(7)]
        x_loaded, res_loaded, x1_stored = sem("x_loaded"), sem("res_loaded"), sem("x1_stored")
        pads_set, now_set = sem("pads_set"), sem("now_set")
        cond_loaded, pair_high, pair_done = sem("cond_loaded"), sem("pair_high"), sem("pair_done")
        mom_high, raw_high, f_high = (sem(n) for n in ("mom_high", "raw_high", "f_high"))
        in_high, in_done = sem("in_high"), sem("in_done")

        def use_feat(t, g):
            return 10 * t + g // 4

        def use_gu(t, c):
            return 10 * t + 2 + c // 2

        def use_out(t, s):
            return SUB // 2 * t + s // 2

        def use_prep(t, s, moments):
            return 2 * SUB * t + 2 * s + moments

        PREP_AT = {2 + 3 * i: (i // 2, i % 2) for i in range(2 * SUB)}

        def schedule(t, has_next, chunk, prep):
            for c in range(IC):
                chunk(t, c)
                if has_next and c in PREP_AT:
                    prep(t + 1, *PREP_AT[c])

        def steps(eng, body):
            body(0, True, False)
            with eng.Fori(1, NT - 1) as t:
                body(t, True, True)
            body(NT - 1, False, True)

        with nc.Block() as block:
            @block.sync
            def _(sp):
                def load_x(t):
                    sp.dma_start(x_in[:, :, 0:D], x_tiles[bass.ds(t, 1)].rearrange("a p s h -> p (a s) h")).then_inc(x_loaded, 16)

                def load_res(t):
                    sp.dma_start(x_res[:, :, :], x_tiles[bass.ds(t, 1)].rearrange("a p s h -> p (a s) h")).then_inc(res_loaded, 16)

                def store_x1(t):
                    for b in range(2):
                        sp.wait_ge(drained[OUT[b]], use_out(t, SUB - 2 + b) + 2)
                    sp.dma_start(out_tiles[bass.ds(t, 1)].rearrange("a p s h -> p (a s) h"), x_res[:, :, :]).then_inc(x1_stored, 16)

                def body(t, has_next, has_last):
                    if has_next:
                        sp.wait_ge(drained[PREP], use_prep(t, SUB - 1, 1) + 2)
                        load_x(t + 1)
                    if has_last:
                        sp.wait_ge(x1_stored, 16 * t)
                    load_res(t)
                    store_x1(t)

                load_x(0)
                steps(sp, body)
                sp.wait_ge(x1_stored, 16 * NT)

            @block.gpsimd
            def _(pool):
                nc.gpsimd.memset(x_in[:, :, D:XW], 0.0)
                nc.gpsimd.memset(pair_hi[:, :, :].bitcast(F32), 0.0)
                nc.gpsimd.memset(pair_lo[:, :, :].bitcast(F32), 0.0).then_inc(pads_set, 1)

                places = [0]

                def alone():
                    at = places[0]
                    places[0] += 1
                    nc.gpsimd.tensor_tensor(idle[:, at:at + 1], small[:, 0:1], small[:, 0:1], ALU.add)


                def gather_cond(t):
                    nc.gpsimd.tensor_copy(cond_now[:, :], cond_idx[:, bass.ds(SUB * t, SUB)]).then_inc(now_set, 1)
                    pool.wait_ge(now_set, t + 1)
                    alone()
                    for s in range(SUB):
                        nc.gpsimd.indirect_dma_start(cond_w[:, s, :], None, cond_rows,
                                                     bass.IndirectOffsetOnAxis(ap=cond_now[:, s:s + 1], axis=0)).then_inc(cond_loaded, 16)

                def body(t, gather):
                    for c in range(IC):
                        pool.wait_ge(in_high, IC * t + c + 1)
                        nc.gpsimd.tensor_tensor(in_lo[:, c, :], inner[c % INNER][:, :], in_hi[:, c, :].bitcast(F32), ALU.subtract).then_inc(in_done, 1)
                    if gather:
                        pool.wait_ge(pair_done, t + 2)
                        alone()
                        gather_cond(t + 2)

                gather_cond(0)
                pool.wait_ge(pair_done, 1)
                gather_cond(1)
                with pool.Fori(0, NT - 1) as t:
                    body(t, True)
                body(NT - 1, False)
                pool.wait_ge(cond_loaded, 16 * SUB * (NT + 1))

            @block.tensor
            def _(pe):
                def product(bank, pairs, last):
                    n = len(pairs)
                    for i, (lh, ll, rh, rl) in enumerate(pairs):
                        nc.tensor.matmul(bank, lh, rh, start=(i == 0), stop=False)
                        nc.tensor.matmul(bank, lh, rl, start=False, stop=False)
                        ins = nc.tensor.matmul(bank, ll, rh, start=False, stop=(i == n - 1))
                    if last is not None:
                        ins.then_inc(last, 1)

                def prep(t, s, moments):
                    n = use_prep(t, s, moments)
                    if not moments:
                        if s == 0:
                            pe.wait_ge(x_loaded, 16 * (t + 1))
                    pe.wait_ge(drained[PREP], n + 1)
                    for k in range(DK):
                        if moments:
                            ins = nc.tensor.matmul(psum[PREP][:, 0:GROUPS * NPOLY], x_t[:, k * P:(k + 1) * P], mom[:, k, :],
                                                   start=(k == 0), stop=(k == DK - 1))
                        else:
                            ins = nc.tensor.transpose(psum[PREP][:, k * P:(k + 1) * P], x_in[:, s, k * P:(k + 1) * P], ident[:, :])
                    ins.then_inc(filled[PREP], 1)

                def features(t):
                    pe.wait_ge(drained[PREP], use_prep(t, SUB - 1, 1) + 2)
                    pe.wait_ge(pair_done, t + 1)
                    for g in range(GROUPS):
                        bank = FEAT[g % 4]
                        pe.wait_ge(drained[bank], use_feat(t, g) + 1)
                        for s in range(SUB):
                            product(psum[bank][0:NF, s * P:(s + 1) * P],
                                    [(feat_hi[:, s, g, :], feat_lo[:, s, g, :], pair_hi[:, s, :], pair_lo[:, s, :])],
                                    filled[bank] if s == SUB - 1 else None)

                def chunk(t, c):
                    g = c * P // GROUP
                    for m, bank in enumerate((GATE[c % 2], UP[c % 2])):
                        pe.wait_ge(drained[bank], use_gu(t, c) + 1)
                        cols = slice(c * P, (c + 1) * P)
                        product(psum[bank][:, 0:TILE], [(gu_hi[:, m, cols], gu_lo[:, m, cols], f_hi[:, g, :], f_lo[:, g, :])], filled[bank])

                def down(t, s):
                    bank = OUT[s % 2]
                    pe.wait_ge(drained[bank], use_out(t, s) + 1)
                    rows = slice(s * P, (s + 1) * P)
                    for c in range(IC):
                        if s == 0:
                            pe.wait_ge(in_done, IC * t + c + 1)
                        nc.tensor.matmul(psum[bank][:, :], in_hi[:, c, rows], down_hi[:, c, :], start=(c == 0), stop=False)
                        nc.tensor.matmul(psum[bank][:, :], in_hi[:, c, rows], down_lo[:, c, :], start=False, stop=False)
                        ins = nc.tensor.matmul(psum[bank][:, :], in_lo[:, c, rows], down_hi[:, c, :], start=False, stop=(c == IC - 1))
                    ins.then_inc(filled[bank], 1)

                def body(t, has_next, _):
                    schedule(t, has_next, chunk, prep)
                    if has_next:
                        features(t + 1)
                    for s in range(SUB):
                        down(t, s)

                for s in range(SUB):
                    prep(0, s, 0)
                    prep(0, s, 1)
                features(0)
                steps(pe, body)

            @block.scalar
            def _(act):
                def pairs(t):
                    act.wait_ge(cond_loaded, 16 * SUB * (t + 1))
                    for half in range(2):
                        rows = slice(64 * half, 64 * half + 64)
                        ins = nc.scalar.activation(pair_hi[rows, :, rows], cond_w[rows, :, :], ACT.Copy)
                    ins.then_inc(pair_high, 1)

                def raw(s):
                    return view(x_in[:, :, :], s * XW, [[KNOT_STEP, GROUPS], [KNOT_GAP, KNOTS], [1, KNOT_W]])

                def prep(t, s, moments):
                    act.wait_ge(filled[PREP], use_prep(t, s, moments) + 1)
                    if not moments:
                        if s == 0:
                            pairs(t)
                        nc.scalar.activation(x_t[:, :], psum[PREP][:, :], ACT.Copy).then_inc(drained[PREP], 1)
                        nc.scalar.activation(feat_hi[:, s, :, NPOLY:NF].rearrange("p g (k w) -> p g k w", k=KNOTS), raw(s),
                                             ACT.Copy).then_inc(raw_high, 1)
                    else:
                        nc.scalar.activation(feat_hi[:, s, :, 0:NPOLY], psum[PREP][:, 0:GROUPS * NPOLY].rearrange("p (g n) -> p g n", g=GROUPS),
                                             ACT.Copy).then_inc(mom_high, 1)

                def features(t):
                    for g in range(GROUPS):
                        bank = FEAT[g % 4]
                        act.wait_ge(filled[bank], use_feat(t, g) + 1)
                        nc.scalar.activation(f_hi[:, g, :], psum[bank][0:NF, 0:TILE], ACT.Copy).then_inc(f_high, 1)

                def chunk(t, c):
                    act.wait_ge(filled[GATE[c % 2]], use_gu(t, c) + 1)
                    act.wait_ge(drained[UP[c % 2]], use_gu(t, c) + 1)
                    nc.scalar.activation(silu[c % 2][:, :], psum[GATE[c % 2]][:, 0:TILE], ACT.Silu).then_inc(drained[GATE[c % 2]], 1)

                def body(t, has_next, _):
                    schedule(t, has_next, chunk, prep)
                    if has_next:
                        features(t + 1)

                act.wait_ge(pads_set, 1)
                for s in range(SUB):
                    prep(0, s, 0)
                    prep(0, s, 1)
                features(0)
                steps(act, body)

            @block.vector
            def _(dve):
                for i in range(7):
                    nc.vector.nop().then_inc(drained[i], 1)

                def pairs(t):
                    dve.wait_ge(pair_high, t + 1)
                    for half in range(2):
                        rows = slice(64 * half, 64 * half + 64)
                        ins = nc.vector.tensor_tensor(pair_lo[rows, :, rows], cond_w[rows, :, :], pair_hi[rows, :, rows].bitcast(F32), ALU.subtract)
                    ins.then_inc(pair_done, 1)

                def prep(t, s, moments):
                    if not moments:
                        if s == 0:
                            pairs(t)
                        dve.wait_ge(raw_high, SUB * t + s + 1)
                        raw = view(x_in[:, :, :], s * XW, [[KNOT_STEP, GROUPS], [KNOT_GAP, KNOTS], [1, KNOT_W]])
                        part = lambda f: f[:, s, :, NPOLY:NF].rearrange("p g (k w) -> p g k w", k=KNOTS)
                        nc.vector.tensor_tensor(part(feat_lo), raw, part(feat_hi).bitcast(F32), ALU.subtract)
                    else:
                        dve.wait_ge(mom_high, SUB * t + s + 1)
                        nc.vector.tensor_tensor(feat_lo[:, s, :, 0:NPOLY], psum[PREP][:, 0:GROUPS * NPOLY].rearrange("p (g n) -> p g n", g=GROUPS),
                                                feat_hi[:, s, :, 0:NPOLY].bitcast(F32), ALU.subtract).then_inc(drained[PREP], 1)

                def features(t):
                    for g in range(GROUPS):
                        bank = FEAT[g % 4]
                        dve.wait_ge(f_high, GROUPS * t + g + 1)
                        nc.vector.tensor_tensor(f_lo[:, g, :], psum[bank][0:NF, 0:TILE], f_hi[:, g, :].bitcast(F32), ALU.subtract).then_inc(drained[bank], 1)

                def high_inner(t, c):
                    dve.wait_ge(drained[UP[c % 2]], use_gu(t, c) + 2)
                    nc.vector.tensor_copy(in_hi[:, c, :], inner[c % INNER][:, :]).then_inc(in_high, 1)

                def chunk(t, c):
                    dve.wait_ge(drained[GATE[c % 2]], use_gu(t, c) + 2)
                    dve.wait_ge(filled[UP[c % 2]], use_gu(t, c) + 1)
                    if not isinstance(t, int) or t > 0 or c >= INNER:
                        dve.wait_ge(in_done, IC * t + c - INNER + 1)
                    nc.vector.tensor_tensor(inner[c % INNER][:, :], silu[c % 2][:, :], psum[UP[c % 2]][:, 0:TILE], ALU.mult).then_inc(drained[UP[c % 2]], 1)
                    if c > 0:
                        high_inner(t, c - 1)
                    if c == IC - 1:
                        high_inner(t, c)

                def add(t, s):
                    dve.wait_ge(filled[OUT[s % 2]], use_out(t, s) + 1)
                    if s == 0:
                        dve.wait_ge(res_loaded, 16 * (t + 1))
                    nc.vector.tensor_tensor(x_res[:, s, :], psum[OUT[s % 2]][:, :], x_res[:, s, :], ALU.add).then_inc(drained[OUT[s % 2]], 1)

                def body(t, has_next, _):
                    schedule(t, has_next, chunk, prep)
                    if has_next:
                        features(t + 1)
                    for s in range(SUB):
                        add(t, s)

                dve.wait_ge(pads_set, 1)
                for s in range(SUB):
                    prep(0, s, 0)
                    prep(0, s, 1)
                features(0)
                steps(dve, body)


def adapted_layer(nc, alloc, sem, psum, ident, layer_tiles, z_tiles, w_hi, w_lo, a_hi, a_lo, b_hi, b_lo,
                  r_hi, r_lo, adapter_scale, logits):
    with ExitStack() as scope:
        sb = alloc(scope)
        x1 = [sb(f"x1_{b}", [P, LSUB, D]) for b in range(2)]
        x1t_hi = [sb(f"x1t_hi{b}", [P, DK, LTILE], F32R) for b in range(2)]
        x1t_lo = [sb(f"x1t_lo{b}", [P, DK, LTILE], F32R) for b in range(2)]
        xa = sb("xa", [P, LTILE])
        xa_hi, xa_lo = sb("xa_hi", [P, LTILE], F32R), sb("xa_lo", [P, LTILE], F32R)
        z_out = [sb(f"z_out{b}", [P, LSUB, D]) for b in range(2)]

        X1T, XA, LOGITS, Z = [0, 1], 2, 3, [4, 5, 6, 7]
        filled = [sem(f"al_filled{i}") for i in range(8)]
        drained = [sem(f"al_drained{i}") for i in range(8)]
        x1_loaded, z_stored = [[sem(f"al_{n}{b}") for b in range(2)] for n in ("x1_loaded", "z_stored")]
        x1t_high, xa_high, xa_done = sem("x1t_high"), sem("xa_high"), sem("xa_done")

        def use_x1t(t, s):
            return LSUB // 2 * t + s // 2

        def pairs_of_steps(eng, body):
            body(0, 0, 0, True, True)
            body(1, 0, 1, True, True)
            with eng.Fori(1, LNT // 2 - 1) as k:
                for b in range(2):
                    body(2 * k + b, k, b, True, False)
            body(LNT - 2, LNT // 2 - 1, 0, True, False)
            body(LNT - 1, LNT // 2 - 1, 1, False, False)

        with nc.Block() as block:
            @block.sync
            def _(sp):
                def load(t, b):
                    sp.dma_start(x1[b][:, :, :], layer_tiles[bass.ds(t, 1)].rearrange("a p s h -> p (a s) h")).then_inc(x1_loaded[b], 16)

                def body(t, n, b, has_next, first):
                    if has_next:
                        if not (first and b == 0):
                            sp.wait_ge(filled[X1T[1]], use_x1t(t - 1, LSUB - 1) + 1)
                        load(t + 1, 1 - b)
                    for s in range(LSUB):
                        sp.wait_ge(drained[Z[s]], t + 2)
                    sp.dma_start(z_tiles[bass.ds(t, 1)].rearrange("a p s h -> p (a s) h"), z_out[b][:, :, :]).then_inc(z_stored[b], 16)

                load(0, 0)
                pairs_of_steps(sp, body)
                for b in range(2):
                    sp.wait_ge(z_stored[b], 16 * LNT // 2)

            @block.gpsimd
            def _(pool):
                pass

            @block.tensor
            def _(pe):
                def product(bank, pairs, last):
                    n = len(pairs)
                    for i, (lh, ll, rh, rl) in enumerate(pairs):
                        nc.tensor.matmul(bank, lh, rh, start=(i == 0), stop=False)
                        nc.tensor.matmul(bank, lh, rl, start=False, stop=False)
                        ins = nc.tensor.matmul(bank, ll, rh, start=False, stop=(i == n - 1))
                    if last is not None:
                        ins.then_inc(last, 1)

                def transpose(t, n, b):
                    pe.wait_ge(x1_loaded[b], 16 * (n + 1))
                    for s in range(LSUB):
                        bank = X1T[s % 2]
                        pe.wait_ge(drained[bank], use_x1t(t, s) + 1)
                        for k in range(DK):
                            ins = nc.tensor.transpose(psum[bank][:, k * P:(k + 1) * P], x1[b][:, s, k * P:(k + 1) * P], ident[:, :])
                        ins.then_inc(filled[bank], 1)

                def body(t, n, b, has_next, first):
                    for s in (LSUB - 2, LSUB - 1):
                        pe.wait_ge(drained[X1T[s % 2]], use_x1t(t, s) + 2)
                    hi, lo = x1t_hi[b], x1t_lo[b]
                    pe.wait_ge(drained[XA], t + 1)
                    product(psum[XA][:, :], [(a_hi[:, k, :], a_lo[:, k, :], hi[:, k, :], lo[:, k, :]) for k in range(DK)], filled[XA])
                    if has_next:
                        transpose(t + 1, n + b, 1 - b)
                    pe.wait_ge(xa_done, t + 1)
                    for s in range(LSUB):
                        rows = slice(s * P, (s + 1) * P)
                        pe.wait_ge(drained[Z[s]], t + 1)
                        product(psum[Z[s]][:, :], [(hi[:, k, rows], lo[:, k, rows], w_hi[:, k, :], w_lo[:, k, :]) for k in range(DK)]
                                + [(xa_hi[:, rows], xa_lo[:, rows], b_hi[:, :], b_lo[:, :])], filled[Z[s]])
                    pe.wait_ge(drained[LOGITS], t + 1)
                    for s in range(LSUB):
                        rows = slice(s * P, (s + 1) * P)
                        product(psum[LOGITS][:, s * NE:(s + 1) * NE],
                                [(hi[:, k, rows], lo[:, k, rows], r_hi[:, k, :], r_lo[:, k, :]) for k in range(DK)]
                                + [(xa_hi[:, rows], xa_lo[:, rows], r_hi[:, DK, :], r_lo[:, DK, :])],
                                filled[LOGITS] if s == LSUB - 1 else None)

                transpose(0, 0, 0)
                pairs_of_steps(pe, body)

            @block.scalar
            def _(act):
                def transpose(t, b):
                    for s in range(LSUB):
                        act.wait_ge(filled[X1T[s % 2]], use_x1t(t, s) + 1)
                        nc.scalar.activation(x1t_hi[b][:, :, s * P:(s + 1) * P], psum[X1T[s % 2]][:, :].rearrange("p (k n) -> p k n", k=DK),
                                             ACT.Copy).then_inc(x1t_high, 1)

                def body(t, n, b, has_next, first):
                    act.wait_ge(drained[XA], t + 2)
                    nc.scalar.activation(xa_hi[:, :], xa[:, :], ACT.Copy).then_inc(xa_high, 1)
                    if has_next:
                        transpose(t + 1, 1 - b)
                    if not first:
                        act.wait_ge(z_stored[b], 16 * n)
                    for s in range(LSUB):
                        act.wait_ge(filled[Z[s]], t + 1)
                        nc.scalar.activation(z_out[b][:, s, :], psum[Z[s]][:, :], ACT.Copy).then_inc(drained[Z[s]], 1)

                transpose(0, 0)
                pairs_of_steps(act, body)

            @block.vector
            def _(dve):
                for i in range(8):
                    nc.vector.nop().then_inc(drained[i], 1)

                def transpose(t, b):
                    for s in range(LSUB):
                        cols = slice(s * P, (s + 1) * P)
                        dve.wait_ge(x1t_high, LSUB * t + s + 1)
                        nc.vector.tensor_tensor(x1t_lo[b][:, :, cols], psum[X1T[s % 2]][:, :].rearrange("p (k n) -> p k n", k=DK),
                                                x1t_hi[b][:, :, cols].bitcast(F32), ALU.subtract).then_inc(drained[X1T[s % 2]], 1)

                def body(t, n, b, has_next, first):
                    dve.wait_ge(filled[XA], t + 1)
                    batches = LTILE // SEQ
                    own = adapter_scale[:, bass.ds(batches * t, batches)]
                    nc.vector.tensor_tensor(xa[:, :].rearrange("p (b c) -> p b c", b=batches), psum[XA][:, :].rearrange("p (b c) -> p b c", b=batches),
                                            own.rearrange("p (b c) -> p b c", c=1).to_broadcast([P, batches, SEQ]), ALU.mult).then_inc(drained[XA], 1)
                    dve.wait_ge(xa_high, t + 1)
                    nc.vector.tensor_tensor(xa_lo[:, :], xa[:, :], xa_hi[:, :].bitcast(F32), ALU.subtract).then_inc(xa_done, 1)
                    if has_next:
                        transpose(t + 1, 1 - b)
                    dve.wait_ge(filled[LOGITS], t + 1)
                    nc.vector.tensor_copy(logits[:, bass.ds(LSUB * t, LSUB), :],
                                          psum[LOGITS][:, 0:LSUB * NE].rearrange("p (s e) -> p s e", s=LSUB)).then_inc(drained[LOGITS], 1)

                transpose(0, 0)
                pairs_of_steps(dve, body)


def experts(nc, alloc, sem, psum, ident, small, idle, tok_ids, logits, expert_dram, table_dram, z_dram, out):
    with ExitStack() as scope:
        sb = alloc(scope)
        slots = sb("slots", [P, SLOTS, EW], F32R)
        lower, ones = sb("lower", [P, P]), sb("ones", [P, P])
        top1, top2, at = sb("top1", [P, NSUB]), sb("top2", [P, NSUB]), sb("at", [P, NSUB])
        below, masked = sb("below", [P, NSUB, NE]), sb("masked", [P, NSUB, NE])
        picked = [sb(f"picked{k}", [P, NSUB, NE]) for k in range(2)]
        both, pos = sb("both", [P, NSUB, NE]), sb("pos", [P, NSUB, NE])
        own_total = sb("own_total", [P, NSUB, NE])
        totals = [sb(f"totals{b}", [P, NSUB, NE]) for b in range(2)]
        count, blocks_from = sb("count", [P, NE]), sb("blocks_from", [P, NSUB])
        full_blocks = sb("full_blocks", [P, NE, NSUB])
        ends = [sb(f"ends{b}", [P, NE]) for b in range(2)]
        n_blocks, start = sb("n_blocks", [P, NE]), sb("start", [P, NE])
        slot_f, slot_i = sb("slot_f", [P, 2, NSUB]), sb("slot_i", [P, 2, NSUB], I32)
        low_i, high_i = sb("low_i", [P, 2, NSUB], I32), sb("high_i", [P, 2, NSUB], I32)
        low_f, high_f, row_f = sb("low_f", [P, 2, NSUB]), sb("high_f", [P, 2, NSUB]), sb("row_f", [P, 2, NSUB])
        row_i = sb("row_i", [P, 2, NSUB], I32)
        gap, share = sb("gap", [P, NSUB]), sb("share", [P, 2, NSUB])
        expo, total = sb("expo", [P, NSUB]), sb("total", [P, NSUB])
        entry = sb("entry", [P, NSUB, 2, 2], I32)
        past_end = sb("past_end", [P, COLS, NE - 1])
        expert_f, wrapped = sb("expert_f", [P, COLS]), sb("wrapped", [P, COLS])
        ctl_f = sb("ctl_f", [P, 2 * COLS + NE])
        ctl = sb("ctl", [P, 2 * COLS + NE], I32)
        table = sb("table", [P, COLS, 2], I32)
        z_now = [sb(f"z_now{b}", [P, D]) for b in range(2)]
        gather_at = [sb(f"gather_at{b}", [P, 1], I32) for b in range(2)]
        scatter_at = [sb(f"scatter_at{b}", [P, 2], I32) for b in range(2)]
        zt_hi, zt_lo = sb("zt_hi", [P, DK, P], F32R), sb("zt_lo", [P, DK, P], F32R)
        silu_g, hid = sb("silu_g", [P, FD]), sb("hid", [P, FP])
        ht_hi, ht_lo = sb("ht_hi", [P, FC, P], F32R), sb("ht_lo", [P, FC, P], F32R)
        result = [sb(f"result{b}", [P, D]) for b in range(2)]

        step, masks_set, masks_ready = sem("route_step"), sem("masks_set"), sem("masks_ready")
        both_ready, ranks_filled = sem("both_ready"), sem("ranks_filled")
        gap_ready, expo_ready = sem("gap_ready"), sem("expo_ready")
        entries_ready, entries_stored, table_loaded = sem("entries_ready"), sem("entries_stored"), sem("table_loaded")
        ctl_ready, weights_loaded = sem("ctl_ready"), sem("weights_loaded")
        ZT, GATE, UP, HT, OUT, RANKS, TOTALS = 0, 1, 2, 3, [4, 5], 6, 7
        filled = [sem(f"ex_filled{i}") for i in range(6)]
        drained = [sem(f"ex_drained{i}") for i in range(6)]
        z_loaded = [sem(f"ex_z_loaded{b}") for b in range(2)]
        zt_high, ht_high = sem("zt_high"), sem("ht_high")
        gather_set, scatter_set, added = sem("gather_set"), sem("scatter_set"), sem("added")

        with nc.Block() as block:
            @block.sync
            def _(sp):
                for e in range(NE):
                    if e >= SLOTS:
                        if e == SLOTS:
                            sp.wait_ge(ctl_ready, 1)
                        end = 2 * COLS + e - SLOTS
                        blocks = sp.value_load(ctl[0:1, end:end + 1], min_val=1, max_val=BLOCKS)
                        sp.wait_ge(filled[HT], blocks + 1)
                    sp.dma_start(slots[:, e % SLOTS, :].bitcast(F32), expert_dram[e]).then_inc(weights_loaded, 16)
                    sp.wait_ge(weights_loaded, 16 * (e + 1))

            @block.gpsimd
            def _(pool):
                nc.gpsimd.memset(lower[:, :], 1.0).then_inc(masks_set, 1)
                nc.gpsimd.memset(ones[:, :], 1.0).then_inc(masks_set, 1)
                nc.gpsimd.memset(hid[:, :], 0.0).then_inc(masks_set, 1)
                pool.wait_ge(masks_set, 1)
                nc.gpsimd.affine_select(out=lower[:, :], in_=lower[:, :], compare_op=ALU.is_gt, fill=0.0,
                                        base=0, pattern=[[1, P]], channel_multiplier=-1).then_inc(masks_ready, 1)
                pool.wait_ge(entries_ready, 1)
                for k in range(2):
                    for n in range(NSUB):
                        nc.gpsimd.indirect_dma_start(table_dram, bass.IndirectOffsetOnAxis(ap=row_i[:, k, n:n + 1], axis=0),
                                                     entry[:, n, k, :], None).then_inc(entries_stored, 16)
                pool.wait_ge(entries_stored, 16 * 2 * NSUB)
                nc.gpsimd.dma_start(table[:, :, :].rearrange("p c w -> p (c w)"),
                                    table_dram.rearrange("(p c) w -> p (c w)", p=P)).then_inc(table_loaded, 16)
                pool.wait_ge(table_loaded, 16)

                places = [0]

                def alone():
                    at = places[0]
                    places[0] += 1
                    nc.gpsimd.tensor_tensor(idle[:, at:at + 1], small[:, 0:1], small[:, 0:1], ALU.add)


                def gather(j, b):
                    nc.gpsimd.tensor_copy(gather_at[b][:, :], table[:, bass.ds(j, 1), 0:1].rearrange("p a b -> p (a b)")).then_inc(gather_set, 1)
                    pool.wait_ge(gather_set, j + 1)
                    alone()
                    nc.gpsimd.indirect_dma_start(z_now[b][:, :], None, z_dram,
                                                 bass.IndirectOffsetOnAxis(ap=gather_at[b][:, 0:1], axis=0)).then_inc(z_loaded[b], 16)

                def set_scatter(j, b):
                    nc.gpsimd.tensor_copy(scatter_at[b][:, :], table[:, bass.ds(j, 1), :].rearrange("p a b -> p (a b)")).then_inc(scatter_set, 1)

                def scatter(j, n, b, first):
                    if not first:
                        pool.wait_ge(added, 16 * j)
                        alone()
                    pool.wait_ge(drained[OUT[b]], n + 2)
                    alone()
                    nc.gpsimd.indirect_dma_start(out, bass.IndirectOffsetOnAxis(ap=scatter_at[b][:, 0:1], axis=0),
                                                 result[b][:, :], None, compute_op=ALU.add).then_inc(added, 16)

                def body(j, n, b, more, first):
                    set_scatter(j - 1, 1 - b)
                    if more:
                        pool.wait_ge(filled[ZT], j + 1)
                        alone()
                        gather(j + 2, b)
                    scatter(j - 1, n - 1 + b, 1 - b, first)

                gather(0, 0)
                gather(1, 1)
                pool.wait_ge(filled[ZT], 1)
                gather(2, 0)
                body(1, 0, 1, True, True)
                body(2, 1, 0, True, False)
                with pool.Fori(1, BLOCKS // 2) as k:
                    body(2 * k + 1, k, 1, True, False)
                    body(2 * k + 2, k + 1, 0, True, False)
                set_scatter(BLOCKS - 1, 0)
                scatter(BLOCKS - 1, BLOCKS // 2, 0, False)
                pool.wait_ge(added, 16 * BLOCKS)
                for b in range(2):
                    pool.wait_ge(z_loaded[b], 16 * ((COLS - b + 1) // 2))

            @block.tensor
            def _(pe):
                pe.wait_ge(masks_set, 3)
                pe.wait_ge(masks_ready, 1)
                pe.wait_ge(both_ready, 1)
                flat = both[:, :, :].rearrange("p n e -> p (n e)")
                nc.tensor.matmul(psum[RANKS][:, 0:NSUB * NE], lower[:, :], flat, start=True, stop=True)
                nc.tensor.matmul(psum[TOTALS][:, 0:NSUB * NE], ones[:, :], flat, start=True, stop=True).then_inc(ranks_filled, 1)

                def transpose_z(j, n, b):
                    pe.wait_ge(z_loaded[b], 16 * (n + 1))
                    pe.wait_ge(drained[ZT], j + 1)
                    for k in range(DK):
                        ins = nc.tensor.transpose(psum[ZT][:, k * P:(k + 1) * P], z_now[b][:, k * P:(k + 1) * P], ident[:, :])
                    ins.then_inc(filled[ZT], 1)

                def gate_up(j, slot):
                    pe.wait_ge(drained[ZT], j + 2)
                    for bank, high, low in ((GATE, GH, GL), (UP, UH, UL)):
                        pe.wait_ge(drained[bank], j + 1)
                        for k in range(DK):
                            w_high = slots[:, bass.ds(slot, 1), high + k * FD:high + (k + 1) * FD].rearrange("p a n -> p (a n)")
                            w_low = slots[:, bass.ds(slot, 1), low + k * FD:low + (k + 1) * FD].rearrange("p a n -> p (a n)")
                            nc.tensor.matmul(psum[bank][:, 0:FD], zt_hi[:, k, :], w_high, start=(k == 0), stop=False)
                            nc.tensor.matmul(psum[bank][:, 0:FD], zt_hi[:, k, :], w_low, start=False, stop=False)
                            ins = nc.tensor.matmul(psum[bank][:, 0:FD], zt_lo[:, k, :], w_high, start=False, stop=(k == DK - 1))
                        ins.then_inc(filled[bank], 1)

                def transpose_h(j):
                    pe.wait_ge(drained[UP], j + 2)
                    pe.wait_ge(drained[HT], j + 1)
                    for f in range(FC):
                        ins = nc.tensor.transpose(psum[HT][:, f * P:(f + 1) * P], hid[:, f * P:(f + 1) * P], ident[:, :])
                    ins.then_inc(filled[HT], 1)

                def down(j, n, b, slot):
                    pe.wait_ge(drained[HT], j + 2)
                    pe.wait_ge(drained[OUT[b]], n + 1)
                    for f in range(FC):
                        w_high = slots[:, bass.ds(slot, 1), DH_ + f * D:DH_ + (f + 1) * D].rearrange("p a n -> p (a n)")
                        w_low = slots[:, bass.ds(slot, 1), DL_ + f * D:DL_ + (f + 1) * D].rearrange("p a n -> p (a n)")
                        nc.tensor.matmul(psum[OUT[b]][:, :], ht_hi[:, f, :], w_high, start=(f == 0), stop=False)
                        nc.tensor.matmul(psum[OUT[b]][:, :], ht_hi[:, f, :], w_low, start=False, stop=False)
                        ins = nc.tensor.matmul(psum[OUT[b]][:, :], ht_lo[:, f, :], w_high, start=False, stop=(f == FC - 1))
                    ins.then_inc(filled[OUT[b]], 1)

                def slot_of(j):
                    pe.wait_ge(ctl_ready, 1)
                    return pe.value_load(ctl[0:1, bass.ds(j, 1)], min_val=0, max_val=SLOTS - 1)

                def wait_weights(j):
                    pe.wait_ge(ctl_ready, 1)
                    loaded = pe.value_load(ctl[0:1, bass.ds(j + COLS, 1)], min_val=16, max_val=16 * NE)
                    pe.wait_ge(weights_loaded, loaded)

                def body(j, n, b):
                    transpose_h(j - 1)
                    now = slot_of(j)
                    wait_weights(j)
                    gate_up(j, now)
                    transpose_z(j + 1, n + b, 1 - b)
                    down(j - 1, n - 1 + b, 1 - b, slot_of(j - 1))

                transpose_z(0, 0, 0)
                first = slot_of(0)
                wait_weights(0)
                gate_up(0, first)
                transpose_z(1, 0, 1)
                with pe.Fori(0, BLOCKS // 2) as k:
                    body(2 * k + 1, k, 1)
                    body(2 * k + 2, k + 1, 0)
                transpose_h(BLOCKS - 1)
                down(BLOCKS - 1, BLOCKS // 2, 0, slot_of(BLOCKS - 1))

            @block.scalar
            def _(act):
                act.wait_ge(gap_ready, 1)
                nc.scalar.activation(expo[:, :], gap[:, :], ACT.Exp).then_inc(expo_ready, 1)

                def high_h(j):
                    act.wait_ge(filled[HT], j + 1)
                    nc.scalar.activation(ht_hi[:, :, :].rearrange("p f n -> p (f n)"), psum[HT][:, 0:FP], ACT.Copy).then_inc(ht_high, 1)

                def gate(j):
                    act.wait_ge(filled[GATE], j + 1)
                    act.wait_ge(drained[UP], j + 1)
                    nc.scalar.activation(silu_g[:, :], psum[GATE][:, 0:FD], ACT.Silu).then_inc(drained[GATE], 1)

                def high_z(j):
                    act.wait_ge(filled[ZT], j + 1)
                    nc.scalar.activation(zt_hi[:, :, :].rearrange("p k n -> p (k n)"), psum[ZT][:, :], ACT.Copy).then_inc(zt_high, 1)

                high_z(0)
                gate(0)
                high_z(1)
                with act.Fori(1, BLOCKS) as j:
                    high_h(j - 1)
                    gate(j)
                    high_z(j + 1)
                high_h(BLOCKS - 1)

            @block.vector
            def _(dve):
                for i in range(6):
                    nc.vector.nop().then_inc(drained[i], 1)
                links = [0]

                def link(ins):
                    links[0] += 1
                    ins.then_inc(step, 1)
                    dve.wait_ge(step, links[0])

                wide = lambda ap: ap.rearrange("p (n e) -> p n e", e=1).to_broadcast([P, NSUB, NE])
                iota = view(small[:, :], 16, [[0, NSUB], [1, NE]])

                def pick(values, top, k):
                    link(nc.vector.tensor_reduce(top[:, :], values[:, :, :], AX.X, ALU.max))
                    link(nc.vector.tensor_tensor(below[:, :, :], values[:, :, :], wide(top[:, :]), ALU.is_lt))
                    link(nc.vector.scalar_tensor_tensor(below[:, :, :], below[:, :, :], float(NE), iota, ALU.mult, ALU.add))
                    link(nc.vector.tensor_reduce(at[:, :], below[:, :, :], AX.X, ALU.min))
                    link(nc.vector.tensor_tensor(picked[k][:, :, :], iota, wide(at[:, :]), ALU.is_equal))

                def prefix(a, spare, n):
                    d = 1
                    while d < n:
                        nc.vector.tensor_copy(spare[:, 0:d, :], a[:, 0:d, :])
                        link(nc.vector.tensor_tensor(spare[:, d:n, :], a[:, d:n, :], a[:, 0:n - d, :], ALU.add))
                        a, spare, d = spare, a, 2 * d
                    return a

                pick(logits, top1, 0)
                link(nc.vector.scalar_tensor_tensor(masked[:, :, :], picked[0][:, :, :], -3e38, logits[:, :, :], ALU.mult, ALU.add))
                pick(masked, top2, 1)
                nc.vector.tensor_tensor(gap[:, :], top2[:, :], top1[:, :], ALU.subtract).then_inc(gap_ready, 1)
                nc.vector.tensor_tensor(both[:, :, :], picked[0][:, :, :], picked[1][:, :, :], ALU.add).then_inc(both_ready, 1)
                dve.wait_ge(ranks_filled, 1)
                counted = psum[TOTALS][:, 0:NSUB * NE].rearrange("p (n e) -> p n e", n=NSUB)
                nc.vector.tensor_copy(own_total[:, :, :], counted)
                link(nc.vector.tensor_copy(totals[0][:, :, :], counted))
                upto = prefix(totals[0][:, :, :], totals[1][:, :, :], NSUB)
                link(nc.vector.tensor_scalar(count[:, :], upto[:, NSUB - 1, :], 1.0, None, ALU.max))
                link(nc.vector.tensor_scalar(blocks_from[:, :], small[:, 24:24 + NSUB], float(P), None, ALU.mult))
                link(nc.vector.tensor_tensor(full_blocks[:, :, :], view(count[:, :], 0, [[1, NE], [0, NSUB]]),
                                             view(blocks_from[:, :], 0, [[0, NE], [1, NSUB]]), ALU.is_gt))
                link(nc.vector.tensor_reduce(n_blocks[:, :], full_blocks[:, :, :], AX.X, ALU.add))
                link(nc.vector.tensor_copy(ends[0][:, :], n_blocks[:, :]))
                tall = lambda t: t[:, :].rearrange("p (e a) -> p e a", a=1)
                end = prefix(tall(ends[0]), tall(ends[1]), NE).rearrange("p e a -> p (e a)")
                link(nc.vector.tensor_tensor(start[:, :], end, n_blocks[:, :], ALU.subtract))
                link(nc.vector.tensor_tensor(pos[:, :, :], upto, own_total[:, :, :], ALU.subtract))
                link(nc.vector.tensor_tensor(pos[:, :, :], pos[:, :, :], psum[RANKS][:, 0:NSUB * NE].rearrange("p (n e) -> p n e", n=NSUB), ALU.add))
                link(nc.vector.scalar_tensor_tensor(pos[:, :, :], view(start[:, :], 0, [[0, NSUB], [1, NE]]), float(P), pos[:, :, :],
                                                    ALU.mult, ALU.add))
                for k in range(2):
                    link(nc.vector.tensor_tensor(picked[k][:, :, :], picked[k][:, :, :], pos[:, :, :], ALU.mult))
                    link(nc.vector.tensor_reduce(slot_f[:, k, :], picked[k][:, :, :], AX.X, ALU.add))
                link(nc.vector.tensor_copy(slot_i[:, :, :], slot_f[:, :, :]))
                nc.vector.tensor_scalar(low_i[:, :, :], slot_i[:, :, :], P - 1, None, ALU.bitwise_and)
                link(nc.vector.tensor_scalar(high_i[:, :, :], slot_i[:, :, :], P.bit_length() - 1, None, ALU.logical_shift_right))
                nc.vector.tensor_copy(low_f[:, :, :], low_i[:, :, :])
                link(nc.vector.tensor_copy(high_f[:, :, :], high_i[:, :, :]))
                link(nc.vector.scalar_tensor_tensor(row_f[:, :, :], low_f[:, :, :], float(COLS), high_f[:, :, :], ALU.mult, ALU.add))
                nc.vector.tensor_copy(row_i[:, :, :], row_f[:, :, :])
                dve.wait_ge(expo_ready, 1)
                link(nc.vector.tensor_scalar(total[:, :], expo[:, :], 1.0, None, ALU.add))
                link(nc.vector.reciprocal(share[:, 0, :], total[:, :]))
                link(nc.vector.tensor_tensor(share[:, 1, :], expo[:, :], share[:, 0, :], ALU.mult))
                for k in range(2):
                    nc.vector.tensor_copy(entry[:, :, k, 0], tok_ids[:, :])
                    ins = nc.vector.tensor_copy(entry[:, :, k, 1].bitcast(F32), share[:, k, :])
                ins.then_inc(entries_ready, 1)
                link(nc.vector.tensor_tensor(past_end[:, :, :], view(small[:, :], 24, [[1, COLS], [0, NE - 1]]),
                                             view(end, 0, [[0, COLS], [1, NE - 1]]), ALU.is_ge))
                link(nc.vector.tensor_reduce(expert_f[:, :], past_end[:, :, :], AX.X, ALU.add))
                link(nc.vector.tensor_copy(ctl_f[:, 0:COLS], expert_f[:, :]))
                for first in range(SLOTS, NE, SLOTS):
                    link(nc.vector.tensor_scalar(wrapped[:, :], expert_f[:, :], float(first), float(SLOTS), ALU.is_ge, ALU.mult))
                    link(nc.vector.tensor_tensor(ctl_f[:, 0:COLS], ctl_f[:, 0:COLS], wrapped[:, :], ALU.subtract))
                nc.vector.tensor_scalar(ctl_f[:, COLS:2 * COLS], expert_f[:, :], 16.0, 16.0, ALU.mult, ALU.add)
                link(nc.vector.tensor_copy(ctl_f[:, 2 * COLS:2 * COLS + NE], end))
                nc.vector.tensor_copy(ctl[:, :], ctl_f[:, :]).then_inc(ctl_ready, 1)

                def low_z(j):
                    dve.wait_ge(zt_high, j + 1)
                    nc.vector.tensor_tensor(zt_lo[:, :, :].rearrange("p k n -> p (k n)"), psum[ZT][:, :],
                                            zt_hi[:, :, :].rearrange("p k n -> p (k n)").bitcast(F32), ALU.subtract).then_inc(drained[ZT], 1)

                def low_h(j):
                    dve.wait_ge(ht_high, j + 1)
                    nc.vector.tensor_tensor(ht_lo[:, :, :].rearrange("p f n -> p (f n)"), psum[HT][:, 0:FP],
                                            ht_hi[:, :, :].rearrange("p f n -> p (f n)").bitcast(F32), ALU.subtract).then_inc(drained[HT], 1)

                def multiply(j):
                    dve.wait_ge(drained[GATE], j + 2)
                    dve.wait_ge(filled[UP], j + 1)
                    nc.vector.tensor_tensor(hid[:, 0:FD], silu_g[:, :], psum[UP][:, 0:FD], ALU.mult).then_inc(drained[UP], 1)

                def weigh(j, n, b, first):
                    dve.wait_ge(filled[OUT[b]], n + 1)
                    dve.wait_ge(scatter_set, j + 1)
                    if not first:
                        dve.wait_ge(added, 16 * (j - 1))
                    nc.vector.tensor_scalar(result[b][:, :], psum[OUT[b]][:, :], scatter_at[b][:, 1:2].bitcast(F32), None,
                                            ALU.mult).then_inc(drained[OUT[b]], 1)

                def body(j, n, b, first):
                    low_h(j - 1)
                    multiply(j)
                    low_z(j + 1)
                    weigh(j - 1, n - 1 + b, 1 - b, first)

                low_z(0)
                multiply(0)
                low_z(1)
                body(1, 0, 1, True)
                body(2, 1, 0, True)
                with dve.Fori(1, BLOCKS // 2) as k:
                    body(2 * k + 1, k, 1, False)
                    body(2 * k + 2, k + 1, 0, False)
                low_h(BLOCKS - 1)
                weigh(BLOCKS - 1, BLOCKS // 2, 0, False)


NAMES = {"x": "x", "cond": "itok_B_1_198", "adapter": "itok_B_0_6", "cond_w": "L0_cond_weights",
         "gate_cp": "L0_ffn_gate_cp", "up_cp": "L0_ffn_up_cp", "down_cp": "L0_ffn_down_cp",
         "W": "L1_cond_W", "A": "L1_cond_A", "Bm": "L1_cond_Bm", "scalings": "L1_cond_scalings",
         "router_w": "L1_ffn_gate_w", "gate_proj": "L1_ffn_gate_proj", "up_proj": "L1_ffn_up_proj", "down_proj": "L1_ffn_down_proj"}


def kernel(**inputs):
    import concourse.bacc as bacc
    from concourse.bass_utils import run_bass_kernel_spmd

    nc = bacc.Bacc("TRN2", target_bir_lowering=False, num_devices=1)
    arrays = {name: np.ascontiguousarray(inputs[key]) for name, key in NAMES.items()}
    arrays.update(spline_constants())
    arrays.update(index_constants())
    io = {name: nc.dram_tensor(f"in_{name}", a.shape, mybir.dt.from_np(a.dtype), kind="ExternalInput").ap()
          for name, a in arrays.items()}
    io["out"] = nc.dram_tensor("out", [TOKP, D], F32, kind="ExternalOutput").ap()
    build(nc, io)
    result = run_bass_kernel_spmd(nc, [{f"in_{name}": a for name, a in arrays.items()}], core_ids=[0])
    return result.results[0]["out"][0:TOK].reshape(BATCH, SEQ, D)
```

```python
from contextlib import ExitStack

import numpy as np

import concourse.bass as bass
from concourse import mybir

F32 = mybir.dt.float32
F32R = mybir.dt.float32r
I32 = mybir.dt.int32
U32 = mybir.dt.uint32
U8 = mybir.dt.uint8
ACT = mybir.ActivationFunctionType
ALU = mybir.AluOpType
AX = mybir.AxisListType

P = 128
BATCH, SEQ, D = 64, 64, 512
TOK = BATCH * SEQ
DK = D // P
INTER = 2048
IC = INTER // P
NCP = 8134
CPP = NCP + 10
PAD = 2
TILE = 256
NT = TOK // TILE
SUB = TILE // P
INNER = 4
RING, LAG = 8, 3
GU_BANKS = 4
LTILE = 512
LNT = TOK // LTILE
LSUB = LTILE // P
NSUB = TOK // P

GROUPS = 8
GROUP = INTER // GROUPS
PIECES, POW = 5, 4
KNOTS, KNOT_W, KNOT_GAP, KNOT_STEP = 4, 18, 129, 16
NPOLY = PIECES * POW
NRAW = KNOTS * KNOT_W
NF = NPOLY + NRAW
XW = 520
HALF = 64.0

NA, RANK = 8, 16
NE, FD = 8, 352
FC = 3
FP = FC * P
REM = FD - 2 * P
BLOCKS = 2 * TOK // P + NE - 1
COLS = BLOCKS + 2
MAX_BLOCKS = TOK // P
REGION = MAX_BLOCKS + 1
TOKP = TOK + P
SLOTS = 3

GH, GL, UH, UL = (i * DK * FD for i in range(4))
DH_, DL_ = 4 * DK * FD, 4 * DK * FD + FC * D
EW = 4 * DK * FD + 2 * FC * D


def spline_constants():
    n = D * INTER
    t = np.linspace(0.0, NCP - 1.0, n, dtype=np.float64)
    iv = np.clip(np.floor(t).astype(np.int64), 0, NCP - 2)
    step = (NCP - 1.0) / (n - 1.0)
    base = 0.5 * np.array([[0, 2, 0, 0], [-1, 0, 1, 0], [2, -5, 4, -1], [-1, 3, -3, 1]], np.float64)

    def cubic(c, s):
        c = np.asarray(c)[..., None]
        return np.stack([base[0] + c * base[1] + c**2 * base[2] + c**3 * base[3],
                         s * (base[1] + 2 * c * base[2] + 3 * c**2 * base[3]),
                         s * s * (base[2] + 3 * c * base[3]),
                         s**3 * base[3] * np.ones_like(c)], -2)

    rt, ri = t.reshape(INTER, D), iv.reshape(INTER, D)
    j0 = ri[:, 0]
    order = np.argsort(j0 - rt[:, 0], kind="stable")
    mom = np.zeros((D, GROUPS, PIECES, POW))
    tabp = np.zeros((INTER, PIECES, POW, 4))
    tabr = np.zeros((INTER, KNOTS, KNOT_W, 5))
    for g in range(GROUPS):
        at = np.arange(g * GROUP, (g + 1) * GROUP)
        r = order[at]
        lo = [KNOT_STEP * g + KNOT_GAP * k for k in range(KNOTS)]
        for p in range(PIECES):
            a, b = ([0] + [x + KNOT_W for x in lo])[p], min((lo + [D])[p], D)
            if b <= a:
                continue
            c = (a + b - 1) / 2
            assert (ri[r, a:b] == (j0[r] + p)[:, None]).all()
            mom[a:b, g, p] = ((np.arange(a, b) - c) / HALF)[:, None] ** np.arange(POW)
            tabp[at, p] = cubic((r * D + c) * step - (j0[r] + p), HALF * step)
        for k in range(KNOTS):
            for w in range(KNOT_W):
                h = lo[k] + w
                if h >= D:
                    continue
                rel = ri[r, h] - j0[r] - k
                assert ((rel == 0) | (rel == 1)).all()
                weight = cubic(rt[r, h] - ri[r, h], 1.0)[:, 0]
                for q in (0, 1):
                    tabr[at[rel == q], k, w, q:q + 4] = weight[rel == q]

    nb = n // P
    b = np.arange(nb)
    jb = iv[b * P]
    jq = np.repeat(jb[::4], 4)
    c4 = b % 4
    tabd = np.zeros((nb, 2, POW, 5))
    for side in range(2):
        weight = cubic((b * P + (P - 1) / 2) * step - jb - side, HALF * step)
        for q in (0, 1):
            s = (jb - jq + 1 - c4) == q
            tabd[s, side, :, q:q + 4] = weight[s]
    assert np.isin(jb - jq + 1 - c4, (0, 1)).all()
    past = (iv.reshape(nb, P) > jb[:, None])
    assert (iv.reshape(nb, P) - jb[:, None] <= 1).all()
    v = ((np.arange(P) - (P - 1) / 2) / HALF)[None] ** np.arange(POW)[:, None]
    vh = np.rint(v * 2**11) / 2**11
    vl = v - vh
    pw = np.zeros((4, 2, 4, POW, 8, P))
    for c in range(4):
        for side in range(2):
            pw[c, side, :, :, 2 * c + side] = np.stack([vh, vl, vh, vl])

    f = lambda a: np.ascontiguousarray(a, dtype=np.float32)
    ints = lambda a: np.ascontiguousarray(a, dtype=np.int32)
    return {
        "c_order": ints(order.reshape(IC, P).T),
        "c_win_gu": ints((j0[order] + PAD - 1).reshape(IC, P).T),
        "c_win_d": ints((jb[::4] + PAD - 2).reshape(16, P).T),
        "c_mom": f(mom.reshape(DK, P, GROUPS * NPOLY).transpose(1, 0, 2)),
        "c_tabp": f(tabp.reshape(IC, P, PIECES, 16).transpose(1, 2, 0, 3).reshape(P, -1)),
        "c_tabr": f(tabr.reshape(IC, P, KNOTS, KNOT_W * 5).transpose(1, 2, 0, 3).reshape(P, -1)),
        "c_tabd": f(tabd.reshape(16, P, 4, 2, 20).transpose(1, 2, 3, 0, 4).reshape(P, -1)),
        "c_pw": f(pw.reshape(P, 8 * P)),
        "c_past": np.ascontiguousarray(past.reshape(16, P, 4, P).transpose(3, 2, 0, 1).reshape(P, -1).astype(np.int32)),
    }


def index_constants():
    p = np.arange(P)
    tok = (np.arange(NSUB)[None] * P + p[:, None]).astype(np.float32)
    small = np.zeros((P, 128), np.float32)
    small[:, 0] = p % 64
    small[:, 1] = p // RANK
    for c in range(3):
        small[:, 2 + c] = p + c * P
    small[:, 8:16] = (p[:, None] // RANK == np.arange(NA))
    small[:, 16:24] = np.arange(NE)
    small[:, 24:24 + COLS] = np.arange(COLS)
    return {"c_tok": tok, "c_small": small,
            "c_no_entry": np.stack([np.tile(TOK + p, NE * REGION).reshape(P, -1), np.zeros((P, NE * REGION))], -1).astype(np.float32)}


def view(ap, offset, dims):
    return bass.AP(tensor=ap.tensor, offset=ap.offset + offset, ap=[list(ap.ap[0])] + [list(d) for d in dims])


def build(nc, io):
    kc = {k: v for k, v in io.items() if k.startswith("c_")}
    dram = lambda n, s, d=F32: nc.dram_tensor(n, s, d, kind="Internal").ap()
    cp_padded = dram("cp_padded", [3, CPP])
    down_natural = dram("down_natural", [INTER, D])
    expert_dram = dram("expert_dram", [NE, P, EW])
    z_dram = dram("z_dram", [TOKP, D])
    table_dram = dram("table_dram", [NE * REGION * P, 2])
    out = io["out"]
    x_flat = io["x"].rearrange("b c h -> (b c) h")
    layer_tiles = out[0:TOK, :].rearrange("(t s p) h -> t p s h", s=LSUB, p=P)
    x_tiles = x_flat.rearrange("(t s p) h -> t p s h", s=SUB, p=P)
    out_tiles = out[0:TOK, :].rearrange("(t s p) h -> t p s h", s=SUB, p=P)
    z_tiles = z_dram[0:TOK, :].rearrange("(t s p) h -> t p s h", s=LSUB, p=P)
    cond_rows = io["cond_w"].rearrange("n c d -> (n c) d")

    top = ExitStack()
    with top:
        def alloc(stack):
            def sb(name, shape, dt=F32):
                return stack.enter_context(nc.sbuf_tensor(name, shape, dt))
            return sb

        def sem(name):
            return top.enter_context(nc.semaphore(name))

        psum = [top.enter_context(nc.psum_tensor(f"bank{i}", [P, 512], F32)) for i in range(8)]
        sb = alloc(top)
        ident = sb("ident", [P, P])
        small = sb("small", [P, 128])
        tok_ids = sb("tok_ids", [P, NSUB])
        lower, ones = sb("lower", [P, P]), sb("ones", [P, P])
        chosen = sb("chosen", [P, LSUB + 1, NE])
        idle = sb("idle", [P, 64])
        ident_set, ident_ready = sem("ident_set"), sem("ident_ready")

        layer = ExitStack()
        sbl = alloc(layer)
        w_hi = sbl("w_hi", [P, DK, D], F32R)
        w_lo = sbl("w_lo", [P, DK, D], F32R)
        a_hi = sbl("a_hi", [P, DK, P], F32R)
        a_lo = sbl("a_lo", [P, DK, P], F32R)
        b_hi = sbl("b_hi", [P, D], F32R)
        b_lo = sbl("b_lo", [P, D], F32R)
        r_hi = sbl("r_hi", [P, DK + 1, NE], F32R)
        r_lo = sbl("r_lo", [P, DK + 1, NE], F32R)
        adapter_scale = sbl("adapter_scale", [P, BATCH])
        main = ExitStack()
        sbm = alloc(main)
        gu_hi = sbm("gu_hi", [NF, 2, INTER], F32R)
        gu_lo = sbm("gu_lo", [NF, 2, INTER], F32R)
        mom = sbm("mom", [P, DK, GROUPS * NPOLY])
        cond_idx = sbm("cond_idx", [P, NSUB + 2 * SUB], I32)
        win_gu = sbm("win_gu", [P, 2, IC, 8])
        win_d = sbm("win_d", [P, 16, 9])
        order_idx = sbm("order_idx", [P, IC], I32)

        expert_weights(nc, io, kc, alloc, sem, psum, ident, ident_set, ident_ready, small, lower, ones, tok_ids,
                       expert_dram, cp_padded, win_gu, win_d, order_idx, table_dram, z_dram, out)
        first_weights(nc, io, kc, alloc, sem, psum, ident, small, mom, gu_hi, gu_lo,
                      w_hi, w_lo, a_hi, a_lo, b_hi, b_lo, r_hi, r_lo, adapter_scale, cond_idx, win_gu)
        down_hi = sbm("down_hi", [P, IC, D], F32R)
        down_lo = sbm("down_lo", [P, IC, D], F32R)
        down_weights(nc, kc, alloc, sem, psum, ident, win_d, order_idx, down_natural, down_hi, down_lo)
        first_ffn(nc, alloc, sem, psum, ident, small, idle, x_tiles, out_tiles, cond_rows, cond_idx, mom,
                  gu_hi, gu_lo, down_hi, down_lo)
        main.close()
        adapted_layer(nc, alloc, sem, psum, ident, small, idle, lower, ones, tok_ids, layer_tiles, z_tiles, w_hi, w_lo, a_hi, a_lo,
                      b_hi, b_lo, r_hi, r_lo, adapter_scale, chosen, table_dram)
        layer.close()
        experts(nc, alloc, sem, psum, ident, small, idle, ones, chosen, expert_dram, table_dram, z_dram, out)


def expert_weights(nc, io, kc, alloc, sem, psum, ident, ident_set, ident_ready, small, lower, ones, tok_ids,
                   expert_dram, cp_padded, win_gu, win_d, order_idx, table_dram, z_dram, out):
    with ExitStack() as scope:
        sb = alloc(scope)
        raw_gu = [[sb(f"raw_{m}{b}", [P, FC, D]) for m in ("gate", "up")] for b in range(2)]
        raw_down = [sb(f"raw_down{b}", [P, DK, FD]) for b in range(2)]
        split = [sb(f"split{b}", [P, EW], F32R) for b in range(2)]
        idx_gu, idx_d = sb("idx_gu", [P, IC], I32), sb("idx_d", [P, 16], I32)
        zeros, no_entry = sb("zeros", [P, D]), sb("no_entry", [P, NE * REGION, 2])
        raw_loaded = [sem(f"raw_loaded{b}") for b in range(2)]
        split_stored = [sem(f"split_stored{b}") for b in range(2)]
        filled = [sem(f"ew_filled{i}") for i in range(4)]
        drained = [sem(f"ew_drained{i}") for i in range(4)]
        high_done = sem("ew_high_done")
        consts_loaded, no_entry_loaded = sem("consts_loaded"), sem("no_entry_loaded")
        cp_stored, win_loaded = sem("cp_stored"), sem("win_loaded")
        zeros_set, masks_set, padding_stored = sem("zeros_set"), sem("masks_set"), sem("padding_stored")
        USES = 2 * DK + FC
        PER = [len(range(i, USES, 4)) for i in range(4)]
        LAST = (USES - 1) % 4

        def use(u):
            if u < 2 * DK:
                m, c = u // DK, u % DK
                return P, FD, (GH, UH)[m] + c * FD, (GL, UL)[m] + c * FD
            f = u - 2 * DK
            return (P if f < 2 else REM), D, DH_ + f * D, DL_ + f * D

        with nc.Block() as block:
            @block.sync
            def _(sp):
                def load(e, b):
                    for m, name in enumerate(("gate_proj", "up_proj")):
                        src = io[name][bass.ds(e, 1)]
                        sp.dma_start(raw_gu[b][m][:, 0:2, :],
                                     src[:, 0:2 * P, :].rearrange("a (c p) d -> p (a c) d", p=P)).then_inc(raw_loaded[b], 16)
                        sp.dma_start(raw_gu[b][m][0:REM, 2, :],
                                     src[:, 2 * P:FD, :].rearrange("a p d -> p (a d)")).then_inc(raw_loaded[b], 16)
                    sp.dma_start(raw_down[b][:, :, :], io["down_proj"][bass.ds(e, 1)]
                                 .rearrange("a (c p) f -> p (a c) f", p=P)).then_inc(raw_loaded[b], 16)

                def store(e, b):
                    sp.wait_ge(drained[LAST], PER[LAST] * (e + 1) + 1)
                    sp.dma_start(expert_dram[bass.ds(e, 1)].rearrange("a p w -> p (a w)"),
                                 split[b][:, :].bitcast(F32)).then_inc(split_stored[b], 16)

                load(0, 0)
                load(1, 1)
                with sp.Fori(0, NE // 2 - 1) as k:
                    for b in range(2):
                        sp.wait_ge(filled[LAST], PER[LAST] * (2 * k + b + 1))
                        load(2 * k + b + 2, b)
                        store(2 * k + b, b)
                store(NE - 2, 0)
                store(NE - 1, 1)
                for b in range(2):
                    sp.wait_ge(split_stored[b], 16 * NE // 2)

            @block.gpsimd
            def _(pool):
                nc.gpsimd.memset(ident[:, :], 0.0).then_inc(ident_set, 1)
                pool.wait_ge(ident_set, 1)
                nc.gpsimd.affine_select(out=ident[:, :], in_=ident[:, :], compare_op=ALU.not_equal, fill=1.0,
                                        base=0, pattern=[[-1, P]], channel_multiplier=1).then_inc(ident_ready, 1)
                nc.gpsimd.memset(zeros[:, :], 0.0).then_inc(zeros_set, 1)
                nc.gpsimd.memset(ones[:, :], 1.0)
                nc.gpsimd.memset(lower[:, :], 1.0).then_inc(masks_set, 1)
                pool.wait_ge(masks_set, 1)
                nc.gpsimd.affine_select(out=lower[:, :], in_=lower[:, :], compare_op=ALU.is_gt, fill=0.0,
                                        base=0, pattern=[[1, P]], channel_multiplier=-1)
                pool.wait_ge(consts_loaded, 16 * 5)
                pool.wait_ge(cp_stored, 16 * 3 * (PAD + 3))
                flat = cp_padded.rearrange("m (a b) -> (m a) b", b=1)
                for m in range(2):
                    for q in range(IC):
                        nc.gpsimd.indirect_dma_start(win_gu[:, m, q, :], None, flat,
                                                     bass.IndirectOffsetOnAxis(ap=idx_gu[:, q:q + 1], axis=0),
                                                     element_offset=m * CPP).then_inc(win_loaded, 16)
                for q in range(16):
                    nc.gpsimd.indirect_dma_start(win_d[:, q, :], None, flat,
                                                 bass.IndirectOffsetOnAxis(ap=idx_d[:, q:q + 1], axis=0),
                                                 element_offset=2 * CPP).then_inc(win_loaded, 16)
                pool.wait_ge(win_loaded, 16 * (2 * IC + 16))

            @block.tensor
            def _(pe):
                pe.wait_ge(ident_ready, 1)
                with pe.Fori(0, NE // 2) as k:
                    for b in range(2):
                        e = 2 * k + b
                        pe.wait_ge(raw_loaded[b], 16 * 5 * (k + 1))
                        for u in range(USES):
                            i = u % 4
                            pe.wait_ge(drained[i], e * PER[i] + u // 4 + 1)
                            if u < 2 * DK:
                                m, c = u // DK, u % DK
                                for f in range(FC):
                                    rows = P if f < 2 else REM
                                    ins = nc.tensor.transpose(psum[i][:, f * P:f * P + rows],
                                                              raw_gu[b][m][0:rows, f, c * P:(c + 1) * P], ident[0:rows, 0:rows])
                            else:
                                f = u - 2 * DK
                                rows = P if f < 2 else REM
                                for c in range(DK):
                                    ins = nc.tensor.transpose(psum[i][0:rows, c * P:(c + 1) * P],
                                                              raw_down[b][:, c, f * P:f * P + rows], ident[:, :])
                            ins.then_inc(filled[i], 1)

            @block.scalar
            def _(act):
                act.dma_start(idx_gu[:, :], kc["c_win_gu"]).then_inc(consts_loaded, 16)
                act.dma_start(idx_d[:, :], kc["c_win_d"]).then_inc(consts_loaded, 16)
                act.dma_start(order_idx[:, :], kc["c_order"]).then_inc(consts_loaded, 16)
                act.dma_start(small[:, :], kc["c_small"]).then_inc(consts_loaded, 16)
                act.dma_start(tok_ids[:, :], kc["c_tok"]).then_inc(consts_loaded, 16)
                for m, name in enumerate(("gate_cp", "up_cp", "down_cp")):
                    cp = io[name].rearrange("(a n) -> a n", a=1)
                    to = cp_padded[m:m + 1, :]
                    act.dma_start(to[:, PAD:PAD + NCP], cp).then_inc(cp_stored, 16)
                    for i in range(PAD):
                        act.dma_start(to[:, i:i + 1], cp[:, 0:1]).then_inc(cp_stored, 16)
                    act.dma_start(to[:, PAD + NCP:PAD + NCP + 1], cp[:, NCP - 1:NCP]).then_inc(cp_stored, 16)
                    act.dma_start(to[:, PAD + NCP + 1:CPP], cp[:, 0:CPP - PAD - NCP - 1]).then_inc(cp_stored, 16)
                act.dma_start(no_entry[:, :, :], kc["c_no_entry"]).then_inc(no_entry_loaded, 16)
                act.wait_ge(zeros_set, 1)
                act.dma_start(z_dram[TOK:TOKP, :], zeros[:, :]).then_inc(padding_stored, 16)
                act.dma_start(out[TOK:TOKP, :], zeros[:, :]).then_inc(padding_stored, 16)
                act.wait_ge(no_entry_loaded, 16)
                act.dma_start(table_dram.rearrange("(p c) w -> p (c w)", p=P),
                              no_entry[:, :, :].rearrange("p c w -> p (c w)")).then_inc(padding_stored, 16)

                def high_parts(k, b, first):
                    e = 2 * k + b
                    if not first:
                        act.wait_ge(split_stored[b], 16 * k)
                    for u in range(USES):
                        rows, w, hi, _ = use(u)
                        act.wait_ge(filled[u % 4], e * PER[u % 4] + u // 4 + 1)
                        nc.scalar.activation(split[b][0:rows, hi:hi + w], psum[u % 4][0:rows, 0:w], ACT.Copy).then_inc(high_done, 1)

                for b in range(2):
                    high_parts(0, b, True)
                with act.Fori(1, NE // 2) as k:
                    for b in range(2):
                        high_parts(k, b, False)
                act.wait_ge(padding_stored, 48)

            @block.vector
            def _(dve):
                for i in range(4):
                    nc.vector.nop().then_inc(drained[i], 1)
                for b in range(2):
                    nc.vector.memset(split[b][REM:P, DH_ + 2 * D:DH_ + 3 * D].bitcast(F32), 0.0)
                    nc.vector.memset(split[b][REM:P, DL_ + 2 * D:DL_ + 3 * D].bitcast(F32), 0.0)
                with dve.Fori(0, NE // 2) as k:
                    for b in range(2):
                        e = 2 * k + b
                        for u in range(USES):
                            rows, w, hi, lo = use(u)
                            dve.wait_ge(high_done, e * USES + u + 1)
                            nc.vector.tensor_tensor(split[b][0:rows, lo:lo + w], psum[u % 4][0:rows, 0:w],
                                                    split[b][0:rows, hi:hi + w].bitcast(F32), ALU.subtract).then_inc(drained[u % 4], 1)


def first_weights(nc, io, kc, alloc, sem, psum, ident, small, mom, gu_hi, gu_lo,
                  w_hi, w_lo, a_hi, a_lo, b_hi, b_lo, r_hi, r_lo, adapter_scale, cond_idx, win_gu):
    with ExitStack() as scope:
        sb = alloc(scope)
        tabp = sb("tabp", [P, PIECES, IC, POW, 4])
        tabr = sb("tabr", [P, KNOTS, IC, KNOT_W, 5])
        prod = [sb(f"prod{b}", [P, IC, KNOT_W, 5]) for b in range(2)]
        rows_gu = sb("rows_gu", [P, 2, IC, NF])
        raw_w = sb("raw_w", [P, DK, D])
        raw_a = sb("raw_a", [P, D])
        raw_b = sb("raw_b", [P, DK, NA, RANK])
        raw_r = sb("raw_r", [NE, D])
        r_t = sb("r_t", [P, DK, NE])
        cond_i, cond_f = sb("cond_i", [P, BATCH], I32), sb("cond_f", [P, BATCH])
        adapt_i, adapt_f = sb("adapt_i", [P, BATCH], I32), sb("adapt_f", [P, BATCH])
        idx_f = sb("idx_f", [P, NSUB])
        scale_all, scale_own = sb("scale_all", [P, NA]), sb("scale_own", [P, 1])
        scale_pick = sb("scale_pick", [P, NA])
        tabs_loaded, raw_loaded, ints_loaded = sem("tabs_loaded"), sem("fw_raw_loaded"), sem("ints_loaded")
        step = sem("fw_step")
        NB = 4
        filled = [sem(f"fw_filled{i}") for i in range(NB)]
        drained = [sem(f"fw_drained{i}") for i in range(NB)]
        high_done, rows_done, rt_done = sem("fw_high_done"), sem("rows_done"), sem("rt_done")
        W_USE, A_USE, B_USE, RT_USE, R_USE, GU_USE = 0, DK, DK + 1, DK + 2, DK + 3, DK + 4
        USES = GU_USE + 2 * IC // 4

        def target(u):
            if u < A_USE:
                return w_hi[:, u, :], w_lo[:, u, :], P, D
            if u == A_USE:
                return (a_hi[:, :, :].rearrange("p k r -> p (k r)"), a_lo[:, :, :].rearrange("p k r -> p (k r)"), P, D)
            if u == B_USE:
                return b_hi[:, :], b_lo[:, :], P, D
            if u == R_USE:
                n = (DK + 1) * NE
                return (r_hi[:, :, :].rearrange("p k e -> p (k e)"), r_lo[:, :, :].rearrange("p k e -> p (k e)"), P, n)
            m, q = (u - GU_USE) // 4, (u - GU_USE) % 4
            return gu_hi[:, m, q * D:(q + 1) * D], gu_lo[:, m, q * D:(q + 1) * D], NF, D

        splits = [u for u in range(USES) if u != RT_USE]

        with nc.Block() as block:
            @block.sync
            def _(sp):
                sp.dma_start(raw_w[:, :, :], io["W"].rearrange("(c p) d -> p c d", p=P)).then_inc(raw_loaded, 16)
                sp.dma_start(raw_a[:, :], io["A"].rearrange("n r d -> (n r) d")).then_inc(raw_loaded, 16)
                for c in range(DK):
                    sp.dma_start(raw_b[:, c, :, :], io["Bm"][:, c * P:(c + 1) * P, :].rearrange("n p r -> p n r")).then_inc(raw_loaded, 16)
                sp.dma_start(raw_r[:, :], io["router_w"]).then_inc(raw_loaded, 16)

            @block.gpsimd
            def _(pool):
                pass

            @block.tensor
            def _(pe):
                pe.wait_ge(raw_loaded, 16 * (3 + DK))
                for u in range(USES):
                    i = u % NB
                    pe.wait_ge(drained[i], u // NB + 1)
                    bank = psum[i]
                    if u < A_USE:
                        for c in range(DK):
                            ins = nc.tensor.transpose(bank[:, c * P:(c + 1) * P], raw_w[:, c, u * P:(u + 1) * P], ident[:, :])
                    elif u == A_USE:
                        for c in range(DK):
                            ins = nc.tensor.transpose(bank[:, c * P:(c + 1) * P], raw_a[:, c * P:(c + 1) * P], ident[:, :])
                    elif u == B_USE:
                        for c in range(DK):
                            ins = nc.tensor.transpose(bank[:, c * P:(c + 1) * P],
                                                      raw_b[:, c, :, :].rearrange("p n r -> p (n r)"), ident[:, :])
                    elif u == RT_USE:
                        for c in range(DK):
                            ins = nc.tensor.transpose(bank[:, c * NE:(c + 1) * NE], raw_r[:, c * P:(c + 1) * P], ident[0:NE, 0:NE])
                    elif u == R_USE:
                        pe.wait_ge(rt_done, 1)
                        for k in range(DK):
                            for c in range(DK):
                                nc.tensor.matmul(bank[:, k * NE:(k + 1) * NE], raw_w[:, c, k * P:(k + 1) * P], r_t[:, c, :],
                                                 start=(c == 0), stop=(c == DK - 1))
                        for c in range(DK):
                            ins = nc.tensor.matmul(bank[:, DK * NE:(DK + 1) * NE], raw_b[:, c, :, :].rearrange("p n r -> p (n r)"),
                                                   r_t[:, c, :], start=(c == 0), stop=(c == DK - 1))
                    else:
                        m, q4 = (u - GU_USE) // 4, (u - GU_USE) % 4
                        pe.wait_ge(rows_done, m + 1)
                        for q in range(4):
                            ins = nc.tensor.transpose(bank[0:NF, q * P:(q + 1) * P], rows_gu[:, m, 4 * q4 + q, :], ident[:, :])
                    ins.then_inc(filled[i], 1)

            @block.scalar
            def _(act):
                act.dma_start(tabp[:, :, :, :, :].rearrange("p a b c d -> p (a b c d)"), kc["c_tabp"]).then_inc(tabs_loaded, 16)
                act.dma_start(tabr[:, :, :, :, :].rearrange("p a b c d -> p (a b c d)"), kc["c_tabr"]).then_inc(tabs_loaded, 16)
                act.dma_start(mom[:, :, :].rearrange("p k n -> p (k n)"), kc["c_mom"].rearrange("p k n -> p (k n)")).then_inc(tabs_loaded, 16)
                act.dma_start(cond_i[:, :], io["cond"].rearrange("(a n) -> a n", a=1).to_broadcast([P, BATCH])).then_inc(ints_loaded, 16)
                act.dma_start(adapt_i[:, :], io["adapter"].rearrange("(a n) -> a n", a=1).to_broadcast([P, BATCH])).then_inc(ints_loaded, 16)
                act.dma_start(scale_all[:, :], io["scalings"].rearrange("(a n) -> a n", a=1).to_broadcast([P, NA])).then_inc(ints_loaded, 16)
                for u in range(USES):
                    act.wait_ge(filled[u % NB], u // NB + 1)
                    if u == RT_USE:
                        nc.scalar.activation(r_t[:, :, :].rearrange("p c e -> p (c e)"), psum[u % NB][:, 0:DK * NE], ACT.Copy).then_inc(rt_done, 1)
                        act.wait_ge(rt_done, 1)
                        nc.scalar.nop().then_inc(drained[u % NB], 1)
                        continue
                    hi, _, rows, w = target(u)
                    nc.scalar.activation(hi, psum[u % NB][0:rows, 0:w], ACT.Copy).then_inc(high_done, 1)

            @block.vector
            def _(dve):
                for i in range(NB):
                    nc.vector.nop().then_inc(drained[i], 1)
                count = [0]

                def link(ins):
                    count[0] += 1
                    ins.then_inc(step, 1)
                    dve.wait_ge(step, count[0])

                def low_part(u):
                    hi, lo, rows, w = target(u)
                    dve.wait_ge(high_done, splits.index(u) + 1)
                    nc.vector.tensor_tensor(lo, psum[u % NB][0:rows, 0:w], hi.bitcast(F32), ALU.subtract).then_inc(drained[u % NB], 1)

                for u in range(RT_USE):
                    low_part(u)
                low_part(R_USE)
                dve.wait_ge(ints_loaded, 48)
                link(nc.vector.tensor_copy(cond_f[:, :], cond_i[:, :]))
                for half in range(2):
                    rows = slice(64 * half, 64 * half + 64)
                    last = nc.vector.tensor_scalar(idx_f[rows, :], cond_f[rows, half::2], 64.0, small[rows, 0:1], ALU.mult, ALU.add)
                    link(last)
                link(nc.vector.memset(cond_idx[:, NSUB:], 0))
                link(nc.vector.tensor_copy(cond_idx[:, 0:NSUB], idx_f[:, :]))
                link(nc.vector.tensor_copy(adapt_f[:, :], adapt_i[:, :]))
                link(nc.vector.tensor_tensor(scale_pick[:, :], scale_all[:, :], small[:, 8:8 + NA], ALU.mult))
                link(nc.vector.tensor_reduce(scale_own[:, :], scale_pick[:, :], AX.X, ALU.add))
                link(nc.vector.tensor_scalar(adapter_scale[:, :], adapt_f[:, :], small[:, 1:2], scale_own[:, 0:1], ALU.is_equal, ALU.mult))
                dve.wait_ge(tabs_loaded, 48)
                turn = 0
                for m in range(2):
                    for p in range(PIECES):
                        pr = prod[turn % 2][:, :, 0:POW, 0:4]
                        link(nc.vector.tensor_tensor(pr, tabp[:, p], view(win_gu[:, m], p, [[8, IC], [0, POW], [1, 4]]), ALU.mult))
                        last = nc.vector.tensor_reduce(rows_gu[:, m, :, p * POW:(p + 1) * POW], pr, AX.X, ALU.add)
                        turn += 1
                    for k in range(KNOTS):
                        pr = prod[turn % 2][:, :, :, :]
                        link(nc.vector.tensor_tensor(pr, tabr[:, k], view(win_gu[:, m], k, [[8, IC], [0, KNOT_W], [1, 5]]), ALU.mult))
                        last = nc.vector.tensor_reduce(rows_gu[:, m, :, NPOLY + k * KNOT_W:NPOLY + (k + 1) * KNOT_W], pr, AX.X, ALU.add)
                        turn += 1
                    last.then_inc(rows_done, 1)
                    for q in range(4):
                        if m == 1:
                            low_part(GU_USE + q)
                for q in range(4):
                    low_part(GU_USE + 4 + q)


def down_weights(nc, kc, alloc, sem, psum, ident, win_d, order_idx, down_natural, down_hi, down_lo):
    with ExitStack() as scope:
        sb = alloc(scope)
        tabd = sb("tabd", [P, 4, 2, 16, POW, 5])
        prod = [sb(f"dprod{b}", [P, 16, POW, 5]) for b in range(2)]
        coef = sb("coef", [P, 16, 8, POW])
        parts = sb("parts", [P, 16, 8, 4, POW])
        powers, powers_r = sb("powers", [P, 8, P]), sb("powers_r", [P, 8, P], F32R)
        past = sb("past", [P, 4, 4, 4 * P], U8)
        coef_t = sb("coef_t", [P, 4, 4 * P], F32R)
        dense = sb("dense", [P, IC, D])
        tabs_loaded, past_loaded, step = sem("dw_tabs_loaded"), sem("past_loaded"), sem("dw_step")
        past_ready = sem("past_ready")
        parts_hi, parts_done, powers_done = sem("parts_hi"), sem("parts_done"), sem("powers_done")
        t_filled, t_drained = [sem(f"dt_filled{i}") for i in range(2)], [sem(f"dt_drained{i}") for i in range(2)]
        filled, before, drained = ([sem(f"dw_{n}{i}") for i in range(3)] for n in ("filled", "before", "drained"))
        stored, gathered, high_done, low_done = sem("dense_stored"), sem("dense_gathered"), sem("dw_high_done"), sem("dw_low_done")

        with nc.Block() as block:
            @block.sync
            def _(sp):
                sp.dma_start(tabd[:, :, :, :, :, :].rearrange("p a b c d e -> p (a b c d e)"), kc["c_tabd"]).then_inc(tabs_loaded, 16)
                sp.dma_start(powers[:, :, :].rearrange("p a b -> p (a b)"), kc["c_pw"]).then_inc(tabs_loaded, 16)
                sp.dma_start(dense[:, :, :].rearrange("p a b -> p (a b)").bitcast(I32), kc["c_past"]).then_inc(past_loaded, 16)
                sp.wait_ge(drained[15 % 3], 16 // 3 + 2)
                sp.dma_start(down_natural.rearrange("(j s) h -> s j h", s=P), dense[:, :, :]).then_inc(stored, 16)
                sp.wait_ge(stored, 16)

            @block.gpsimd
            def _(pool):
                pool.wait_ge(stored, 16)
                for q in range(IC):
                    nc.gpsimd.indirect_dma_start(dense[:, q, :], None, down_natural,
                                                 bass.IndirectOffsetOnAxis(ap=order_idx[:, q:q + 1], axis=0)).then_inc(gathered, 16)
                pool.wait_ge(gathered, 16 * IC)

            @block.tensor
            def _(pe):
                pe.wait_ge(parts_done, 1)
                for g in range(4):
                    pe.wait_ge(t_drained[g % 2], g // 2 + 1)
                    for q in range(4):
                        ins = nc.tensor.transpose(psum[6 + g % 2][:, q * P:(q + 1) * P],
                                                  parts[:, 4 * g + q, :, :, :].rearrange("p a b c -> p (a b c)"), ident[:, :])
                    ins.then_inc(t_filled[g % 2], 1)
                pe.wait_ge(powers_done, 1)
                for n in range(16):
                    g, c, i = n // 4, n % 4, n % 3
                    pe.wait_ge(t_drained[g % 2], g // 2 + 2)
                    pe.wait_ge(drained[i], n // 3 + 1)
                    nc.tensor.matmul(psum[2 * i][:, :], powers_r[:, 2 * c, :], coef_t[:, g, :], start=True, stop=True)
                    nc.tensor.matmul(psum[2 * i + 1][:, :], powers_r[:, 2 * c + 1, :], coef_t[:, g, :],
                                     start=True, stop=True).then_inc(filled[i], 1)

            def place(n):
                g, c = n // 4, n % 4
                return view(dense[:, :, :], c * D + g * P, [[32, 4], [1, 32], [4 * D, 4]])

            @block.scalar
            def _(act):
                act.wait_ge(tabs_loaded, 32)
                nc.scalar.activation(powers_r[:, :, :], powers[:, :, :], ACT.Copy).then_inc(powers_done, 1)
                for g in range(4):
                    act.wait_ge(t_filled[g % 2], g // 2 + 1)
                    nc.scalar.activation(coef_t[:, g, :], psum[6 + g % 2][:, :], ACT.Copy).then_inc(t_drained[g % 2], 1)
                act.wait_ge(past_ready, 1)
                for n in range(16):
                    i = n % 3
                    act.wait_ge(filled[i], n // 3 + 1)
                    nc.scalar.activation(place(n), psum[2 * i][:, :].rearrange("p (a b c) -> p a b c", a=4, c=4),
                                         ACT.Copy).then_inc(before[i], 1)
                act.wait_ge(gathered, 16 * IC)
                for q in range(IC):
                    nc.scalar.activation(down_hi[:, q, :], dense[:, q, :], ACT.Copy).then_inc(high_done, 1)

            @block.vector
            def _(dve):
                for i in range(2):
                    nc.vector.nop().then_inc(t_drained[i], 1)
                for i in range(3):
                    nc.vector.nop().then_inc(drained[i], 1)
                count = [0]

                def link(ins):
                    count[0] += 1
                    ins.then_inc(step, 1)
                    dve.wait_ge(step, count[0])

                dve.wait_ge(tabs_loaded, 32)
                for c in range(4):
                    for side in range(2):
                        pr = prod[side][:, :, :, :]
                        link(nc.vector.tensor_tensor(pr, tabd[:, c, side], view(win_d[:, :, :], c + side, [[9, 16], [0, POW], [1, 5]]), ALU.mult))
                        last = nc.vector.tensor_reduce(coef[:, :, 2 * c + side, :], pr, AX.X, ALU.add)
                link(last)
                flat = coef[:, :, :, :].rearrange("p q c m -> p (q c) m")
                to = parts[:, :, :, :, :].rearrange("p q c r m -> p (q c) r m")
                for r in range(2):
                    link(nc.vector.tensor_copy(to[:, :, r, :].bitcast(F32R), flat))
                nc.vector.tensor_tensor(to[:, :, 2, :].bitcast(F32R), flat, to[:, :, 0, :], ALU.subtract)
                nc.vector.tensor_tensor(to[:, :, 3, :].bitcast(F32R), flat, to[:, :, 0, :], ALU.subtract).then_inc(parts_done, 1)
                dve.wait_ge(past_loaded, 16)
                nc.vector.tensor_copy(past[:, :, :, :].rearrange("p a b c -> p (a b c)"),
                                      dense[:, :, :].rearrange("p a b -> p (a b)").bitcast(I32)).then_inc(past_ready, 1)
                dve.wait_ge(past_ready, 1)
                for n in range(16):
                    i = n % 3
                    dve.wait_ge(before[i], n // 3 + 1)
                    nc.vector.copy_predicated(place(n), past[:, n % 4, n // 4, :].rearrange("p (a b c) -> p a b c", a=4, c=4),
                                              psum[2 * i + 1][:, :].rearrange("p (a b c) -> p a b c", a=4, c=4)).then_inc(drained[i], 1)
                for q in range(IC):
                    dve.wait_ge(high_done, q + 1)
                    last = nc.vector.tensor_tensor(down_lo[:, q, :], dense[:, q, :], down_hi[:, q, :].bitcast(F32), ALU.subtract)
                last.then_inc(low_done, 1)
                dve.wait_ge(low_done, 1)


def first_ffn(nc, alloc, sem, psum, ident, small, idle, x_tiles, out_tiles, cond_rows, cond_idx, mom,
              gu_hi, gu_lo, down_hi, down_lo):
    with ExitStack() as scope:
        sb = alloc(scope)
        x_in = sb("x_in", [P, SUB, XW])
        x_res = sb("x_res", [P, SUB, D])
        x_t = sb("x_t", [P, D])
        cond_now = sb("cond_now", [P, SUB], I32)
        cond_w = sb("cond_w", [P, SUB, SEQ])
        pair_hi, pair_lo = sb("pair_hi", [P, SUB, P], F32R), sb("pair_lo", [P, SUB, P], F32R)
        feat_hi, feat_lo = sb("feat_hi", [P, SUB, GROUPS, NF], F32R), sb("feat_lo", [P, SUB, GROUPS, NF], F32R)
        f_hi, f_lo = sb("f_hi", [NF, GROUPS, TILE], F32R), sb("f_lo", [NF, GROUPS, TILE], F32R)
        silu = [sb(f"silu{b}", [P, TILE]) for b in range(GU_BANKS)]
        inner = [sb(f"inner{b}", [P, TILE]) for b in range(INNER)]
        in_hi, in_lo = sb("in_hi", [P, RING, TILE], F32R), sb("in_lo", [P, RING, TILE], F32R)

        GU, OUT, FEAT, PREP = list(range(GU_BANKS)), [4, 5], 6, 7
        filled = [sem(f"filled{i}") for i in range(8)]
        drained = [sem(f"drained{i}") for i in range(8)]
        x_loaded, res_loaded, x1_stored = sem("x_loaded"), sem("res_loaded"), sem("x1_stored")
        pads_set, now_set = sem("pads_set"), sem("now_set")
        cond_loaded, pair_high, pair_done = sem("cond_loaded"), sem("pair_high"), sem("pair_done")
        mom_high, raw_high, f_high = (sem(n) for n in ("mom_high", "raw_high", "f_high"))
        silu_done, in_high, in_done = sem("silu_done"), sem("in_high"), sem("in_done")

        def use_feat(t, pair):
            return GROUPS // 2 * t + pair

        def use_gu(t, c):
            return IC // GU_BANKS * t + c // GU_BANKS

        def use_prep(t, s, moments):
            return 2 * SUB * t + 2 * s + moments

        PREP_AT = {2 * i: (i // 2, i % 2) for i in range(2 * SUB)}
        FEAT_AT = {8: 0, 10: 1, 12: 2, 15: 3}

        def schedule(t, has_next, has_last, chunk, down, add, prep, features):
            for c in range(IC):
                chunk(t, c)
                if c >= LAG:
                    down(t, c - LAG)
                elif has_last:
                    down(t - 1, IC + c - LAG)
                if has_last and c == LAG - 1:
                    add(t - 1)
                if has_next and c in PREP_AT:
                    prep(t + 1, *PREP_AT[c])
                if has_next and c in FEAT_AT:
                    features(t + 1, FEAT_AT[c])

        def nothing(*_):
            pass

        def steps(eng, chunk, down, add, prep, features):
            for s in range(SUB):
                prep(0, s, 0)
                prep(0, s, 1)
            for pair in range(GROUPS // 2):
                features(0, pair)
            schedule(0, True, False, chunk, down, add, prep, features)
            with eng.Fori(1, NT - 1) as t:
                schedule(t, True, True, chunk, down, add, prep, features)
            schedule(NT - 1, False, True, chunk, down, add, prep, features)
            for c in range(IC - LAG, IC):
                down(NT - 1, c)
            add(NT - 1)

        with nc.Block() as block:
            @block.sync
            def _(sp):
                def load_x(t):
                    sp.dma_start(x_in[:, :, 0:D], x_tiles[bass.ds(t, 1)].rearrange("a p s h -> p (a s) h")).then_inc(x_loaded, 16)

                def load_res(t):
                    sp.dma_start(x_res[:, :, :], x_tiles[bass.ds(t, 1)].rearrange("a p s h -> p (a s) h")).then_inc(res_loaded, 16)

                def store_x1(t):
                    for s in range(SUB):
                        sp.wait_ge(drained[OUT[s]], t + 2)
                    sp.dma_start(out_tiles[bass.ds(t, 1)].rearrange("a p s h -> p (a s) h"), x_res[:, :, :]).then_inc(x1_stored, 16)

                def next_x(t):
                    sp.wait_ge(drained[PREP], use_prep(t, SUB - 1, 1) + 2)
                    load_x(t + 1)

                def last_x1(t):
                    store_x1(t)
                    sp.wait_ge(x1_stored, 16 * (t + 1))

                load_x(0)
                load_res(0)
                next_x(0)
                next_x(1)
                with sp.Fori(1, NT - 2) as t:
                    last_x1(t - 1)
                    load_res(t)
                    next_x(t + 1)
                for t in (NT - 2, NT - 1):
                    last_x1(t - 1)
                    load_res(t)
                last_x1(NT - 1)

            @block.gpsimd
            def _(pool):
                nc.gpsimd.memset(x_in[:, :, D:XW], 0.0)
                nc.gpsimd.memset(pair_hi[:, :, :].bitcast(F32), 0.0)
                nc.gpsimd.memset(pair_lo[:, :, :].bitcast(F32), 0.0).then_inc(pads_set, 1)
                places = [0]

                def alone():
                    at = places[0]
                    places[0] += 1
                    nc.gpsimd.tensor_tensor(idle[:, at:at + 1], small[:, 0:1], small[:, 0:1], ALU.add)

                def gather_cond(t):
                    nc.gpsimd.tensor_copy(cond_now[:, :], cond_idx[:, bass.ds(SUB * t, SUB)]).then_inc(now_set, 1)
                    pool.wait_ge(now_set, t + 1)
                    alone()
                    for s in range(SUB):
                        nc.gpsimd.indirect_dma_start(cond_w[:, s, :], None, cond_rows,
                                                     bass.IndirectOffsetOnAxis(ap=cond_now[:, s:s + 1], axis=0)).then_inc(cond_loaded, 16)

                def body(t, gather):
                    for c in range(IC):
                        pool.wait_ge(in_high, IC * t + c + 1)
                        nc.gpsimd.tensor_tensor(in_lo[:, c % RING, :], inner[c % INNER][:, :], in_hi[:, c % RING, :].bitcast(F32),
                                                ALU.subtract).then_inc(in_done, 1)
                        if gather and c == IC // 2:
                            pool.wait_ge(pair_done, t + 2)
                            alone()
                            gather_cond(t + 2)

                gather_cond(0)
                pool.wait_ge(pair_done, 1)
                gather_cond(1)
                with pool.Fori(0, NT - 1) as t:
                    body(t, True)
                body(NT - 1, False)
                pool.wait_ge(cond_loaded, 16 * SUB * (NT + 1))

            @block.tensor
            def _(pe):
                def product(bank, lh, ll, rh, rl, last):
                    nc.tensor.matmul(bank, lh, rh, start=True, stop=False)
                    nc.tensor.matmul(bank, lh, rl, start=False, stop=False)
                    ins = nc.tensor.matmul(bank, ll, rh, start=False, stop=True)
                    if last is not None:
                        ins.then_inc(last, 1)

                def prep(t, s, moments):
                    if not moments and s == 0:
                        pe.wait_ge(x_loaded, 16 * (t + 1))
                    pe.wait_ge(drained[PREP], use_prep(t, s, moments) + 1)
                    for k in range(DK):
                        if moments:
                            ins = nc.tensor.matmul(psum[PREP][:, 0:GROUPS * NPOLY], x_t[:, k * P:(k + 1) * P], mom[:, k, :],
                                                   start=(k == 0), stop=(k == DK - 1))
                        else:
                            ins = nc.tensor.transpose(psum[PREP][:, k * P:(k + 1) * P], x_in[:, s, k * P:(k + 1) * P], ident[:, :])
                    ins.then_inc(filled[PREP], 1)

                def features(t, pair):
                    if pair == 0:
                        pe.wait_ge(drained[PREP], use_prep(t, SUB - 1, 1) + 2)
                        pe.wait_ge(pair_done, t + 1)
                    pe.wait_ge(drained[FEAT], use_feat(t, pair) + 1)
                    for i in range(2):
                        for s in range(SUB):
                            at = i * TILE + s * P
                            product(psum[FEAT][0:NF, at:at + P], feat_hi[:, s, 2 * pair + i, :], feat_lo[:, s, 2 * pair + i, :],
                                    pair_hi[:, s, :], pair_lo[:, s, :], filled[FEAT] if (i, s) == (1, SUB - 1) else None)

                def chunk(t, c):
                    g, bank = c * P // GROUP, GU[c % GU_BANKS]
                    if c % (2 * GROUP // P) == 0:
                        pe.wait_ge(drained[FEAT], use_feat(t, g // 2) + 2)
                    pe.wait_ge(drained[bank], use_gu(t, c) + 1)
                    cols = slice(c * P, (c + 1) * P)
                    for m in range(2):
                        product(psum[bank][:, m * TILE:(m + 1) * TILE], gu_hi[:, m, cols], gu_lo[:, m, cols], f_hi[:, g, :], f_lo[:, g, :],
                                filled[bank] if m else None)

                def down(t, c):
                    pe.wait_ge(in_done, IC * t + c + 1)
                    for s in range(SUB):
                        bank, rows = OUT[s], slice(s * P, (s + 1) * P)
                        if c == 0:
                            pe.wait_ge(drained[bank], t + 1)
                        nc.tensor.matmul(psum[bank][:, :], in_hi[:, c % RING, rows], down_hi[:, c, :], start=(c == 0), stop=False)
                        nc.tensor.matmul(psum[bank][:, :], in_hi[:, c % RING, rows], down_lo[:, c, :], start=False, stop=False)
                        ins = nc.tensor.matmul(psum[bank][:, :], in_lo[:, c % RING, rows], down_hi[:, c, :], start=False, stop=(c == IC - 1))
                        if c == IC - 1:
                            ins.then_inc(filled[bank], 1)

                steps(pe, chunk, down, nothing, prep, features)

            @block.scalar
            def _(act):
                def pairs(t):
                    act.wait_ge(cond_loaded, 16 * SUB * (t + 1))
                    for half in range(2):
                        rows = slice(64 * half, 64 * half + 64)
                        ins = nc.scalar.activation(pair_hi[rows, :, rows], cond_w[rows, :, :], ACT.Copy)
                    ins.then_inc(pair_high, 1)

                def raw(s):
                    return view(x_in[:, :, :], s * XW, [[KNOT_STEP, GROUPS], [KNOT_GAP, KNOTS], [1, KNOT_W]])

                def prep(t, s, moments):
                    act.wait_ge(filled[PREP], use_prep(t, s, moments) + 1)
                    if not moments:
                        if s == 0:
                            pairs(t)
                        nc.scalar.activation(x_t[:, :], psum[PREP][:, :], ACT.Copy).then_inc(drained[PREP], 1)
                        nc.scalar.activation(feat_hi[:, s, :, NPOLY:NF].rearrange("p g (k w) -> p g k w", k=KNOTS), raw(s),
                                             ACT.Copy).then_inc(raw_high, 1)
                    else:
                        nc.scalar.activation(feat_hi[:, s, :, 0:NPOLY], psum[PREP][:, 0:GROUPS * NPOLY].rearrange("p (g n) -> p g n", g=GROUPS),
                                             ACT.Copy).then_inc(mom_high, 1)

                def features(t, pair):
                    act.wait_ge(filled[FEAT], use_feat(t, pair) + 1)
                    nc.scalar.activation(f_hi[:, 2 * pair:2 * pair + 2, :].rearrange("p g n -> p (g n)"), psum[FEAT][0:NF, :], ACT.Copy).then_inc(f_high, 1)

                def chunk(t, c):
                    bank = GU[c % GU_BANKS]
                    act.wait_ge(filled[bank], use_gu(t, c) + 1)
                    nc.scalar.activation(silu[c % GU_BANKS][:, :], psum[bank][:, 0:TILE], ACT.Silu).then_inc(silu_done, 1)

                act.wait_ge(pads_set, 1)
                steps(act, chunk, nothing, nothing, prep, features)

            @block.vector
            def _(dve):
                for i in range(8):
                    nc.vector.nop().then_inc(drained[i], 1)

                def pairs(t):
                    dve.wait_ge(pair_high, t + 1)
                    for half in range(2):
                        rows = slice(64 * half, 64 * half + 64)
                        ins = nc.vector.tensor_tensor(pair_lo[rows, :, rows], cond_w[rows, :, :], pair_hi[rows, :, rows].bitcast(F32), ALU.subtract)
                    ins.then_inc(pair_done, 1)

                def prep(t, s, moments):
                    if not moments:
                        if s == 0:
                            pairs(t)
                        dve.wait_ge(raw_high, SUB * t + s + 1)
                        raw = view(x_in[:, :, :], s * XW, [[KNOT_STEP, GROUPS], [KNOT_GAP, KNOTS], [1, KNOT_W]])
                        part = lambda f: f[:, s, :, NPOLY:NF].rearrange("p g (k w) -> p g k w", k=KNOTS)
                        nc.vector.tensor_tensor(part(feat_lo), raw, part(feat_hi).bitcast(F32), ALU.subtract)
                    else:
                        dve.wait_ge(mom_high, SUB * t + s + 1)
                        nc.vector.tensor_tensor(feat_lo[:, s, :, 0:NPOLY], psum[PREP][:, 0:GROUPS * NPOLY].rearrange("p (g n) -> p g n", g=GROUPS),
                                                feat_hi[:, s, :, 0:NPOLY].bitcast(F32), ALU.subtract).then_inc(drained[PREP], 1)

                def features(t, pair):
                    dve.wait_ge(f_high, GROUPS // 2 * t + pair + 1)
                    flat = lambda f: f[:, 2 * pair:2 * pair + 2, :].rearrange("p g n -> p (g n)")
                    nc.vector.tensor_tensor(flat(f_lo), psum[FEAT][0:NF, :], flat(f_hi).bitcast(F32), ALU.subtract).then_inc(drained[FEAT], 1)

                def high_inner(t, c):
                    dve.wait_ge(drained[GU[c % GU_BANKS]], use_gu(t, c) + 2)
                    nc.vector.tensor_copy(in_hi[:, c % RING, :], inner[c % INNER][:, :]).then_inc(in_high, 1)

                def chunk(t, c):
                    bank = GU[c % GU_BANKS]
                    dve.wait_ge(silu_done, IC * t + c + 1)
                    if not isinstance(t, int) or t > 0 or c >= INNER:
                        dve.wait_ge(in_done, IC * t + c - INNER + 1)
                    nc.vector.tensor_tensor(inner[c % INNER][:, :], silu[c % GU_BANKS][:, :], psum[bank][:, TILE:2 * TILE],
                                            ALU.mult).then_inc(drained[bank], 1)
                    high_inner(t, c)

                def add(t):
                    dve.wait_ge(res_loaded, 16 * (t + 1))
                    for s in range(SUB):
                        dve.wait_ge(filled[OUT[s]], t + 1)
                        nc.vector.tensor_tensor(x_res[:, s, :], psum[OUT[s]][:, :], x_res[:, s, :], ALU.add).then_inc(drained[OUT[s]], 1)

                dve.wait_ge(pads_set, 1)
                steps(dve, chunk, nothing, add, prep, features)


def adapted_layer(nc, alloc, sem, psum, ident, small, idle, lower, ones, tok_ids, layer_tiles, z_tiles, w_hi, w_lo, a_hi, a_lo,
                  b_hi, b_lo, r_hi, r_lo, adapter_scale, chosen, table_dram):
    with ExitStack() as scope:
        sb = alloc(scope)
        x1 = [sb(f"x1_{b}", [P, LSUB, D]) for b in range(2)]
        x1t_hi = [sb(f"x1t_hi{b}", [P, DK, LTILE], F32R) for b in range(2)]
        x1t_lo = [sb(f"x1t_lo{b}", [P, DK, LTILE], F32R) for b in range(2)]
        xa = sb("xa", [P, LTILE])
        xa_hi, xa_lo = sb("xa_hi", [P, LTILE], F32R), sb("xa_lo", [P, LTILE], F32R)
        z_out = [sb(f"z_out{b}", [P, LSUB, D]) for b in range(2)]
        logits_t, logits = sb("logits_t", [NE, LTILE]), sb("logits", [P, LSUB, NE])
        top1, top2, at = sb("top1", [P, LSUB]), sb("top2", [P, LSUB]), sb("at", [P, LSUB])
        below, masked = sb("below", [P, LSUB, NE]), sb("masked", [P, LSUB, NE])
        picked = [sb(f"picked{k}", [P, LSUB, NE]) for k in range(2)]
        both, pos, row_f = sb("both", [P, LSUB, NE]), sb("pos", [P, LSUB, NE]), sb("row_f", [P, 2, LSUB])
        gap, expo, total = sb("gap", [P, LSUB]), sb("expo", [P, LSUB]), sb("total", [P, LSUB])
        row_i, entry = sb("row_i", [P, 2, LSUB], I32), sb("entry", [P, LSUB, 2, 2])

        X1T, XA, TR, Z = [0, 1, 2, 3], 4, 5, [6, 7]
        filled = [sem(f"al_filled{i}") for i in range(8)]
        drained = [sem(f"al_drained{i}") for i in range(8)]
        x1_loaded, z_stored = [[sem(f"al_{n}{b}") for b in range(2)] for n in ("x1_loaded", "z_stored")]
        x1t_high, xa_high, xa_done = sem("x1t_high"), sem("xa_high"), sem("xa_done")
        idle_done, chosen_set, step, both_ready = sem("idle_done"), sem("chosen_set"), sem("route_step"), sem("both_ready")
        gap_ready, expo_ready, entries_ready, entries_stored = (sem(n) for n in ("gap_ready", "expo_ready", "entries_ready", "entries_stored"))
        LINKS = 23

        def use_z(t, s):
            return LSUB // 2 * t + s // 2

        def pairs_of_steps(eng, body):
            body(0, 0, 0, True, True)
            body(1, 0, 1, True, True)
            with eng.Fori(1, LNT // 2 - 1) as k:
                for b in range(2):
                    body(2 * k + b, k, b, True, False)
            body(LNT - 2, LNT // 2 - 1, 0, True, False)
            body(LNT - 1, LNT // 2 - 1, 1, False, False)

        with nc.Block() as block:
            @block.sync
            def _(sp):
                def load(t, b):
                    sp.dma_start(x1[b][:, :, :], layer_tiles[bass.ds(t, 1)].rearrange("a p s h -> p (a s) h")).then_inc(x1_loaded[b], 16)

                def body(t, n, b, has_next, first):
                    if has_next:
                        if not (first and b == 0):
                            sp.wait_ge(filled[X1T[LSUB - 1]], t)
                        load(t + 1, 1 - b)

                load(0, 0)
                pairs_of_steps(sp, body)
                for b in range(2):
                    sp.wait_ge(z_stored[b], 16 * LNT // 2)

            @block.gpsimd
            def _(pool):
                def body(t, n, b, has_next, first):
                    if not (first and b == 0):
                        pool.wait_ge(idle_done, t)
                    pool.wait_ge(entries_ready, t + 1)
                    nc.gpsimd.tensor_tensor(idle[:, 0:1], small[:, 0:1], small[:, 0:1], ALU.add).then_inc(idle_done, 1)
                    for k in range(2):
                        for s in range(LSUB):
                            nc.gpsimd.indirect_dma_start(table_dram, bass.IndirectOffsetOnAxis(ap=row_i[:, k, s:s + 1], axis=0),
                                                         entry[:, s, k, :], None).then_inc(entries_stored, 16)

                pairs_of_steps(pool, body)
                pool.wait_ge(entries_stored, 16 * 2 * LSUB * LNT)

            @block.tensor
            def _(pe):
                def product(bank, pairs, last):
                    n = len(pairs)
                    for i, (lh, ll, rh, rl) in enumerate(pairs):
                        nc.tensor.matmul(bank, lh, rh, start=(i == 0), stop=False)
                        nc.tensor.matmul(bank, lh, rl, start=False, stop=False)
                        ins = nc.tensor.matmul(bank, ll, rh, start=False, stop=(i == n - 1))
                    ins.then_inc(last, 1)

                def transpose(t, n, b):
                    pe.wait_ge(x1_loaded[b], 16 * (n + 1))
                    for s in range(LSUB):
                        bank = X1T[s]
                        pe.wait_ge(drained[bank], t + 1)
                        for k in range(DK):
                            ins = nc.tensor.transpose(psum[bank][:, k * P:(k + 1) * P], x1[b][:, s, k * P:(k + 1) * P], ident[:, :])
                        ins.then_inc(filled[bank], 1)

                def body(t, n, b, has_next, first):
                    for s in range(LSUB):
                        pe.wait_ge(drained[X1T[s]], t + 2)
                    hi, lo = x1t_hi[b], x1t_lo[b]
                    pe.wait_ge(drained[XA], 2 * t + 1)
                    product(psum[XA][:, :], [(a_hi[:, k, :], a_lo[:, k, :], hi[:, k, :], lo[:, k, :]) for k in range(DK)], filled[XA])
                    if has_next:
                        transpose(t + 1, n + b, 1 - b)
                    pe.wait_ge(xa_done, t + 1)
                    pe.wait_ge(drained[TR], 2 * t + 1)
                    product(psum[TR][0:NE, :], [(r_hi[:, k, :], r_lo[:, k, :], hi[:, k, :], lo[:, k, :]) for k in range(DK)]
                            + [(r_hi[:, DK, :], r_lo[:, DK, :], xa_hi[:, :], xa_lo[:, :])], filled[TR])
                    for s in range(LSUB):
                        rows = slice(s * P, (s + 1) * P)
                        if s == 1:
                            pe.wait_ge(drained[TR], 2 * t + 2)
                            pe.wait_ge(drained[XA], 2 * t + 2)
                        pe.wait_ge(drained[Z[s % 2]], use_z(t, s) + 1)
                        product(psum[Z[s % 2]][:, :], [(hi[:, k, rows], lo[:, k, rows], w_hi[:, k, :], w_lo[:, k, :]) for k in range(DK)]
                                + [(xa_hi[:, rows], xa_lo[:, rows], b_hi[:, :], b_lo[:, :])], filled[Z[s % 2]])
                        if s == 1:
                            for i in range(LSUB):
                                ins = nc.tensor.transpose(psum[XA][:, i * NE:(i + 1) * NE], logits_t[:, i * P:(i + 1) * P], ident[0:NE, 0:NE])
                            ins.then_inc(filled[XA], 1)
                        if s == LSUB - 1:
                            pe.wait_ge(both_ready, t + 1)
                            nc.tensor.matmul(psum[TR][:, 0:LSUB * NE], lower[:, :], both[:, :, :].rearrange("p s e -> p (s e)"), start=True, stop=False)
                            nc.tensor.matmul(psum[TR][:, 0:LSUB * NE], ones[:, :], chosen[:, 0:LSUB, :].rearrange("p s e -> p (s e)"),
                                             start=False, stop=True).then_inc(filled[TR], 1)

                transpose(0, 0, 0)
                pairs_of_steps(pe, body)

            @block.scalar
            def _(act):
                def transpose(t, b):
                    for s in range(LSUB):
                        act.wait_ge(filled[X1T[s]], t + 1)
                        nc.scalar.activation(x1t_hi[b][:, :, s * P:(s + 1) * P], psum[X1T[s]][:, :].rearrange("p (k n) -> p k n", k=DK),
                                             ACT.Copy).then_inc(x1t_high, 1)

                def body(t, n, b, has_next, first):
                    act.wait_ge(drained[XA], 2 * t + 2)
                    nc.scalar.activation(xa_hi[:, :], xa[:, :], ACT.Copy).then_inc(xa_high, 1)
                    if has_next:
                        transpose(t + 1, 1 - b)
                    act.wait_ge(filled[TR], 2 * t + 1)
                    nc.scalar.activation(logits_t[:, :], psum[TR][0:NE, :], ACT.Copy).then_inc(drained[TR], 1)
                    if not first:
                        act.wait_ge(z_stored[b], 16 * n)
                    for s in range(LSUB):
                        act.wait_ge(filled[Z[s % 2]], use_z(t, s) + 1)
                        nc.scalar.activation(z_out[b][:, s, :], psum[Z[s % 2]][:, :], ACT.Copy).then_inc(drained[Z[s % 2]], 1)
                        if s == LSUB - 1:
                            act.wait_ge(gap_ready, t + 1)
                            nc.scalar.activation(expo[:, :], gap[:, :], ACT.Exp).then_inc(expo_ready, 1)
                    for s in (LSUB - 2, LSUB - 1):
                        act.wait_ge(drained[Z[s % 2]], use_z(t, s) + 2)
                    act.dma_start(z_tiles[bass.ds(t, 1)].rearrange("a p s h -> p (a s) h"), z_out[b][:, :, :]).then_inc(z_stored[b], 16)

                transpose(0, 0)
                pairs_of_steps(act, body)

            @block.vector
            def _(dve):
                for i in range(8):
                    nc.vector.nop().then_inc(drained[i], 1)
                nc.vector.memset(chosen[:, :, :], 0.0).then_inc(chosen_set, 1)
                dve.wait_ge(chosen_set, 1)

                def transpose(t, b):
                    for s in range(LSUB):
                        cols = slice(s * P, (s + 1) * P)
                        dve.wait_ge(x1t_high, LSUB * t + s + 1)
                        nc.vector.tensor_tensor(x1t_lo[b][:, :, cols], psum[X1T[s]][:, :].rearrange("p (k n) -> p k n", k=DK),
                                                x1t_hi[b][:, :, cols].bitcast(F32), ALU.subtract).then_inc(drained[X1T[s]], 1)

                wide = lambda ap: ap.rearrange("p (n e) -> p n e", e=1).to_broadcast([P, LSUB, NE])
                iota = view(small[:, :], 16, [[0, LSUB], [1, NE]])

                def route(t, first):
                    links = [0]

                    def link(ins):
                        links[0] += 1
                        ins.then_inc(step, 1)
                        dve.wait_ge(step, LINKS * t + links[0])

                    def pick(values, top, k):
                        link(nc.vector.tensor_reduce(top[:, :], values[:, :, :], AX.X, ALU.max))
                        link(nc.vector.tensor_tensor(below[:, :, :], values[:, :, :], wide(top[:, :]), ALU.is_lt))
                        link(nc.vector.scalar_tensor_tensor(below[:, :, :], below[:, :, :], float(NE), iota, ALU.mult, ALU.add))
                        link(nc.vector.tensor_reduce(at[:, :], below[:, :, :], AX.X, ALU.min))
                        link(nc.vector.tensor_tensor(picked[k][:, :, :], iota, wide(at[:, :]), ALU.is_equal))

                    dve.wait_ge(filled[XA], 2 * t + 2)
                    nc.vector.tensor_copy(logits[:, :, :], psum[XA][:, 0:LSUB * NE].rearrange("p (s e) -> p s e", s=LSUB)).then_inc(drained[XA], 1)
                    dve.wait_ge(drained[XA], 2 * t + 3)
                    pick(logits, top1, 0)
                    link(nc.vector.scalar_tensor_tensor(masked[:, :, :], picked[0][:, :, :], -3e38, logits[:, :, :], ALU.mult, ALU.add))
                    pick(masked, top2, 1)
                    nc.vector.tensor_tensor(gap[:, :], top2[:, :], top1[:, :], ALU.subtract).then_inc(gap_ready, 1)
                    nc.vector.tensor_copy(chosen[:, 0, :], chosen[:, LSUB, :])
                    link(nc.vector.tensor_tensor(both[:, :, :], picked[0][:, :, :], picked[1][:, :, :], ALU.add))
                    for s in range(LSUB):
                        link(nc.vector.tensor_tensor(chosen[:, s + 1, :], chosen[:, s, :], both[:, s, :], ALU.add))
                    nc.vector.nop().then_inc(both_ready, 1)
                    dve.wait_ge(filled[TR], 2 * t + 2)
                    nc.vector.scalar_tensor_tensor(pos[:, :, :], iota, float(REGION * P), psum[TR][:, 0:LSUB * NE].rearrange("p (s e) -> p s e", s=LSUB),
                                                   ALU.mult, ALU.add).then_inc(drained[TR], 1)
                    dve.wait_ge(drained[TR], 2 * t + 3)
                    for k in range(2):
                        link(nc.vector.tensor_tensor(picked[k][:, :, :], picked[k][:, :, :], pos[:, :, :], ALU.mult))
                        link(nc.vector.tensor_reduce(row_f[:, k, :], picked[k][:, :, :], AX.X, ALU.add))
                    if not first:
                        dve.wait_ge(entries_stored, 16 * 2 * LSUB * t)
                    nc.vector.tensor_copy(row_i[:, :, :], row_f[:, :, :])
                    for k in range(2):
                        nc.vector.tensor_copy(entry[:, :, k, 0], tok_ids[:, bass.ds(LSUB * t, LSUB)])
                    dve.wait_ge(expo_ready, t + 1)
                    link(nc.vector.tensor_scalar(total[:, :], expo[:, :], 1.0, None, ALU.add))
                    link(nc.vector.reciprocal(entry[:, :, 0, 1], total[:, :]))
                    link(nc.vector.tensor_tensor(entry[:, :, 1, 1], expo[:, :], entry[:, :, 0, 1], ALU.mult))
                    nc.vector.nop().then_inc(entries_ready, 1)
                    assert links[0] == LINKS, links[0]

                def body(t, n, b, has_next, first):
                    dve.wait_ge(filled[XA], 2 * t + 1)
                    batches = LTILE // SEQ
                    own = adapter_scale[:, bass.ds(batches * t, batches)]
                    nc.vector.tensor_tensor(xa[:, :].rearrange("p (b c) -> p b c", b=batches), psum[XA][:, :].rearrange("p (b c) -> p b c", b=batches),
                                            own.rearrange("p (b c) -> p b c", c=1).to_broadcast([P, batches, SEQ]), ALU.mult).then_inc(drained[XA], 1)
                    dve.wait_ge(xa_high, t + 1)
                    nc.vector.tensor_tensor(xa_lo[:, :], xa[:, :], xa_hi[:, :].bitcast(F32), ALU.subtract).then_inc(xa_done, 1)
                    if has_next:
                        transpose(t + 1, 1 - b)
                    route(t, first and b == 0)

                transpose(0, 0)
                pairs_of_steps(dve, body)


def experts(nc, alloc, sem, psum, ident, small, idle, ones, chosen, expert_dram, table_dram, z_dram, out):
    with ExitStack() as scope:
        sb = alloc(scope)
        slots = sb("slots", [P, SLOTS, EW], F32R)
        count, blocks_from = sb("count", [P, NE]), sb("blocks_from", [P, MAX_BLOCKS])
        full_blocks = sb("full_blocks", [P, NE, MAX_BLOCKS])
        n_blocks, ends = sb("n_blocks", [P, NE]), [sb(f"ends{b}", [P, NE]) for b in range(2)]
        past_end, past_blocks = sb("past_end", [P, COLS, NE - 1]), sb("past_blocks", [P, COLS, NE - 1])
        expert_f, start_f, wrapped = sb("expert_f", [P, COLS]), sb("start_f", [P, COLS]), sb("wrapped", [P, COLS])
        column = sb("column", [P, COLS])
        ctl_f = sb("ctl_f", [P, 2 * COLS + NE])
        ctl = sb("ctl", [P, 2 * COLS + NE], I32)
        CHUNKS = -(-NE * REGION // P)
        REST = NE * REGION - (CHUNKS - 1) * P
        columns, chosen_at = sb("columns", [P, CHUNKS, P, 2]), sb("chosen_at", [P, CHUNKS, COLS])
        row_of, share_of = sb("row_of", [P, COLS], I32), sb("share_of", [P, COLS])
        z_now = [sb(f"z_now{b}", [P, D]) for b in range(2)]
        gather_at = [sb(f"gather_at{b}", [P, 1], I32) for b in range(2)]
        scatter_at = [sb(f"scatter_at{b}", [P, 1], I32) for b in range(2)]
        zt_hi, zt_lo = sb("zt_hi", [P, DK, P], F32R), sb("zt_lo", [P, DK, P], F32R)
        silu_g, hid = sb("silu_g", [P, FD]), sb("hid", [P, FP])
        ht_hi, ht_lo = sb("ht_hi", [P, FC, P], F32R), sb("ht_lo", [P, FC, P], F32R)
        result = [sb(f"result{b}", [P, D]) for b in range(2)]

        step, counted, columns_loaded = sem("place_step"), sem("counted"), sem("columns_loaded")
        column_ready, sorted_filled, table_ready, hid_set = sem("column_ready"), sem("sorted_filled"), sem("table_ready"), sem("hid_set")
        ctl_ready, weights_loaded = sem("ctl_ready"), sem("weights_loaded")
        ZT, GATE, UP, HT, OUT, COUNTS, SORTED = 0, 1, 2, 3, [4, 5], 6, 7
        filled = [sem(f"ex_filled{i}") for i in range(6)]
        drained = [sem(f"ex_drained{i}") for i in range(6)]
        z_loaded = [sem(f"ex_z_loaded{b}") for b in range(2)]
        zt_high, ht_high = sem("zt_high"), sem("ht_high")
        gather_set, scatter_set, added = sem("gather_set"), sem("scatter_set"), sem("added")

        with nc.Block() as block:
            @block.sync
            def _(sp):
                full = table_dram[0:(CHUNKS - 1) * P * P, :].rearrange("(c q p) w -> q c (p w)", q=P, p=P)
                sp.dma_start(columns[:, 0:CHUNKS - 1, :, :].rearrange("q c p w -> q c (p w)"), full).then_inc(columns_loaded, 16)
                sp.dma_start(columns[0:REST, CHUNKS - 1, :, :].rearrange("q p w -> q (p w)"),
                             table_dram[(CHUNKS - 1) * P * P:, :].rearrange("(q p) w -> q (p w)", p=P)).then_inc(columns_loaded, 16)
                for e in range(NE):
                    if e >= SLOTS:
                        if e == SLOTS:
                            sp.wait_ge(ctl_ready, 1)
                        end = 2 * COLS + e - SLOTS
                        blocks = sp.value_load(ctl[0:1, end:end + 1], min_val=1, max_val=BLOCKS)
                        sp.wait_ge(filled[HT], blocks + 1)
                    sp.dma_start(slots[:, e % SLOTS, :].bitcast(F32), expert_dram[e]).then_inc(weights_loaded, 16)
                    sp.wait_ge(weights_loaded, 16 * (e + 1))

            @block.gpsimd
            def _(pool):
                nc.gpsimd.memset(hid[:, :], 0.0).then_inc(hid_set, 1)
                pool.wait_ge(table_ready, 1)
                places = [0]

                def alone():
                    at = places[0]
                    places[0] += 1
                    nc.gpsimd.tensor_tensor(idle[:, at:at + 1], small[:, 0:1], small[:, 0:1], ALU.add)


                def gather(j, b):
                    nc.gpsimd.tensor_copy(gather_at[b][:, :], row_of[:, bass.ds(j, 1)]).then_inc(gather_set, 1)
                    pool.wait_ge(gather_set, j + 1)
                    alone()
                    nc.gpsimd.indirect_dma_start(z_now[b][:, :], None, z_dram,
                                                 bass.IndirectOffsetOnAxis(ap=gather_at[b][:, 0:1], axis=0)).then_inc(z_loaded[b], 16)

                def set_scatter(j, b):
                    nc.gpsimd.tensor_copy(scatter_at[b][:, :], row_of[:, bass.ds(j, 1)]).then_inc(scatter_set, 1)

                def scatter(j, n, b, first):
                    if not first:
                        pool.wait_ge(added, 16 * j)
                        alone()
                    pool.wait_ge(scatter_set, j + 1)
                    pool.wait_ge(drained[OUT[b]], n + 2)
                    alone()
                    nc.gpsimd.indirect_dma_start(out, bass.IndirectOffsetOnAxis(ap=scatter_at[b][:, 0:1], axis=0),
                                                 result[b][:, :], None, compute_op=ALU.add).then_inc(added, 16)

                def body(j, n, b, more, first):
                    set_scatter(j - 1, 1 - b)
                    if more:
                        pool.wait_ge(filled[ZT], j + 1)
                        alone()
                        gather(j + 2, b)
                    scatter(j - 1, n - 1 + b, 1 - b, first)

                gather(0, 0)
                gather(1, 1)
                pool.wait_ge(filled[ZT], 1)
                gather(2, 0)
                body(1, 0, 1, True, True)
                body(2, 1, 0, True, False)
                with pool.Fori(1, BLOCKS // 2) as k:
                    body(2 * k + 1, k, 1, True, False)
                    body(2 * k + 2, k + 1, 0, True, False)
                set_scatter(BLOCKS - 1, 0)
                scatter(BLOCKS - 1, BLOCKS // 2, 0, False)
                pool.wait_ge(added, 16 * BLOCKS)
                for b in range(2):
                    pool.wait_ge(z_loaded[b], 16 * ((COLS - b + 1) // 2))

            @block.tensor
            def _(pe):
                nc.tensor.matmul(psum[COUNTS][:, 0:NE], ones[:, :], chosen[:, LSUB, :], start=True, stop=True).then_inc(counted, 1)
                pe.wait_ge(columns_loaded, 32)
                pe.wait_ge(column_ready, 1)
                for w in range(2):
                    for c in range(CHUNKS):
                        rows = P if c < CHUNKS - 1 else REST
                        ins = nc.tensor.matmul(psum[SORTED][:, w * COLS:(w + 1) * COLS], columns[0:rows, c, :, w], chosen_at[0:rows, c, :],
                                               start=(c == 0), stop=(c == CHUNKS - 1))
                ins.then_inc(sorted_filled, 1)
                pe.wait_ge(hid_set, 1)

                def transpose_z(j, n, b):
                    pe.wait_ge(z_loaded[b], 16 * (n + 1))
                    pe.wait_ge(drained[ZT], j + 1)
                    for k in range(DK):
                        ins = nc.tensor.transpose(psum[ZT][:, k * P:(k + 1) * P], z_now[b][:, k * P:(k + 1) * P], ident[:, :])
                    ins.then_inc(filled[ZT], 1)

                def gate_up(j, slot):
                    pe.wait_ge(drained[ZT], j + 2)
                    for bank, high, low in ((GATE, GH, GL), (UP, UH, UL)):
                        pe.wait_ge(drained[bank], j + 1)
                        for k in range(DK):
                            w_high = slots[:, bass.ds(slot, 1), high + k * FD:high + (k + 1) * FD].rearrange("p a n -> p (a n)")
                            w_low = slots[:, bass.ds(slot, 1), low + k * FD:low + (k + 1) * FD].rearrange("p a n -> p (a n)")
                            nc.tensor.matmul(psum[bank][:, 0:FD], zt_hi[:, k, :], w_high, start=(k == 0), stop=False)
                            nc.tensor.matmul(psum[bank][:, 0:FD], zt_hi[:, k, :], w_low, start=False, stop=False)
                            ins = nc.tensor.matmul(psum[bank][:, 0:FD], zt_lo[:, k, :], w_high, start=False, stop=(k == DK - 1))
                        ins.then_inc(filled[bank], 1)

                def transpose_h(j):
                    pe.wait_ge(drained[UP], j + 2)
                    pe.wait_ge(drained[HT], j + 1)
                    for f in range(FC):
                        ins = nc.tensor.transpose(psum[HT][:, f * P:(f + 1) * P], hid[:, f * P:(f + 1) * P], ident[:, :])
                    ins.then_inc(filled[HT], 1)

                def down(j, n, b, slot):
                    pe.wait_ge(drained[HT], j + 2)
                    pe.wait_ge(drained[OUT[b]], n + 1)
                    for f in range(FC):
                        w_high = slots[:, bass.ds(slot, 1), DH_ + f * D:DH_ + (f + 1) * D].rearrange("p a n -> p (a n)")
                        w_low = slots[:, bass.ds(slot, 1), DL_ + f * D:DL_ + (f + 1) * D].rearrange("p a n -> p (a n)")
                        nc.tensor.matmul(psum[OUT[b]][:, :], ht_hi[:, f, :], w_high, start=(f == 0), stop=False)
                        nc.tensor.matmul(psum[OUT[b]][:, :], ht_hi[:, f, :], w_low, start=False, stop=False)
                        ins = nc.tensor.matmul(psum[OUT[b]][:, :], ht_lo[:, f, :], w_high, start=False, stop=(f == FC - 1))
                    ins.then_inc(filled[OUT[b]], 1)

                def slot_of(j):
                    pe.wait_ge(ctl_ready, 1)
                    return pe.value_load(ctl[0:1, bass.ds(j, 1)], min_val=0, max_val=SLOTS - 1)

                def wait_weights(j):
                    pe.wait_ge(ctl_ready, 1)
                    loaded = pe.value_load(ctl[0:1, bass.ds(j + COLS, 1)], min_val=16, max_val=16 * NE)
                    pe.wait_ge(weights_loaded, loaded)

                def body(j, n, b):
                    transpose_h(j - 1)
                    now = slot_of(j)
                    wait_weights(j)
                    gate_up(j, now)
                    transpose_z(j + 1, n + b, 1 - b)
                    down(j - 1, n - 1 + b, 1 - b, slot_of(j - 1))

                transpose_z(0, 0, 0)
                first = slot_of(0)
                wait_weights(0)
                gate_up(0, first)
                transpose_z(1, 0, 1)
                with pe.Fori(0, BLOCKS // 2) as k:
                    body(2 * k + 1, k, 1)
                    body(2 * k + 2, k + 1, 0)
                transpose_h(BLOCKS - 1)
                down(BLOCKS - 1, BLOCKS // 2, 0, slot_of(BLOCKS - 1))

            @block.scalar
            def _(act):
                def high_h(j):
                    act.wait_ge(filled[HT], j + 1)
                    nc.scalar.activation(ht_hi[:, :, :].rearrange("p f n -> p (f n)"), psum[HT][:, 0:FP], ACT.Copy).then_inc(ht_high, 1)

                def gate(j):
                    act.wait_ge(filled[GATE], j + 1)
                    act.wait_ge(drained[UP], j + 1)
                    nc.scalar.activation(silu_g[:, :], psum[GATE][:, 0:FD], ACT.Silu).then_inc(drained[GATE], 1)

                def high_z(j):
                    act.wait_ge(filled[ZT], j + 1)
                    nc.scalar.activation(zt_hi[:, :, :].rearrange("p k n -> p (k n)"), psum[ZT][:, :], ACT.Copy).then_inc(zt_high, 1)

                high_z(0)
                gate(0)
                high_z(1)
                with act.Fori(1, BLOCKS) as j:
                    high_h(j - 1)
                    gate(j)
                    high_z(j + 1)
                high_h(BLOCKS - 1)

            @block.vector
            def _(dve):
                for i in range(6):
                    nc.vector.nop().then_inc(drained[i], 1)
                links = [0]

                def link(ins):
                    links[0] += 1
                    ins.then_inc(step, 1)
                    dve.wait_ge(step, links[0])

                def prefix(a, spare, n):
                    d = 1
                    while d < n:
                        nc.vector.tensor_copy(spare[:, 0:d, :], a[:, 0:d, :])
                        link(nc.vector.tensor_tensor(spare[:, d:n, :], a[:, d:n, :], a[:, 0:n - d, :], ALU.add))
                        a, spare, d = spare, a, 2 * d
                    return a

                dve.wait_ge(counted, 1)
                link(nc.vector.tensor_scalar(count[:, :], psum[COUNTS][:, 0:NE], 1.0, None, ALU.max))
                link(nc.vector.tensor_scalar(blocks_from[:, :], small[:, 24:24 + MAX_BLOCKS], float(P), None, ALU.mult))
                link(nc.vector.tensor_tensor(full_blocks[:, :, :], view(count[:, :], 0, [[1, NE], [0, MAX_BLOCKS]]),
                                             view(blocks_from[:, :], 0, [[0, NE], [1, MAX_BLOCKS]]), ALU.is_gt))
                link(nc.vector.tensor_reduce(n_blocks[:, :], full_blocks[:, :, :], AX.X, ALU.add))
                link(nc.vector.tensor_copy(ends[0][:, :], n_blocks[:, :]))
                tall = lambda t: t[:, :].rearrange("p (e a) -> p e a", a=1)
                end = prefix(tall(ends[0]), tall(ends[1]), NE).rearrange("p e a -> p (e a)")
                link(nc.vector.tensor_tensor(past_end[:, :, :], view(small[:, :], 24, [[1, COLS], [0, NE - 1]]),
                                             view(end, 0, [[0, COLS], [1, NE - 1]]), ALU.is_ge))
                link(nc.vector.tensor_tensor(past_blocks[:, :, :], past_end[:, :, :], view(n_blocks[:, :], 0, [[0, COLS], [1, NE - 1]]), ALU.mult))
                nc.vector.tensor_reduce(expert_f[:, :], past_end[:, :, :], AX.X, ALU.add)
                link(nc.vector.tensor_reduce(start_f[:, :], past_blocks[:, :, :], AX.X, ALU.add))
                link(nc.vector.tensor_tensor(column[:, :], small[:, 24:24 + COLS], start_f[:, :], ALU.subtract))
                link(nc.vector.tensor_scalar(column[:, :], column[:, :], float(MAX_BLOCKS), None, ALU.min))
                link(nc.vector.scalar_tensor_tensor(column[:, :], expert_f[:, :], float(REGION), column[:, :], ALU.mult, ALU.add))
                for c in range(CHUNKS):
                    ins = nc.vector.tensor_scalar(chosen_at[:, c, :], column[:, :], small[:, 2 + c:3 + c], None, ALU.is_equal)
                ins.then_inc(column_ready, 1)
                link(nc.vector.tensor_copy(ctl_f[:, 0:COLS], expert_f[:, :]))
                for first in range(SLOTS, NE, SLOTS):
                    link(nc.vector.tensor_scalar(wrapped[:, :], expert_f[:, :], float(first), float(SLOTS), ALU.is_ge, ALU.mult))
                    link(nc.vector.tensor_tensor(ctl_f[:, 0:COLS], ctl_f[:, 0:COLS], wrapped[:, :], ALU.subtract))
                nc.vector.tensor_scalar(ctl_f[:, COLS:2 * COLS], expert_f[:, :], 16.0, 16.0, ALU.mult, ALU.add)
                link(nc.vector.tensor_copy(ctl_f[:, 2 * COLS:2 * COLS + NE], end))
                nc.vector.tensor_copy(ctl[:, :], ctl_f[:, :]).then_inc(ctl_ready, 1)
                dve.wait_ge(sorted_filled, 1)
                nc.vector.tensor_copy(share_of[:, :], psum[SORTED][:, COLS:2 * COLS])
                nc.vector.tensor_copy(row_of[:, :], psum[SORTED][:, 0:COLS]).then_inc(table_ready, 1)
                dve.wait_ge(table_ready, 1)

                def low_z(j):
                    dve.wait_ge(zt_high, j + 1)
                    nc.vector.tensor_tensor(zt_lo[:, :, :].rearrange("p k n -> p (k n)"), psum[ZT][:, :],
                                            zt_hi[:, :, :].rearrange("p k n -> p (k n)").bitcast(F32), ALU.subtract).then_inc(drained[ZT], 1)

                def low_h(j):
                    dve.wait_ge(ht_high, j + 1)
                    nc.vector.tensor_tensor(ht_lo[:, :, :].rearrange("p f n -> p (f n)"), psum[HT][:, 0:FP],
                                            ht_hi[:, :, :].rearrange("p f n -> p (f n)").bitcast(F32), ALU.subtract).then_inc(drained[HT], 1)

                def multiply(j):
                    dve.wait_ge(drained[GATE], j + 2)
                    dve.wait_ge(filled[UP], j + 1)
                    nc.vector.tensor_tensor(hid[:, 0:FD], silu_g[:, :], psum[UP][:, 0:FD], ALU.mult).then_inc(drained[UP], 1)

                def weigh(j, n, b, first):
                    dve.wait_ge(filled[OUT[b]], n + 1)
                    if not first:
                        dve.wait_ge(added, 16 * (j - 1))
                    nc.vector.tensor_tensor(result[b][:, :], psum[OUT[b]][:, :], share_of[:, bass.ds(j, 1)].to_broadcast([P, D]),
                                            ALU.mult).then_inc(drained[OUT[b]], 1)

                def body(j, n, b, first):
                    low_h(j - 1)
                    multiply(j)
                    low_z(j + 1)
                    weigh(j - 1, n - 1 + b, 1 - b, first)

                low_z(0)
                multiply(0)
                low_z(1)
                body(1, 0, 1, True)
                body(2, 1, 0, True)
                with dve.Fori(1, BLOCKS // 2) as k:
                    body(2 * k + 1, k, 1, False)
                    body(2 * k + 2, k + 1, 0, False)
                low_h(BLOCKS - 1)
                weigh(BLOCKS - 1, BLOCKS // 2, 0, False)


NAMES = {"x": "x", "cond": "itok_B_1_198", "adapter": "itok_B_0_6", "cond_w": "L0_cond_weights",
         "gate_cp": "L0_ffn_gate_cp", "up_cp": "L0_ffn_up_cp", "down_cp": "L0_ffn_down_cp",
         "W": "L1_cond_W", "A": "L1_cond_A", "Bm": "L1_cond_Bm", "scalings": "L1_cond_scalings",
         "router_w": "L1_ffn_gate_w", "gate_proj": "L1_ffn_gate_proj", "up_proj": "L1_ffn_up_proj", "down_proj": "L1_ffn_down_proj"}


def kernel(**inputs):
    import concourse.bacc as bacc
    from concourse.bass_utils import run_bass_kernel_spmd

    nc = bacc.Bacc("TRN2", target_bir_lowering=False, num_devices=1)
    arrays = {name: np.ascontiguousarray(inputs[key]) for name, key in NAMES.items()}
    arrays.update(spline_constants())
    arrays.update(index_constants())
    io = {name: nc.dram_tensor(f"in_{name}", a.shape, mybir.dt.from_np(a.dtype), kind="ExternalInput").ap()
          for name, a in arrays.items()}
    io["out"] = nc.dram_tensor("out", [TOKP, D], F32, kind="ExternalOutput").ap()
    build(nc, io)
    result = run_bass_kernel_spmd(nc, [{f"in_{name}": a for name, a in arrays.items()}], core_ids=[0])
    return result.results[0]["out"][0:TOK].reshape(BATCH, SEQ, D)
```

```python
from contextlib import ExitStack

import numpy as np

import concourse.bass as bass
from concourse import mybir

F32 = mybir.dt.float32
F32R = mybir.dt.float32r
I32 = mybir.dt.int32
U32 = mybir.dt.uint32
U8 = mybir.dt.uint8
ACT = mybir.ActivationFunctionType
ALU = mybir.AluOpType
AX = mybir.AxisListType

P = 128
BATCH, SEQ, D = 64, 64, 512
TOK = BATCH * SEQ
DK = D // P
INTER = 2048
IC = INTER // P
NCP = 8134
CPP = NCP + 10
PAD = 2
TILE = 256
NT = TOK // TILE
SUB = TILE // P
INNER = 4
RING, LAG = 8, 3
GU_BANKS = 4
LTILE = 512
LNT = TOK // LTILE
LSUB = LTILE // P
NSUB = TOK // P

GROUPS = 8
GROUP = INTER // GROUPS
PIECES, POW = 5, 4
KNOTS, KNOT_W, KNOT_GAP, KNOT_STEP = 4, 18, 129, 16
NPOLY = PIECES * POW
NRAW = KNOTS * KNOT_W
NF = NPOLY + NRAW
XW = 520
HALF = 64.0

NA, RANK = 8, 16
WIDE = D + 8
HALFW = WIDE // 2
NE, FD = 8, 352
FC = 3
FP = FC * P
REM = FD - 2 * P
BLOCKS = 2 * TOK // P + NE - 1
COLS = BLOCKS + 2
MAX_BLOCKS = TOK // P
REGION = MAX_BLOCKS + 1
CHUNKS = -(-NE * REGION // P)
REST = NE * REGION - (CHUNKS - 1) * P
PLACES = LSUB * WIDE + 6 * LSUB * NE
TOKP = TOK + P
SLOTS = 3
LOADS = 64

GH, GL, UH, UL = (i * DK * FD for i in range(4))
DH_, DL_ = 4 * DK * FD, 4 * DK * FD + FC * D
EW = 4 * DK * FD + 2 * FC * D


def spline_constants():
    n = D * INTER
    t = np.linspace(0.0, NCP - 1.0, n, dtype=np.float64)
    iv = np.clip(np.floor(t).astype(np.int64), 0, NCP - 2)
    step = (NCP - 1.0) / (n - 1.0)
    base = 0.5 * np.array([[0, 2, 0, 0], [-1, 0, 1, 0], [2, -5, 4, -1], [-1, 3, -3, 1]], np.float64)

    def cubic(c, s):
        c = np.asarray(c)[..., None]
        return np.stack([base[0] + c * base[1] + c**2 * base[2] + c**3 * base[3],
                         s * (base[1] + 2 * c * base[2] + 3 * c**2 * base[3]),
                         s * s * (base[2] + 3 * c * base[3]),
                         s**3 * base[3] * np.ones_like(c)], -2)

    rt, ri = t.reshape(INTER, D), iv.reshape(INTER, D)
    j0 = ri[:, 0]
    order = np.argsort(j0 - rt[:, 0], kind="stable")
    mom = np.zeros((D, GROUPS, PIECES, POW))
    tabp = np.zeros((INTER, PIECES, POW, 4))
    tabr = np.zeros((INTER, KNOTS, KNOT_W, 5))
    for g in range(GROUPS):
        at = np.arange(g * GROUP, (g + 1) * GROUP)
        r = order[at]
        lo = [KNOT_STEP * g + KNOT_GAP * k for k in range(KNOTS)]
        for p in range(PIECES):
            a, b = ([0] + [x + KNOT_W for x in lo])[p], min((lo + [D])[p], D)
            if b <= a:
                continue
            c = (a + b - 1) / 2
            assert (ri[r, a:b] == (j0[r] + p)[:, None]).all()
            mom[a:b, g, p] = ((np.arange(a, b) - c) / HALF)[:, None] ** np.arange(POW)
            tabp[at, p] = cubic((r * D + c) * step - (j0[r] + p), HALF * step)
        for k in range(KNOTS):
            for w in range(KNOT_W):
                h = lo[k] + w
                if h >= D:
                    continue
                rel = ri[r, h] - j0[r] - k
                assert ((rel == 0) | (rel == 1)).all()
                weight = cubic(rt[r, h] - ri[r, h], 1.0)[:, 0]
                for q in (0, 1):
                    tabr[at[rel == q], k, w, q:q + 4] = weight[rel == q]

    nb = n // P
    b = np.arange(nb)
    jb = iv[b * P]
    jq = np.repeat(jb[::4], 4)
    c4 = b % 4
    tabd = np.zeros((nb, 2, POW, 5))
    for side in range(2):
        weight = cubic((b * P + (P - 1) / 2) * step - jb - side, HALF * step)
        for q in (0, 1):
            s = (jb - jq + 1 - c4) == q
            tabd[s, side, :, q:q + 4] = weight[s]
    assert np.isin(jb - jq + 1 - c4, (0, 1)).all()
    past = (iv.reshape(nb, P) > jb[:, None])
    assert (iv.reshape(nb, P) - jb[:, None] <= 1).all()
    v = ((np.arange(P) - (P - 1) / 2) / HALF)[None] ** np.arange(POW)[:, None]
    vh = np.rint(v * 2**11) / 2**11
    vl = v - vh
    pw = np.zeros((4, 2, 4, POW, 8, P))
    for c in range(4):
        for side in range(2):
            pw[c, side, :, :, 2 * c + side] = np.stack([vh, vl, vh, vl])

    f = lambda a: np.ascontiguousarray(a, dtype=np.float32)
    ints = lambda a: np.ascontiguousarray(a, dtype=np.int32)
    return {
        "c_order": ints(order.reshape(IC, P).T),
        "c_win_gu": ints((j0[order] + PAD - 1).reshape(IC, P).T),
        "c_win_d": ints((jb[::4] + PAD - 2).reshape(16, P).T),
        "c_mom": f(mom.reshape(DK, P, GROUPS * NPOLY).transpose(1, 0, 2)),
        "c_tabp": f(tabp.reshape(IC, P, PIECES, 16).transpose(1, 2, 0, 3).reshape(P, -1)),
        "c_tabr": f(tabr.reshape(IC, P, KNOTS, KNOT_W * 5).transpose(1, 2, 0, 3).reshape(P, -1)),
        "c_tabd": f(tabd.reshape(16, P, 4, 2, 20).transpose(1, 2, 3, 0, 4).reshape(P, -1)),
        "c_pw": f(pw.reshape(P, 8 * P)),
        "c_before": f((P - past.sum(-1)).reshape(16, P, 4).transpose(2, 0, 1).reshape(1, -1)),
    }


def index_constants():
    p = np.arange(P)
    tok = (np.arange(NSUB)[None] * P + p[:, None]).astype(np.float32)
    small = np.zeros((P, 128), np.float32)
    small[:, 0] = p % 64
    small[:, 1] = p // RANK
    for c in range(3):
        small[:, 2 + c] = p + c * P
    small[:, 5] = p + 1
    small[:, 8:16] = (p[:, None] // RANK == np.arange(NA))
    small[:, 16:24] = np.arange(NE)
    small[:, 24:24 + COLS] = np.arange(COLS)
    return {"c_tok": tok, "c_small": small,
            "c_no_entry": np.stack([np.tile(TOK + p, NE * REGION).reshape(P, -1), np.zeros((P, NE * REGION))], -1).astype(np.float32)}


def view(ap, offset, dims):
    return bass.AP(tensor=ap.tensor, offset=ap.offset + offset, ap=[list(ap.ap[0])] + [list(d) for d in dims])


def build(nc, io):
    kc = {k: v for k, v in io.items() if k.startswith("c_")}
    dram = lambda n, s, d=F32: nc.dram_tensor(n, s, d, kind="Internal").ap()
    cp_padded = [dram(f"{m}_cp_padded", [CPP, 1]) for m in ("gate", "up", "down")]
    down_natural = dram("down_natural", [INTER, D])
    gate_up_dram = dram("gate_up_dram", [2 * NE, P, 2 * DK * FD])
    expert_down_dram = dram("expert_down_dram", [2 * NE, P, 2 * FC * D // 2])
    z_dram = dram("z_dram", [TOKP, D])
    table_dram = dram("table_dram", [NE * REGION * P, 2])
    out = io["out"]
    x_flat = io["x"].rearrange("b c h -> (b c) h")
    layer_tiles = out[0:TOK, :].rearrange("(t s p) h -> t p s h", s=LSUB, p=P)
    x_tiles = x_flat.rearrange("(t s p) h -> t p s h", s=SUB, p=P)
    out_tiles = out[0:TOK, :].rearrange("(t s p) h -> t p s h", s=SUB, p=P)
    z_tiles = z_dram[0:TOK, :].rearrange("(t s p) h -> t p s h", s=LSUB, p=P)
    cond_rows = io["cond_w"].rearrange("n c d -> (n c) d")

    top = ExitStack()
    with top:
        def alloc(stack):
            def sb(name, shape, dt=F32):
                return stack.enter_context(nc.sbuf_tensor(name, shape, dt))
            return sb

        def sem(name):
            return top.enter_context(nc.semaphore(name))

        psum = [top.enter_context(nc.psum_tensor(f"bank{i}", [P, 512], F32)) for i in range(8)]
        sb = alloc(top)
        ident = sb("ident", [P, P])
        small = sb("small", [P, 128])
        tok_ids = sb("tok_ids", [P, NSUB])
        lower, ones = sb("lower", [P, P]), sb("ones", [P, P])
        chosen = sb("chosen", [P, LSUB + 1, NE])
        idle = sb("idle", [P, 64])
        staging = sb("staging", [P, DK * D + 3 * D])
        x_both = sb("x_both", [P, 2, SUB, XW])
        x_in, x_res = x_both[:, 0], x_both[:, 1, :, 0:D]
        raw_w = staging[:, 0:DK * D].rearrange("p (c d) -> p c d", c=DK)
        raw_a, raw_b, raw_r = (staging[:, (DK + i) * D:(DK + i + 1) * D] for i in range(3))
        x_loaded, x1_stored, split_stored = sem("x_loaded"), sem("x1_stored"), sem("split_stored")
        w_loaded, raw_loaded = sem("w_loaded"), sem("lw_raw_loaded")

        def load_x(sp, t):
            sp.dma_start(x_in[:, :, 0:D], x_tiles[bass.ds(t, 1)].rearrange("a p s h -> p (a s) h")).then_inc(x_loaded, 16)

        def load_layer_weights(sp):
            sp.dma_start(raw_w, io["W"].rearrange("(c p) d -> p c d", p=P)).then_inc(w_loaded, 16)
            sp.dma_start(raw_a, io["A"].rearrange("n r d -> (n r) d")).then_inc(raw_loaded, 16)
            sp.dma_start(raw_r[0:NE, :], io["router_w"]).then_inc(raw_loaded, 16)
            for c in range(DK):
                sp.dma_start(raw_b[:, c * P:(c + 1) * P].rearrange("p (n r) -> p n r", n=NA),
                             io["Bm"][:, c * P:(c + 1) * P, :].rearrange("n p r -> p n r")).then_inc(raw_loaded, 16)

        main = ExitStack()
        sbm = alloc(main)
        gu_hi = sbm("gu_hi", [NF, 2, INTER], F32R)
        gu_lo = sbm("gu_lo", [NF, 2, INTER], F32R)
        mom = sbm("mom", [P, DK, GROUPS * NPOLY])
        cond_idx = sbm("cond_idx", [P, NSUB + 2 * SUB], I32)
        down_hi = sbm("down_hi", [P, IC, D], F32R)
        down_lo = sbm("down_lo", [P, IC, D], F32R)
        prepare(nc, io, kc, alloc, sem, psum, ident, small, lower, ones, tok_ids, mom, cond_idx, gu_hi, gu_lo, down_hi, down_lo,
                cp_padded, down_natural, table_dram, z_dram, out, staging, x_in, load_x)
        first_ffn(nc, io, alloc, sem, psum, ident, small, idle, x_tiles, out_tiles, cond_rows, cond_idx, mom,
                  x_in, x_res, x_loaded, x1_stored, split_stored, load_x, load_layer_weights, gu_hi, gu_lo, down_hi, down_lo, gate_up_dram, expert_down_dram)
        main.close()
        slots = sb("slots", [P, SLOTS, EW], F32R)
        weights_loaded = sem("weights_loaded")

        def load_expert(sp, e, wait):
            slot = slots[:, e % SLOTS, :].bitcast(F32)
            down = slot[:, DH_:].rearrange("p (l f a d) -> p l f a d", l=2, f=FC, a=2)
            sp.dma_start(slot[:, GH:UH], gate_up_dram[e]).then_inc(weights_loaded, 16)
            if wait:
                sp.wait_ge(weights_loaded, LOADS * e + 16)
            sp.dma_start(slot[:, UH:DH_], gate_up_dram[NE + e]).then_inc(weights_loaded, 16)
            if wait:
                sp.wait_ge(weights_loaded, LOADS * e + 32)
            for a in range(2):
                sp.dma_start(down[:, :, :, a, :], expert_down_dram[2 * e + a].rearrange("p (l f d) -> p l f d", l=2, f=FC)).then_inc(weights_loaded, 16)
            sp.wait_ge(weights_loaded, LOADS * (e + 1))

        ctl = view(staging[:, :], PLACES, [[1, 2 * COLS + NE]]).bitcast(I32)
        chosen_at = view(staging[:, :], PLACES + 2 * COLS + NE, [[COLS, CHUNKS], [1, COLS]])
        ctl_ready = sem("ctl_ready")

        layer = ExitStack()
        sbl = alloc(layer)
        w_hi = sbl("w_hi", [P, DK + 1, WIDE], F32R)
        w_lo = sbl("w_lo", [P, DK + 1, WIDE], F32R)
        a_hi = sbl("a_hi", [P, DK, P], F32R)
        a_lo = sbl("a_lo", [P, DK, P], F32R)
        adapter_scale = sbl("adapter_scale", [P, BATCH])
        x1 = [sbl(f"x1_{b}", [P, LSUB, D]) for b in range(2)]
        x1_loaded = [sem(f"x1_loaded{b}") for b in range(2)]
        layer_weights(nc, io, alloc, sem, psum, ident, small, w_hi, w_lo, a_hi, a_lo, adapter_scale, layer_tiles, x1, x1_loaded,
                      raw_w, raw_a, raw_b, raw_r, w_loaded, raw_loaded, x1_stored, split_stored)
        adapted_layer(nc, alloc, sem, psum, ident, small, idle, lower, ones, tok_ids, layer_tiles, z_tiles, x1, x1_loaded,
                      w_hi, w_lo, a_hi, a_lo, adapter_scale, chosen, table_dram, load_expert, staging, x_both, ctl, chosen_at, ctl_ready)
        layer.close()
        experts(nc, alloc, sem, psum, ident, small, idle, slots, weights_loaded, load_expert, table_dram, z_dram, out,
                ctl, chosen_at, ctl_ready)


def prepare(nc, io, kc, alloc, sem, psum, ident, small, lower, ones, tok_ids, mom, cond_idx, gu_hi, gu_lo, down_hi, down_lo,
            cp_padded, down_natural, table_dram, z_dram, out, staging, x_in, load_x):
    with ExitStack() as scope:
        sb = alloc(scope)
        idx_gu, idx_d, order_idx = sb("idx_gu", [P, IC], I32), sb("idx_d", [P, 16], I32), sb("order_idx", [P, IC], I32)
        tabp = sb("tabp", [P, PIECES, IC, POW, 4])
        tabr = [sb(f"tabr{b}", [P, IC, KNOT_W, 5]) for b in range(2)]
        prod = sb("prod", [P, IC, KNOT_W, 5])
        rows_gu = sb("rows_gu", [P, 2, IC, NF])
        parts = view(staging[:, :], 0, [[8 * 4 * POW, 16], [4 * POW, 8], [POW, 4], [1, POW]])
        coef = view(staging[:, :], DK * D, [[8 * POW, 16], [POW, 8], [1, POW]])
        zeros = view(staging[:, :], (DK + 1) * D, [[1, D]])
        win_gu = view(staging[:, :], (DK + 2) * D, [[8 * IC, 2], [8, IC], [1, 8]])
        win_d = view(staging[:, :], (DK + 2) * D + 2 * 8 * IC, [[9, 16], [1, 9]])
        powers = view(x_in[:, :, :], 0, [[P, 8], [1, P]])
        powers_r = view(down_lo[:, :, :], 0, [[P, 8], [1, P]])
        past = sb("past", [P, 4, 4, 4 * P], U8)
        coef_t = sb("coef_t", [P, 4, 4 * P], F32R)
        ones_r = coef_t[0:1, 0, 0:P]
        dense = sb("dense", [P, IC, D])
        cond_i, cond_f, cond_rows_f = sb("cond_i", [P, BATCH], I32), sb("cond_f", [P, BATCH]), sb("cond_rows_f", [P, NSUB])
        no_entry = sb("no_entry", [P, NE * REGION, 2])
        PIECE_D = 16 * POW * 5

        ident_ready, masks_set, ones_ready = (sem(n) for n in ("ident_ready", "masks_set", "ones_ready"))
        before_rounded = sem("before_rounded")
        idx_d_loaded, idx_loaded, consts_loaded = sem("idx_d_loaded"), sem("idx_loaded"), sem("consts_loaded")
        cp_stored = [sem(f"cp_stored{m}") for m in range(3)]
        win_d_loaded, win_loaded = [sem(f"win_d_loaded{h}") for h in range(2)], [sem(f"win_loaded{m}") for m in range(2)]
        no_entry_loaded, padding_stored = sem("no_entry_loaded"), sem("padding_stored")
        tabd_loaded, powers_loaded, before_loaded, tabp_loaded, mom_loaded = (sem(n) for n in (
            "tabd_loaded", "powers_loaded", "before_loaded", "tabp_loaded", "mom_loaded"))
        tabr_loaded, tabr_used = [sem(f"tabr_loaded{b}") for b in range(2)], [sem(f"tabr_used{b}") for b in range(2)]
        step, past_filled, past_set, powers_done, parts_done, rows_done = (sem(n) for n in (
            "prep_step", "past_filled", "past_set", "powers_done", "parts_done", "rows_done"))
        T_USES, GU_USES = 4, 2 * IC // 4
        POOL_LOW = 11
        t_filled, t_drained = [sem(f"t_filled{i}") for i in range(2)], [sem(f"t_drained{i}") for i in range(2)]
        filled, before, drained = ([sem(f"piece_{n}{i}") for i in range(3)] for n in ("filled", "before", "drained"))
        stored, gathered, down_high, down_done, gu_high = (sem(n) for n in ("dense_stored", "dense_gathered", "down_high", "down_done", "gu_high"))
        gu_filled = sem("gu_filled")

        def place(n):
            g, c = n // 4, n % 4
            return view(dense[:, :, :], c * D + g * P, [[32, 4], [1, 32], [4 * D, 4]])

        def gu_target(u):
            m, q = u // 4, u % 4
            return gu_hi[:, m, q * D:(q + 1) * D], gu_lo[:, m, q * D:(q + 1) * D]

        with nc.Block() as block:
            @block.sync
            def _(sp):
                sp.dma_start(view(rows_gu[:, :, :, :], 0, [[1, 8 * PIECE_D]]), kc["c_tabd"]).then_inc(tabd_loaded, 16)
                sp.dma_start(powers[:, :, :].rearrange("p a b -> p (a b)"), kc["c_pw"]).then_inc(powers_loaded, 16)
                sp.dma_start(dense[0:1, :, :].rearrange("p a b -> p (a b)"), kc["c_before"]).then_inc(before_loaded, 16)
                for m in range(3):
                    sp.wait_ge(cp_stored[m], 16 * (PAD + 3))
                sp.dma_start(tabp[:, :, :, :, :].rearrange("p a b c d -> p (a b c d)"), kc["c_tabp"]).then_inc(tabp_loaded, 16)
                width = IC * KNOT_W * 5
                for k in range(KNOTS):
                    if k >= 2:
                        sp.wait_ge(tabr_used[k % 2], 1)
                    sp.dma_start(tabr[k % 2][:, :, :, :].rearrange("p a b c -> p (a b c)"), kc["c_tabr"][:, k * width:(k + 1) * width]).then_inc(tabr_loaded[k % 2], 16)
                    if k == 1:
                        sp.dma_start(mom[:, :, :].rearrange("p k n -> p (k n)"), kc["c_mom"].rearrange("p k n -> p (k n)")).then_inc(mom_loaded, 16)
                        for g in range(4):
                            for i in range(3):
                                sp.wait_ge(drained[i], len(range(i, 4 * g + 4, 3)) + 1)
                            cols = slice(g * P, (g + 1) * P)
                            sp.dma_start(down_natural.rearrange("(j s) h -> s j h", s=P)[:, :, cols], dense[:, :, cols]).then_inc(stored, 16)
                sp.wait_ge(powers_done, 1)
                load_x(sp, 0)
                sp.wait_ge(stored, 64)
                sp.wait_ge(mom_loaded, 16)

            @block.gpsimd
            def _(pool):
                nc.gpsimd.memset(ident[:, :], 0.0)
                nc.gpsimd.memset(zeros, 0.0)
                nc.gpsimd.memset(ones[:, :], 1.0)
                nc.gpsimd.memset(lower[:, :], 1.0).then_inc(masks_set, 1)
                pool.wait_ge(masks_set, 1)
                nc.gpsimd.affine_select(out=ident[:, :], in_=ident[:, :], compare_op=ALU.not_equal, fill=1.0,
                                        base=0, pattern=[[-1, P]], channel_multiplier=1).then_inc(ident_ready, 1)
                nc.gpsimd.affine_select(out=lower[:, :], in_=lower[:, :], compare_op=ALU.is_gt, fill=0.0,
                                        base=0, pattern=[[1, P]], channel_multiplier=-1)
                pool.wait_ge(idx_d_loaded, 16)
                pool.wait_ge(cp_stored[2], 16 * (PAD + 3))
                for q in range(16):
                    nc.gpsimd.indirect_dma_start(win_d[:, q, :], None, cp_padded[2], bass.IndirectOffsetOnAxis(ap=idx_d[:, q:q + 1], axis=0)).then_inc(win_d_loaded[q // 8], 16)
                pool.wait_ge(idx_loaded, 32)
                for m in range(2):
                    pool.wait_ge(cp_stored[m], 16 * (PAD + 3))
                    for q in range(IC):
                        nc.gpsimd.indirect_dma_start(win_gu[:, m, q, :], None, cp_padded[m], bass.IndirectOffsetOnAxis(ap=idx_gu[:, q:q + 1], axis=0)).then_inc(win_loaded[m], 16)
                pool.wait_ge(stored, 64)
                for q in range(IC):
                    nc.gpsimd.indirect_dma_start(dense[:, q, :], None, down_natural,
                                                 bass.IndirectOffsetOnAxis(ap=order_idx[:, q:q + 1], axis=0)).then_inc(gathered, 16)
                for q in range(POOL_LOW):
                    pool.wait_ge(down_high, q + 1)
                    ins = nc.gpsimd.tensor_tensor(down_lo[:, q, :], dense[:, q, :], down_hi[:, q, :].bitcast(F32), ALU.subtract)
                ins.then_inc(down_done, 1)
                pool.wait_ge(down_done, 1)

            @block.tensor
            def _(pe):
                pe.wait_ge(ident_ready, 1)
                pe.wait_ge(ones_ready, 1)
                for n in range(16):
                    if n % 4 == 0:
                        pe.wait_ge(before_rounded, n // 4 + 1)
                    if n >= 4:
                        pe.wait_ge(past_set, n - 3)
                    nc.tensor.matmul(psum[n % 4][:, :], ones_r, down_hi[0:1, n, :], start=True, stop=True).then_inc(past_filled, 1)
                for g in range(T_USES):
                    if g % 2 == 0:
                        pe.wait_ge(parts_done, g // 2 + 1)
                    pe.wait_ge(t_drained[g % 2], g // 2 + 1)
                    for q in range(4):
                        ins = nc.tensor.transpose(psum[6 + g % 2][:, q * P:(q + 1) * P],
                                                  parts[:, 4 * g + q, :, :, :].rearrange("p a b c -> p (a b c)"), ident[:, :])
                    ins.then_inc(t_filled[g % 2], 1)
                pe.wait_ge(powers_done, 1)
                pe.wait_ge(past_set, 16)
                for n in range(16):
                    g, c, i = n // 4, n % 4, n % 3
                    pe.wait_ge(t_drained[g % 2], g // 2 + 2)
                    pe.wait_ge(drained[i], n // 3 + 1)
                    nc.tensor.matmul(psum[2 * i][:, :], powers_r[:, 2 * c, :], coef_t[:, g, :], start=True, stop=True)
                    nc.tensor.matmul(psum[2 * i + 1][:, :], powers_r[:, 2 * c + 1, :], coef_t[:, g, :],
                                     start=True, stop=True).then_inc(filled[i], 1)
                for u in range(GU_USES):
                    m, q4 = u // 4, u % 4
                    if q4 == 0:
                        pe.wait_ge(rows_done, m + 1)
                    if u < 6:
                        pe.wait_ge(drained[u // 2], len(range(u // 2, 16, 3)) + 1)
                    for q in range(4):
                        ins = nc.tensor.transpose(psum[u][0:NF, q * P:(q + 1) * P], rows_gu[:, m, 4 * q4 + q, :], ident[:, :])
                    ins.then_inc(gu_filled, 1)

            @block.scalar
            def _(act):
                act.dma_start(idx_d[:, :], kc["c_win_d"]).then_inc(idx_d_loaded, 16)

                def pad(m, name):
                    cp, to = io[name].rearrange("(a n) -> a n", a=1), cp_padded[m].rearrange("n a -> a n")
                    act.dma_start(to[:, PAD:PAD + NCP], cp).then_inc(cp_stored[m], 16)
                    for i in range(PAD):
                        act.dma_start(to[:, i:i + 1], cp[:, 0:1]).then_inc(cp_stored[m], 16)
                    act.dma_start(to[:, PAD + NCP:PAD + NCP + 1], cp[:, NCP - 1:NCP]).then_inc(cp_stored[m], 16)
                    act.dma_start(to[:, PAD + NCP + 1:CPP], cp[:, 0:CPP - PAD - NCP - 1]).then_inc(cp_stored[m], 16)

                pad(2, "down_cp")
                act.dma_start(idx_gu[:, :], kc["c_win_gu"]).then_inc(idx_loaded, 16)
                act.dma_start(order_idx[:, :], kc["c_order"]).then_inc(idx_loaded, 16)
                pad(0, "gate_cp")
                pad(1, "up_cp")
                act.dma_start(small[:, :], kc["c_small"]).then_inc(consts_loaded, 16)
                act.dma_start(tok_ids[:, :], kc["c_tok"]).then_inc(consts_loaded, 16)
                act.dma_start(cond_i[:, :], io["cond"].rearrange("(a n) -> a n", a=1).to_broadcast([P, BATCH])).then_inc(consts_loaded, 16)
                act.dma_start(no_entry[:, :, :], kc["c_no_entry"]).then_inc(no_entry_loaded, 16)
                act.wait_ge(masks_set, 1)
                act.dma_start(z_dram[TOK:TOKP, :], zeros[:, :]).then_inc(padding_stored, 16)
                act.dma_start(out[TOK:TOKP, :], zeros[:, :]).then_inc(padding_stored, 16)
                act.wait_ge(masks_set, 1)
                nc.scalar.activation(ones_r, ones[0:1, :], ACT.Copy).then_inc(ones_ready, 1)
                act.wait_ge(powers_loaded, 16)
                nc.scalar.activation(powers_r[:, :, :], powers[:, :, :], ACT.Copy).then_inc(powers_done, 1)
                act.wait_ge(consts_loaded, 48)
                for n in range(16):
                    act.wait_ge(past_filled, n + 1)
                    nc.scalar.activation(past[:, n // 4, n % 4, :], psum[n % 4][:, :], ACT.Relu, bias=small[:, 5:6], scale=-1.0).then_inc(past_set, 1)
                act.wait_ge(no_entry_loaded, 16)
                act.dma_start(table_dram.rearrange("(p c) w -> p (c w)", p=P),
                              no_entry[:, :, :].rearrange("p c w -> p (c w)")).then_inc(padding_stored, 16)
                for g in range(T_USES):
                    act.wait_ge(t_filled[g % 2], g // 2 + 1)
                    nc.scalar.activation(coef_t[:, g, :], psum[6 + g % 2][:, :], ACT.Copy).then_inc(t_drained[g % 2], 1)
                for n in range(16):
                    i = n % 3
                    act.wait_ge(filled[i], n // 3 + 1)
                    nc.scalar.activation(place(n), psum[2 * i][:, :].rearrange("p (a b c) -> p a b c", a=4, c=4),
                                         ACT.Copy).then_inc(before[i], 1)

                def gu_highs(m):
                    for u in range(4 * m, 4 * m + 4):
                        act.wait_ge(gu_filled, u + 1)
                        nc.scalar.activation(gu_target(u)[0], psum[u][0:NF, :], ACT.Copy).then_inc(gu_high, 1)

                act.wait_ge(gathered, 16 * IC)
                for q in range(IC):
                    if q == POOL_LOW:
                        gu_highs(0)
                    nc.scalar.activation(down_hi[:, q, :], dense[:, q, :], ACT.Copy).then_inc(down_high, 1)
                gu_highs(1)
                act.wait_ge(padding_stored, 48)

            @block.vector
            def _(dve):
                for i in range(2):
                    nc.vector.nop().then_inc(t_drained[i], 1)
                for i in range(3):
                    nc.vector.nop().then_inc(drained[i], 1)
                count = [0]

                def link(ins):
                    count[0] += 1
                    ins.then_inc(step, 1)
                    dve.wait_ge(step, count[0])

                dve.wait_ge(before_loaded, 16)
                for n in range(0, 16, 4):
                    nc.vector.tensor_copy(down_hi[0:1, n:n + 4, :], dense[0:1, n:n + 4, :]).then_inc(before_rounded, 1)
                dve.wait_ge(consts_loaded, 48)
                nc.vector.memset(cond_idx[:, NSUB:], 0)
                link(nc.vector.tensor_copy(cond_f[:, :], cond_i[:, :]))
                for half in range(2):
                    rows = slice(64 * half, 64 * half + 64)
                    last = nc.vector.tensor_scalar(cond_rows_f[rows, :], cond_f[rows, half::2], 64.0, small[rows, 0:1], ALU.mult, ALU.add)
                link(last)
                link(nc.vector.tensor_copy(cond_idx[:, 0:NSUB], cond_rows_f[:, :]))
                dve.wait_ge(tabd_loaded, 16)
                for h in range(2):
                    half, first = slice(8 * h, 8 * h + 8), 8 * h * POW * 5
                    dve.wait_ge(win_d_loaded[h], 8 * 16)
                    for c in range(4):
                        for side in range(2):
                            pr = view(prod[:, :, :, :], side * PIECE_D, [[POW * 5, 8], [5, POW], [1, 5]])
                            tabd = view(rows_gu[:, :, :, :], (2 * c + side) * PIECE_D + first, [[POW * 5, 8], [5, POW], [1, 5]])
                            link(nc.vector.tensor_tensor(pr, tabd, view(win_d, 9 * 8 * h + c + side, [[9, 8], [0, POW], [1, 5]]), ALU.mult))
                            last = nc.vector.tensor_reduce(coef[:, half, 2 * c + side, :], pr, AX.X, ALU.add)
                    link(last)
                    flat = coef[:, half, :, :].rearrange("p q c m -> p (q c) m")
                    to = parts[:, half, :, :, :].rearrange("p q c r m -> p (q c) r m")
                    for r in range(2):
                        link(nc.vector.tensor_copy(to[:, :, r, :].bitcast(F32R), flat))
                    nc.vector.tensor_tensor(to[:, :, 2, :].bitcast(F32R), flat, to[:, :, 0, :], ALU.subtract)
                    nc.vector.tensor_tensor(to[:, :, 3, :].bitcast(F32R), flat, to[:, :, 0, :], ALU.subtract).then_inc(parts_done, 1)
                for n in range(16):
                    i = n % 3
                    dve.wait_ge(before[i], n // 3 + 1)
                    nc.vector.copy_predicated(place(n), past[:, n % 4, n // 4, :].rearrange("p (a b c) -> p a b c", a=4, c=4),
                                              psum[2 * i + 1][:, :].rearrange("p (a b c) -> p a b c", a=4, c=4)).then_inc(drained[i], 1)
                def pieces(m):
                    dve.wait_ge(win_loaded[m], 16 * IC)
                    for p in range(PIECES):
                        pr = view(prod[:, :, :, :], p % 2 * PIECE_D, [[POW * 4, IC], [4, POW], [1, 4]])
                        link(nc.vector.tensor_tensor(pr, tabp[:, p], view(win_gu[:, m], p, [[8, IC], [0, POW], [1, 4]]), ALU.mult))
                        last = nc.vector.tensor_reduce(rows_gu[:, m, :, p * POW:(p + 1) * POW], pr, AX.X, ALU.add)
                    link(last)

                def knot(k, m):
                    dve.wait_ge(tabr_loaded[k % 2], 16 * (k // 2 + 1))
                    pr = prod[:, :, :, :]
                    link(nc.vector.tensor_tensor(pr, tabr[k % 2][:, :, :, :], view(win_gu[:, m], k, [[8, IC], [0, KNOT_W], [1, 5]]), ALU.mult))
                    if m == 1:
                        nc.vector.nop().then_inc(tabr_used[k % 2], 1)
                    link(nc.vector.tensor_reduce(rows_gu[:, m, :, NPOLY + k * KNOT_W:NPOLY + (k + 1) * KNOT_W], pr, AX.X, ALU.add))

                def gu_lows(m):
                    for u in range(4 * m, 4 * m + 4):
                        hi, lo = gu_target(u)
                        dve.wait_ge(gu_high, u + 1)
                        nc.vector.tensor_tensor(lo, psum[u][0:NF, :], hi.bitcast(F32), ALU.subtract)

                dve.wait_ge(tabp_loaded, 16)
                pieces(0)
                knot(0, 0)
                knot(1, 0)
                pieces(1)
                knot(0, 1)
                knot(1, 1)
                knot(2, 0)
                knot(3, 0)
                nc.vector.nop().then_inc(rows_done, 1)
                knot(2, 1)
                knot(3, 1)
                nc.vector.nop().then_inc(rows_done, 1)
                gu_lows(0)
                for q in range(POOL_LOW, IC):
                    dve.wait_ge(down_high, q + 1)
                    nc.vector.tensor_tensor(down_lo[:, q, :], dense[:, q, :], down_hi[:, q, :].bitcast(F32), ALU.subtract)
                gu_lows(1)


def layer_weights(nc, io, alloc, sem, psum, ident, small, w_hi, w_lo, a_hi, a_lo, adapter_scale, layer_tiles, x1, x1_loaded,
                  raw_w, raw_a, raw_b, raw_r, w_loaded, raw_loaded, x1_stored, split_stored):
    with ExitStack() as scope:
        sb = alloc(scope)
        r_t = sb("r_t", [P, DK, NE])
        adapt_i, adapt_f = sb("adapt_i", [P, BATCH], I32), sb("adapt_f", [P, BATCH])
        scale_all, scale_own = sb("scale_all", [P, NA]), sb("scale_own", [P, 1])
        scale_pick = sb("scale_pick", [P, NA])
        ints_loaded = sem("ints_loaded")
        step = sem("lw_step")
        NB = 4
        filled = [sem(f"lw_filled{i}") for i in range(NB)]
        drained = [sem(f"lw_drained{i}") for i in range(NB)]
        high_done, rt_done = sem("lw_high_done"), sem("rt_done")
        W_USE, A_USE, RT_USE, B_USE, R_USE = 0, DK, DK + 1, DK + 2, DK + 3
        USES = DK + 4

        def target(u):
            if u < A_USE:
                return w_hi[:, u - W_USE, 0:D], w_lo[:, u - W_USE, 0:D], D
            if u == A_USE:
                return a_hi[:, :, :].rearrange("p k r -> p (k r)"), a_lo[:, :, :].rearrange("p k r -> p (k r)"), D
            if u == B_USE:
                return w_hi[:, DK, 0:D], w_lo[:, DK, 0:D], D
            return w_hi[:, :, D:], w_lo[:, :, D:], (DK + 1) * NE

        def filled_part(u, w):
            bank = psum[u % NB][:, 0:w]
            return bank.rearrange("p (k e) -> p k e", e=NE) if u == R_USE else bank

        with nc.Block() as block:
            @block.sync
            def _(sp):
                sp.wait_ge(x1_stored, 16 * NT)
                sp.dma_start(x1[0][:, :, :], layer_tiles[0]).then_inc(x1_loaded[0], 16)
                sp.wait_ge(split_stored, 32 * NT)

            @block.tensor
            def _(pe):
                pe.wait_ge(w_loaded, 16)
                for u in range(USES):
                    if u == A_USE:
                        pe.wait_ge(raw_loaded, 16 * (2 + DK))
                    i = u % NB
                    pe.wait_ge(drained[i], u // NB + 1)
                    bank = psum[i]
                    if u < A_USE:
                        for c in range(DK):
                            ins = nc.tensor.transpose(bank[:, c * P:(c + 1) * P], raw_w[:, c, (u - W_USE) * P:(u - W_USE + 1) * P], ident[:, :])
                    elif u == A_USE:
                        for c in range(DK):
                            ins = nc.tensor.transpose(bank[:, c * P:(c + 1) * P], raw_a[:, c * P:(c + 1) * P], ident[:, :])
                    elif u == RT_USE:
                        for c in range(DK):
                            ins = nc.tensor.transpose(bank[:, c * NE:(c + 1) * NE], raw_r[0:NE, c * P:(c + 1) * P], ident[0:NE, 0:NE])
                    elif u == B_USE:
                        for c in range(DK):
                            ins = nc.tensor.transpose(bank[:, c * P:(c + 1) * P],
                                                      raw_b[:, c * P:(c + 1) * P], ident[:, :])
                    else:
                        pe.wait_ge(rt_done, 1)
                        for k in range(DK):
                            for c in range(DK):
                                nc.tensor.matmul(bank[:, k * NE:(k + 1) * NE], raw_w[:, c, k * P:(k + 1) * P], r_t[:, c, :],
                                                 start=(c == 0), stop=(c == DK - 1))
                        for c in range(DK):
                            ins = nc.tensor.matmul(bank[:, DK * NE:(DK + 1) * NE], raw_b[:, c * P:(c + 1) * P],
                                                   r_t[:, c, :], start=(c == 0), stop=(c == DK - 1))
                    ins.then_inc(filled[i], 1)

            @block.scalar
            def _(act):
                act.dma_start(adapt_i[:, :], io["adapter"].rearrange("(a n) -> a n", a=1).to_broadcast([P, BATCH])).then_inc(ints_loaded, 16)
                act.dma_start(scale_all[:, :], io["scalings"].rearrange("(a n) -> a n", a=1).to_broadcast([P, NA])).then_inc(ints_loaded, 16)
                for u in range(USES):
                    act.wait_ge(filled[u % NB], u // NB + 1)
                    if u == RT_USE:
                        nc.scalar.activation(r_t[:, :, :].rearrange("p c e -> p (c e)"), psum[u % NB][:, 0:DK * NE], ACT.Copy).then_inc(rt_done, 1)
                        act.wait_ge(rt_done, 1)
                        nc.scalar.nop().then_inc(drained[u % NB], 1)
                        continue
                    hi, _, w = target(u)
                    nc.scalar.activation(hi, filled_part(u, w), ACT.Copy).then_inc(high_done, 1)

            @block.vector
            def _(dve):
                for i in range(NB):
                    nc.vector.nop().then_inc(drained[i], 1)
                count = [0]

                def link(ins):
                    count[0] += 1
                    ins.then_inc(step, 1)
                    dve.wait_ge(step, count[0])

                for n, u in enumerate(u for u in range(USES) if u != RT_USE):
                    if u == A_USE:
                        dve.wait_ge(ints_loaded, 32)
                        link(nc.vector.tensor_copy(adapt_f[:, :], adapt_i[:, :]))
                        link(nc.vector.tensor_tensor(scale_pick[:, :], scale_all[:, :], small[:, 8:8 + NA], ALU.mult))
                        link(nc.vector.tensor_reduce(scale_own[:, :], scale_pick[:, :], AX.X, ALU.add))
                        link(nc.vector.tensor_scalar(adapter_scale[:, :], adapt_f[:, :], small[:, 1:2], scale_own[:, 0:1], ALU.is_equal, ALU.mult))
                    hi, lo, w = target(u)
                    dve.wait_ge(high_done, n + 1)
                    nc.vector.tensor_tensor(lo, filled_part(u, w), hi.bitcast(F32), ALU.subtract).then_inc(drained[u % NB], 1)


def first_ffn(nc, io, alloc, sem, psum, ident, small, idle, x_tiles, out_tiles, cond_rows, cond_idx, mom,
              x_in, x_res, x_loaded, x1_stored, split_stored, load_x, load_layer_weights, gu_hi, gu_lo, down_hi, down_lo, gate_up_dram, expert_down_dram):
    with ExitStack() as scope:
        sb = alloc(scope)
        x_t = sb("x_t", [P, D])
        cond_now = sb("cond_now", [P, SUB], I32)
        cond_w = sb("cond_w", [P, SUB, SEQ])
        pair = sb("pair", [P, SUB, 2, P], F32R)
        pair_hi, pair_lo = pair[:, :, 0, :], pair[:, :, 1, :]
        feat_hi, feat_lo = sb("feat_hi", [P, SUB, GROUPS, NF], F32R), sb("feat_lo", [P, SUB, GROUPS, NF], F32R)
        f_sum = [sb(f"f_sum{b}", [NF, TILE]) for b in range(2)]
        f_hi, f_lo = sb("f_hi", [NF, GROUPS, TILE], F32R), sb("f_lo", [NF, GROUPS, TILE], F32R)
        silu_all = sb("silu_all", [P, GU_BANKS, TILE])
        silu = [silu_all[:, b, :] for b in range(GU_BANKS)]
        x_t_first = view(silu_all[:, :, :], 0, [[1, D]])
        inner = [sb(f"inner{b}", [P, TILE]) for b in range(INNER)]
        in_hi, in_lo = sb("in_hi", [P, RING, TILE], F32R), sb("in_lo", [P, RING, TILE], F32R)

        raw_gu, raw_down = sb("raw_gu", [P, FC, D]), sb("raw_down", [P, 2, FD])
        split_gu = sb("split_gu", [P, 2, DK, FD], F32R)
        split_down = sb("split_down", [P, 2, FC, D // 2], F32R)

        GU, OUT, FEAT, PREP = list(range(GU_BANKS)), [4, 5], 6, 7
        filled = [sem(f"filled{i}") for i in range(8)]
        drained = [sem(f"drained{i}") for i in range(8)]
        res_loaded = sem("res_loaded")
        pads_set, now_set = sem("pads_set"), sem("now_set")
        cond_loaded, pair_high, pair_done = sem("cond_loaded"), sem("pair_high"), sem("pair_done")
        mom_high, raw_high, f_high, f_done = (sem(n) for n in ("mom_high", "raw_high", "f_high", "f_done"))
        raw_loaded, split_high = sem("raw_loaded"), sem("split_high")
        silu_done, in_high, in_done = sem("silu_done"), sem("in_high"), sem("in_done")

        def first_tile(t):
            return isinstance(t, int) and t == 0

        PREPS, PARTS, FIRST_PREPS = 2 * SUB, DK + FC, 2
        FIRST_FEATS = GROUPS - GU_BANKS

        def feat_bank(t, g):
            return GU[g] if first_tile(t) and g < GU_BANKS else FEAT

        def use_feat(t, g):
            if first_tile(t):
                return 0 if g < GU_BANKS else FIRST_PREPS + g - GU_BANKS
            return FIRST_PREPS + FIRST_FEATS + GROUPS * (t - 1) + g

        def use_gu(t, c):
            return 1 + IC // GU_BANKS * t + c // GU_BANKS

        def prep_bank(t, s):
            return FEAT if first_tile(t) and s else PREP

        def x_turned(t, s):
            return x_t_first if first_tile(t) and s else x_t

        def use_prep(t, s, moments):
            return moments if first_tile(t) else (PREPS + PARTS) * (t - 1) + FIRST_PREPS + 2 * s + moments

        def use_part(t, i):
            at = FIRST_PREPS if isinstance(t, int) and t == NT - 1 else FIRST_PREPS + PREPS
            return (PREPS + PARTS) * t + at + i

        def wait_prepared(eng, t):
            for s in range(SUB) if first_tile(t) else [SUB - 1]:
                eng.wait_ge(drained[prep_bank(t, s)], use_prep(t, s, 1) + 2)

        PREP_AT = {2 * i: (i // 2, i % 2) for i in range(2 * SUB)}
        FIRST_PREP_AT = {FIRST_FEATS + i: (i // 2, i % 2) for i in range(2 * SUB)}
        FEAT_AT = {IC - GROUPS + g: g for g in range(GROUPS)}
        PART_AT = {7: 0, 8: 1, 9: 2, 11: 3, 12: 4, 13: 5, 14: 6}
        assert NT == 2 * NE and len(PART_AT) == PARTS

        def part_rows(i):
            return P if i < FC - 1 else REM

        def schedule(t, has_next, has_last, chunk, down, add, prep, features, part):
            for c in range(IC):
                if first_tile(t) and c < FIRST_FEATS:
                    features(t, GU_BANKS + c)
                chunk(t, c)
                if c >= LAG:
                    down(t, c - LAG)
                elif has_last:
                    down(t - 1, IC + c - LAG)
                if has_last and c == LAG - 1:
                    add(t - 1)
                prep_at = FIRST_PREP_AT if first_tile(t) else PREP_AT
                if has_next and c in prep_at:
                    prep(t + 1, *prep_at[c])
                if has_next and c in FEAT_AT:
                    features(t + 1, FEAT_AT[c])
                if c in PART_AT:
                    part(t, PART_AT[c])

        def nothing(*_):
            pass

        def steps(eng, chunk, down, add, prep, features, part):
            for moments in range(2):
                for s in range(SUB):
                    prep(0, s, moments)
            for g in range(GU_BANKS):
                features(0, g)
            schedule(0, True, False, chunk, down, add, prep, features, part)
            with eng.Fori(1, NT - 1) as t:
                schedule(t, True, True, chunk, down, add, prep, features, part)
            schedule(NT - 1, False, True, chunk, down, add, prep, features, part)
            for c in range(IC - LAG, IC):
                down(NT - 1, c)
            add(NT - 1)

        with nc.Block() as block:
            @block.sync
            def _(sp):
                def load_res(t):
                    sp.dma_start(x_res[:, :, :], x_tiles[bass.ds(t, 1)].rearrange("a p s h -> p (a s) h")).then_inc(res_loaded, 16)

                def store_x1(t):
                    for s in range(SUB):
                        sp.wait_ge(drained[OUT[s]], t + 2)
                    sp.dma_start(out_tiles[bass.ds(t, 1)].rearrange("a p s h -> p (a s) h"), x_res[:, :, :]).then_inc(x1_stored, 16)

                def next_x(t):
                    wait_prepared(sp, t)
                    load_x(sp, t + 1)

                def last_x1(t):
                    store_x1(t)
                    sp.wait_ge(x1_stored, 16 * (t + 1))

                down_halves = io["down_proj"].rearrange("e (a q p) f -> (e a) p q f", a=2, p=P)

                def load_part(t, name, e):
                    src = io[name][bass.ds(e, 1)]
                    sp.dma_start(raw_gu[:, 0:2, :], src[:, 0:2 * P, :].rearrange("a (c p) d -> p (a c) d", p=P)).then_inc(raw_loaded, 16)
                    sp.dma_start(raw_gu[0:REM, 2, :], src[:, 2 * P:FD, :].rearrange("a p d -> p (a d)")).then_inc(raw_loaded, 16)
                    sp.dma_start(raw_down[:, :, :], down_halves[bass.ds(t, 1)].rearrange("a p q f -> p (a q) f")).then_inc(raw_loaded, 16)

                def store_part(t):
                    sp.wait_ge(drained[PREP], use_part(t, PARTS - 1) + 2)
                    sp.dma_start(gate_up_dram[bass.ds(t, 1)].rearrange("a p w -> p (a w)"),
                                 split_gu[:, :, :, :].rearrange("p l k f -> p (l k f)").bitcast(F32)).then_inc(split_stored, 16)
                    sp.dma_start(expert_down_dram[bass.ds(t, 1)].rearrange("a p w -> p (a w)"),
                                 split_down[:, :, :, :].rearrange("p l f d -> p (l f d)").bitcast(F32)).then_inc(split_stored, 16)

                load_res(0)
                load_part(0, "gate_proj", 0)
                next_x(0)
                next_x(1)
                load_layer_weights(sp)
                store_part(0)
                load_part(1, "gate_proj", 1)
                for first, end, name in ((1, NE - 1, "gate_proj"), (NE - 1, NT - 2, "up_proj")):
                    with sp.Fori(first, end) as t:
                        last_x1(t - 1)
                        load_res(t)
                        next_x(t + 1)
                        store_part(t)
                        load_part(t + 1, name, t + 1 - NE if name == "up_proj" else t + 1)
                for t in (NT - 2, NT - 1):
                    last_x1(t - 1)
                    load_res(t)
                    store_part(t)
                    if t < NT - 1:
                        load_part(t + 1, "up_proj", t + 1 - NE)
                store_x1(NT - 1)

            @block.gpsimd
            def _(pool):
                nc.gpsimd.memset(x_in[:, :, D:XW], 0.0)
                nc.gpsimd.memset(pair[:, :, :, :].bitcast(F32), 0.0).then_inc(pads_set, 1)
                places = [0]

                def alone():
                    at = places[0]
                    places[0] += 1
                    nc.gpsimd.tensor_tensor(idle[:, at:at + 1], small[:, 0:1], small[:, 0:1], ALU.add)

                def gather_cond(t):
                    nc.gpsimd.tensor_copy(cond_now[:, :], cond_idx[:, bass.ds(SUB * t, SUB)]).then_inc(now_set, 1)
                    pool.wait_ge(now_set, t + 1)
                    alone()
                    for s in range(SUB):
                        nc.gpsimd.indirect_dma_start(cond_w[:, s, :], None, cond_rows,
                                                     bass.IndirectOffsetOnAxis(ap=cond_now[:, s:s + 1], axis=0)).then_inc(cond_loaded, 16)

                def features(t, g):
                    pool.wait_ge(f_high, GROUPS * t + g + 1)
                    nc.gpsimd.tensor_tensor(f_lo[:, g, :], f_sum[g % 2][:, :], f_hi[:, g, :].bitcast(F32), ALU.subtract).then_inc(f_done, 1)

                def body(t, gather, has_next):
                    for c in range(IC):
                        if first_tile(t) and c < FIRST_FEATS:
                            features(t, GU_BANKS + c)
                        pool.wait_ge(in_high, IC * t + c + 1)
                        nc.gpsimd.tensor_tensor(in_lo[:, c % RING, :], inner[c % INNER][:, :], in_hi[:, c % RING, :].bitcast(F32),
                                                ALU.subtract).then_inc(in_done, 1)
                        if gather and c == IC // 2:
                            pool.wait_ge(pair_done, t + 2)
                            alone()
                            gather_cond(t + 2)
                        if has_next and c in FEAT_AT:
                            features(t + 1, FEAT_AT[c])

                gather_cond(0)
                pool.wait_ge(pair_done, 1)
                gather_cond(1)
                for g in range(GU_BANKS):
                    features(0, g)
                body(0, True, True)
                with pool.Fori(1, NT - 1) as t:
                    body(t, True, True)
                body(NT - 1, False, False)
                pool.wait_ge(cond_loaded, 16 * SUB * (NT + 1))

            @block.tensor
            def _(pe):
                def product(bank, lh, ll, rh, rl, last):
                    nc.tensor.matmul(bank, lh, rh, start=True, stop=False)
                    nc.tensor.matmul(bank, lh, rl, start=False, stop=False)
                    ins = nc.tensor.matmul(bank, ll, rh, start=False, stop=True)
                    if last is not None:
                        ins.then_inc(last, 1)

                def prep(t, s, moments):
                    if not moments and s == 0:
                        pe.wait_ge(x_loaded, 16 * (t + 1))
                    bank = prep_bank(t, s)
                    pe.wait_ge(drained[bank], use_prep(t, s, moments) + 1)
                    for k in range(DK):
                        if moments:
                            ins = nc.tensor.matmul(psum[bank][:, 0:GROUPS * NPOLY], x_turned(t, s)[:, k * P:(k + 1) * P], mom[:, k, :],
                                                   start=(k == 0), stop=(k == DK - 1))
                        else:
                            ins = nc.tensor.transpose(psum[bank][:, k * P:(k + 1) * P], x_in[:, s, k * P:(k + 1) * P], ident[:, :])
                    ins.then_inc(filled[bank], 1)

                def features(t, g):
                    if g == 0:
                        wait_prepared(pe, t)
                        pe.wait_ge(pair_done, t + 1)
                    bank = feat_bank(t, g)
                    pe.wait_ge(drained[bank], use_feat(t, g) + 1)
                    for s in range(SUB):
                        at, both = psum[bank][0:NF, s * 2 * P:(s + 1) * 2 * P], pair[:, s, :, :].rearrange("p l n -> p (l n)")
                        nc.tensor.matmul(at, feat_hi[:, s, g, :], both, start=True, stop=False)
                        ins = nc.tensor.matmul(at[:, 0:P], feat_lo[:, s, g, :], pair_hi[:, s, :], start=False, stop=True)
                    ins.then_inc(filled[bank], 1)

                def chunk(t, c):
                    g, bank = c * P // GROUP, GU[c % GU_BANKS]
                    if c % (GROUP // P) == 0:
                        pe.wait_ge(f_done, GROUPS * t + g + 1)
                    pe.wait_ge(drained[bank], use_gu(t, c) + 1)
                    cols = slice(c * P, (c + 1) * P)
                    for m in range(2):
                        product(psum[bank][:, m * TILE:(m + 1) * TILE], gu_hi[:, m, cols], gu_lo[:, m, cols], f_hi[:, g, :], f_lo[:, g, :],
                                filled[bank] if m else None)

                def down(t, c):
                    pe.wait_ge(in_done, IC * t + c + 1)
                    for s in range(SUB):
                        bank, rows = OUT[s], slice(s * P, (s + 1) * P)
                        if c == 0:
                            pe.wait_ge(drained[bank], t + 1)
                        nc.tensor.matmul(psum[bank][:, :], in_hi[:, c % RING, rows], down_hi[:, c, :], start=(c == 0), stop=False)
                        nc.tensor.matmul(psum[bank][:, :], in_hi[:, c % RING, rows], down_lo[:, c, :], start=False, stop=False)
                        ins = nc.tensor.matmul(psum[bank][:, :], in_lo[:, c % RING, rows], down_hi[:, c, :], start=False, stop=(c == IC - 1))
                        if c == IC - 1:
                            ins.then_inc(filled[bank], 1)

                def part(t, i):
                    if i == 0:
                        pe.wait_ge(raw_loaded, 48 * (t + 1))
                    pe.wait_ge(drained[PREP], use_part(t, i) + 1)
                    if i < DK:
                        for f in range(FC):
                            rows = part_rows(f)
                            ins = nc.tensor.transpose(psum[PREP][:, f * P:f * P + rows], raw_gu[0:rows, f, i * P:(i + 1) * P], ident[0:rows, 0:rows])
                    else:
                        f = i - DK
                        rows = part_rows(f)
                        for q in range(2):
                            ins = nc.tensor.transpose(psum[PREP][0:rows, q * P:(q + 1) * P], raw_down[:, q, f * P:f * P + rows], ident[:, :])
                    ins.then_inc(filled[PREP], 1)

                steps(pe, chunk, down, nothing, prep, features, part)

            @block.scalar
            def _(act):
                def pairs(t):
                    act.wait_ge(cond_loaded, 16 * SUB * (t + 1))
                    for half in range(2):
                        rows = slice(64 * half, 64 * half + 64)
                        ins = nc.scalar.activation(pair_hi[rows, :, rows], cond_w[rows, :, :], ACT.Copy)
                    ins.then_inc(pair_high, 1)

                def raw(s):
                    return view(x_in[:, :, :], s * XW, [[KNOT_STEP, GROUPS], [KNOT_GAP, KNOTS], [1, KNOT_W]])

                def prep(t, s, moments):
                    bank = prep_bank(t, s)
                    act.wait_ge(filled[bank], use_prep(t, s, moments) + 1)
                    if not moments:
                        if s == 0 and not first_tile(t):
                            pairs(t)
                        nc.scalar.activation(x_turned(t, s)[:, :], psum[bank][:, :], ACT.Copy).then_inc(drained[bank], 1)
                        nc.scalar.activation(feat_hi[:, s, :, NPOLY:NF].rearrange("p g (k w) -> p g k w", k=KNOTS), raw(s),
                                             ACT.Copy).then_inc(raw_high, 1)
                    else:
                        nc.scalar.activation(feat_hi[:, s, :, 0:NPOLY], psum[bank][:, 0:GROUPS * NPOLY].rearrange("p (g n) -> p g n", g=GROUPS),
                                             ACT.Copy).then_inc(mom_high, 1)
                        if s == SUB - 1 and first_tile(t):
                            pairs(t)

                def features(t, g):
                    act.wait_ge(drained[feat_bank(t, g)], use_feat(t, g) + 2)
                    nc.scalar.activation(f_hi[:, g, :], f_sum[g % 2][:, :], ACT.Copy).then_inc(f_high, 1)

                def chunk(t, c):
                    bank = GU[c % GU_BANKS]
                    act.wait_ge(filled[bank], use_gu(t, c) + 1)
                    nc.scalar.activation(silu[c % GU_BANKS][:, :], psum[bank][:, 0:TILE], ACT.Silu).then_inc(silu_done, 1)

                def part(t, i):
                    if i == 0 and not (isinstance(t, int) and t == 0):
                        act.wait_ge(split_stored, 32 * t)
                    act.wait_ge(filled[PREP], use_part(t, i) + 1)
                    if i < DK:
                        nc.scalar.activation(split_gu[:, 0, i, :], psum[PREP][:, 0:FD], ACT.Copy).then_inc(split_high, 1)
                    else:
                        rows = part_rows(i - DK)
                        nc.scalar.activation(split_down[0:rows, 0, i - DK, :], psum[PREP][0:rows, 0:D // 2], ACT.Copy).then_inc(split_high, 1)

                nc.scalar.activation(idle[:, 63:64], small[:, 0:1], ACT.Silu)
                act.wait_ge(pads_set, 1)
                steps(act, chunk, nothing, nothing, prep, features, part)

            @block.vector
            def _(dve):
                for i in range(8):
                    nc.vector.nop().then_inc(drained[i], 1)

                def pairs(t):
                    dve.wait_ge(pair_high, t + 1)
                    for half in range(2):
                        rows = slice(64 * half, 64 * half + 64)
                        ins = nc.vector.tensor_tensor(pair_lo[rows, :, rows], cond_w[rows, :, :], pair_hi[rows, :, rows].bitcast(F32), ALU.subtract)
                    ins.then_inc(pair_done, 1)

                def prep(t, s, moments):
                    if not moments:
                        if s == 0 and not first_tile(t):
                            pairs(t)
                        dve.wait_ge(raw_high, SUB * t + s + 1)
                        raw = view(x_in[:, :, :], s * XW, [[KNOT_STEP, GROUPS], [KNOT_GAP, KNOTS], [1, KNOT_W]])
                        part = lambda f: f[:, s, :, NPOLY:NF].rearrange("p g (k w) -> p g k w", k=KNOTS)
                        nc.vector.tensor_tensor(part(feat_lo), raw, part(feat_hi).bitcast(F32), ALU.subtract)
                    else:
                        dve.wait_ge(mom_high, SUB * t + s + 1)
                        nc.vector.tensor_tensor(feat_lo[:, s, :, 0:NPOLY], psum[prep_bank(t, s)][:, 0:GROUPS * NPOLY].rearrange("p (g n) -> p g n", g=GROUPS),
                                                feat_hi[:, s, :, 0:NPOLY].bitcast(F32), ALU.subtract).then_inc(drained[prep_bank(t, s)], 1)
                        if s == SUB - 1 and first_tile(t):
                            pairs(t)

                def features(t, g):
                    bank = feat_bank(t, g)
                    dve.wait_ge(filled[bank], use_feat(t, g) + 1)
                    if not (first_tile(t) and g < 2):
                        dve.wait_ge(f_done, GROUPS * t + g - 1)
                    nc.vector.tensor_reduce(f_sum[g % 2][:, :].rearrange("p (s n) -> p s n", s=SUB),
                                            view(psum[bank][0:NF, :], 0, [[2 * P, SUB], [1, P], [P, 2]]), AX.X, ALU.add).then_inc(drained[bank], 1)

                def high_inner(t, c):
                    dve.wait_ge(drained[GU[c % GU_BANKS]], use_gu(t, c) + 2)
                    nc.vector.tensor_copy(in_hi[:, c % RING, :], inner[c % INNER][:, :]).then_inc(in_high, 1)

                def chunk(t, c):
                    bank = GU[c % GU_BANKS]
                    dve.wait_ge(silu_done, IC * t + c + 1)
                    if not isinstance(t, int) or t > 0 or c >= INNER:
                        dve.wait_ge(in_done, IC * t + c - INNER + 1)
                    nc.vector.tensor_tensor(inner[c % INNER][:, :], silu[c % GU_BANKS][:, :], psum[bank][:, TILE:2 * TILE],
                                            ALU.mult).then_inc(drained[bank], 1)
                    high_inner(t, c)

                def add(t):
                    dve.wait_ge(res_loaded, 16 * (t + 1))
                    for s in range(SUB):
                        dve.wait_ge(filled[OUT[s]], t + 1)
                        nc.vector.tensor_tensor(x_res[:, s, :], psum[OUT[s]][:, :], x_res[:, s, :], ALU.add).then_inc(drained[OUT[s]], 1)

                def part(t, i):
                    dve.wait_ge(split_high, PARTS * t + i + 1)
                    if i < DK:
                        nc.vector.tensor_tensor(split_gu[:, 1, i, :], psum[PREP][:, 0:FD], split_gu[:, 0, i, :].bitcast(F32),
                                                ALU.subtract).then_inc(drained[PREP], 1)
                    else:
                        rows = part_rows(i - DK)
                        nc.vector.tensor_tensor(split_down[0:rows, 1, i - DK, :], psum[PREP][0:rows, 0:D // 2],
                                                split_down[0:rows, 0, i - DK, :].bitcast(F32), ALU.subtract).then_inc(drained[PREP], 1)

                nc.vector.memset(split_down[REM:P, :, FC - 1, :].bitcast(F32), 0.0)
                dve.wait_ge(pads_set, 1)
                steps(dve, chunk, nothing, add, prep, features, part)


def adapted_layer(nc, alloc, sem, psum, ident, small, idle, lower, ones, tok_ids, layer_tiles, z_tiles, x1, x1_loaded,
                  w_hi, w_lo, a_hi, a_lo, adapter_scale, chosen, table_dram, load_expert, staging, x_both, ctl, chosen_at, ctl_ready):
    with ExitStack() as scope:
        sb = alloc(scope)
        x1t_hi = [sb(f"x1t_hi{b}", [P, DK, LTILE], F32R) for b in range(2)]
        x1t_lo = [sb(f"x1t_lo{b}", [P, DK, LTILE], F32R) for b in range(2)]
        xa = sb("xa", [P, LTILE])
        xa_hi, xa_lo = sb("xa_hi", [P, LTILE], F32R), sb("xa_lo", [P, LTILE], F32R)
        z_out = [view(place, 0, [[WIDE, LSUB], [1, WIDE]]) for place in (staging[:, :], x_both[:, :, :, :])]
        top1, top2, at = sb("top1", [P, LSUB]), sb("top2", [P, LSUB]), sb("at", [P, LSUB])
        below, masked, *picked, both, pos = (view(staging[:, :], LSUB * WIDE + i * LSUB * NE, [[NE, LSUB], [1, NE]]) for i in range(6))
        row_f = sb("row_f", [P, 2, LSUB])
        gap, expo, total = sb("gap", [P, LSUB]), sb("expo", [P, LSUB]), sb("total", [P, LSUB])
        row_i, entry = sb("row_i", [P, 2, LSUB], I32), sb("entry", [P, LSUB, 2, 2])
        taken, free = PLACES + 2 * COLS + NE + CHUNKS * COLS, [(DK + 3) * D]

        def spare(*shape):
            free[0] -= int(np.prod(shape))
            assert free[0] >= taken
            return view(staging[:, :], free[0], [[int(np.prod(shape[i + 1:])), n] for i, n in enumerate(shape)])

        count, blocks_from, full_blocks = spare(NE), spare(MAX_BLOCKS), spare(NE, MAX_BLOCKS)
        n_blocks, ends = spare(NE), [spare(NE) for _ in range(2)]
        expert_f, start_f, wrapped, column = (spare(COLS) for _ in range(4))
        ctl_f = spare(2 * COLS + NE)
        past_end, past_blocks = (view(staging[:, :], i * COLS * (NE - 1), [[NE - 1, COLS], [1, NE - 1]]) for i in range(2))
        place_step, counted = sem("place_step"), sem("counted")

        X1T, XA, RANKS, Z = [0, 1], 2, 3, [[4, 5], [6, 7]]
        filled = [sem(f"al_filled{i}") for i in range(8)]
        drained = [sem(f"al_drained{i}") for i in range(8)]
        z_stored = [sem(f"z_stored{b}") for b in range(2)]
        x1t_high, xa_high, xa_done, idle_done = sem("x1t_high"), sem("xa_high"), sem("xa_done"), sem("idle_done")
        chosen_set, step, both_ready = sem("chosen_set"), sem("route_step"), sem("both_ready")
        gap_ready, expo_ready, entries_ready, entries_stored = (sem(n) for n in ("gap_ready", "expo_ready", "entries_ready", "entries_stored"))
        LINKS = 23
        FIRST_LINKS = 16

        def use(t, s):
            return LSUB // 2 * t + s // 2

        def steps(eng, body):
            body(0, 0, 0, True, True)
            body(1, 0, 1, True, True)
            with eng.Fori(1, LNT // 2 - 1) as k:
                for b in range(2):
                    body(2 * k + b, k, b, True, False)
            body(LNT - 2, LNT // 2 - 1, 0, True, False)
            body(LNT - 1, LNT // 2 - 1, 1, False, False)

        with nc.Block() as block:
            @block.sync
            def _(sp):
                def body(t, n, b, has_next, first):
                    if has_next:
                        if not (first and b == 0):
                            sp.wait_ge(filled[X1T[1]], use(t, LSUB - 1) - LSUB // 2 + 1)
                        sp.dma_start(x1[1 - b][:, :, :], layer_tiles[bass.ds(t + 1, 1)].rearrange("a p s h -> p (a s) h")).then_inc(x1_loaded[1 - b], 16)
                    if first:
                        load_expert(sp, b, False)

                steps(sp, body)
                load_expert(sp, SLOTS - 1, False)
                for b in range(2):
                    sp.wait_ge(z_stored[b], 16 * LNT // 2)

            @block.gpsimd
            def _(pool):
                def body(t, n, b, has_next, first):
                    if not (first and b == 0):
                        pool.wait_ge(idle_done, t)
                    pool.wait_ge(entries_ready, t + 1)
                    nc.gpsimd.tensor_tensor(idle[:, 0:1], small[:, 0:1], small[:, 0:1], ALU.add).then_inc(idle_done, 1)
                    for k in range(2):
                        for s in range(LSUB):
                            nc.gpsimd.indirect_dma_start(table_dram, bass.IndirectOffsetOnAxis(ap=row_i[:, k, s:s + 1], axis=0),
                                                         entry[:, s, k, :], None).then_inc(entries_stored, 16)

                steps(pool, body)
                pool.wait_ge(entries_stored, 16 * 2 * LSUB * LNT)

            @block.tensor
            def _(pe):
                def transpose(t, n, b, s):
                    if s == 0:
                        pe.wait_ge(x1_loaded[b], 16 * (n + 1))
                    bank = X1T[s % 2]
                    pe.wait_ge(drained[bank], use(t, s) + 1)
                    for k in range(DK):
                        ins = nc.tensor.transpose(psum[bank][:, k * P:(k + 1) * P], x1[b][:, s, k * P:(k + 1) * P], ident[:, :])
                    ins.then_inc(filled[bank], 1)

                def ranks(t):
                    pe.wait_ge(both_ready, t + 1)
                    nc.tensor.matmul(psum[RANKS][:, 0:LSUB * NE], lower[:, :], both[:, :, :].rearrange("p s e -> p (s e)"), start=True, stop=False)
                    nc.tensor.matmul(psum[RANKS][:, 0:LSUB * NE], ones[:, :], chosen[:, 0:LSUB, :].rearrange("p s e -> p (s e)"),
                                     start=False, stop=True).then_inc(filled[RANKS], 1)

                def body(t, n, b, has_next, first):
                    for s in (LSUB - 2, LSUB - 1):
                        pe.wait_ge(drained[X1T[s % 2]], use(t, s) + 2)
                    hi, lo = x1t_hi[b], x1t_lo[b]
                    pe.wait_ge(drained[XA], t + 1)
                    for k in range(DK):
                        nc.tensor.matmul(psum[XA][:, :], a_hi[:, k, :], hi[:, k, :], start=(k == 0), stop=False)
                        nc.tensor.matmul(psum[XA][:, :], a_hi[:, k, :], lo[:, k, :], start=False, stop=False)
                        ins = nc.tensor.matmul(psum[XA][:, :], a_lo[:, k, :], hi[:, k, :], start=False, stop=(k == DK - 1))
                    ins.then_inc(filled[XA], 1)

                    def product(s, half, chunks):
                        bank, rows = Z[s % 2][half], slice(s * P, (s + 1) * P)
                        if 0 in chunks:
                            pe.wait_ge(drained[bank], use(t, s) + 1)
                        for k in chunks:
                            x_high, x_low = (hi[:, k, rows], lo[:, k, rows]) if k < DK else (xa_hi[:, rows], xa_lo[:, rows])
                            for i, (x, w) in enumerate(((x_high, w_hi), (x_high, w_lo), (x_low, w_hi))):
                                last = k == DK and i == 2
                                ins = nc.tensor.matmul(psum[bank][:, 0:HALFW], x, w[:, k, half * HALFW:(half + 1) * HALFW],
                                                       start=(k == 0 and i == 0), stop=last)
                        if DK in chunks:
                            ins.then_inc(filled[bank], 1)

                    for s in range(2):
                        if has_next:
                            transpose(t + 1, n + b, 1 - b, s)
                        product(s, 1, range(DK))
                    pe.wait_ge(xa_done, t + 1)
                    for s in range(2):
                        product(s, 1, [DK])
                    for s in range(2, LSUB):
                        if has_next:
                            transpose(t + 1, n + b, 1 - b, s)
                        product(s, 1, range(DK + 1))
                    for s in range(LSUB):
                        product(s, 0, range(DK + 1))
                        if s == LSUB - 2:
                            ranks(t)

                for s in range(LSUB):
                    transpose(0, 0, 0, s)
                steps(pe, body)
                nc.tensor.matmul(psum[XA][:, 0:NE], ones[:, :], chosen[:, LSUB, :], start=True, stop=True).then_inc(counted, 1)

            @block.scalar
            def _(act):
                def transpose(t, b, s):
                    act.wait_ge(filled[X1T[s % 2]], use(t, s) + 1)
                    nc.scalar.activation(x1t_hi[b][:, :, s * P:(s + 1) * P], psum[X1T[s % 2]][:, :].rearrange("p (k n) -> p k n", k=DK),
                                         ACT.Copy).then_inc(x1t_high, 1)

                def shares(t):
                    act.wait_ge(gap_ready, t + 1)
                    nc.scalar.activation(expo[:, :], gap[:, :], ACT.Exp).then_inc(expo_ready, 1)

                def body(t, n, b, has_next, first):
                    act.wait_ge(drained[XA], t + 2)
                    nc.scalar.activation(xa_hi[:, :], xa[:, :], ACT.Copy).then_inc(xa_high, 1)
                    def copy(s, half):
                        bank = Z[s % 2][half]
                        act.wait_ge(filled[bank], use(t, s) + 1)
                        nc.scalar.activation(z_out[b][:, s, half * HALFW:(half + 1) * HALFW], psum[bank][:, 0:HALFW], ACT.Copy).then_inc(drained[bank], 1)

                    if has_next:
                        transpose(t + 1, 1 - b, 0)
                        transpose(t + 1, 1 - b, 1)
                    if not first:
                        act.wait_ge(z_stored[b], 16 * n)
                    copy(0, 1)
                    copy(1, 1)
                    for s in range(2, LSUB):
                        if has_next:
                            transpose(t + 1, 1 - b, s)
                        copy(s, 1)
                    for s in range(LSUB):
                        copy(s, 0)
                        if s == LSUB - 2:
                            shares(t)
                    for bank in (*Z[0], *Z[1]):
                        act.wait_ge(drained[bank], use(t, LSUB - 1) + 2)
                    act.dma_start(z_tiles[bass.ds(t, 1)].rearrange("a p s h -> p (a s) h"), z_out[b][:, :, 0:D]).then_inc(z_stored[b], 16)

                for s in range(LSUB):
                    transpose(0, 0, s)
                steps(act, body)

            @block.vector
            def _(dve):
                for i in range(8):
                    nc.vector.nop().then_inc(drained[i], 1)
                nc.vector.memset(chosen[:, :, :], 0.0).then_inc(chosen_set, 1)
                dve.wait_ge(chosen_set, 1)

                def transpose(t, b, s):
                    cols = slice(s * P, (s + 1) * P)
                    dve.wait_ge(x1t_high, LSUB * t + s + 1)
                    nc.vector.tensor_tensor(x1t_lo[b][:, :, cols], psum[X1T[s % 2]][:, :].rearrange("p (k n) -> p k n", k=DK),
                                            x1t_hi[b][:, :, cols].bitcast(F32), ALU.subtract).then_inc(drained[X1T[s % 2]], 1)

                wide = lambda ap: ap.rearrange("p (n e) -> p n e", e=1).to_broadcast([P, LSUB, NE])
                iota = view(small[:, :], 16, [[0, LSUB], [1, NE]])
                links = [0]

                def link(t, ins):
                    links[0] += 1
                    ins.then_inc(step, 1)
                    dve.wait_ge(step, LINKS * t + links[0])

                def pick(t, values, top, k):
                    link(t, nc.vector.tensor_reduce(top[:, :], values, AX.X, ALU.max))
                    link(t, nc.vector.tensor_tensor(below[:, :, :], values, wide(top[:, :]), ALU.is_lt))
                    link(t, nc.vector.scalar_tensor_tensor(below[:, :, :], below[:, :, :], float(NE), iota, ALU.mult, ALU.add))
                    link(t, nc.vector.tensor_reduce(at[:, :], below[:, :, :], AX.X, ALU.min))
                    link(t, nc.vector.tensor_tensor(picked[k][:, :, :], iota, wide(at[:, :]), ALU.is_equal))

                def choose(t, b):
                    links[0] = 0
                    for s in (LSUB - 2, LSUB - 1):
                        dve.wait_ge(drained[Z[s % 2][1]], use(t, s) + 2)
                    logits = z_out[b][:, :, D:]
                    pick(t, logits, top1, 0)
                    link(t, nc.vector.scalar_tensor_tensor(masked[:, :, :], picked[0][:, :, :], -3e38, logits, ALU.mult, ALU.add))
                    pick(t, masked[:, :, :], top2, 1)
                    nc.vector.tensor_tensor(gap[:, :], top2[:, :], top1[:, :], ALU.subtract).then_inc(gap_ready, 1)
                    nc.vector.tensor_copy(chosen[:, 0, :], chosen[:, LSUB, :])
                    link(t, nc.vector.tensor_tensor(both[:, :, :], picked[0][:, :, :], picked[1][:, :, :], ALU.add))
                    for s in range(LSUB):
                        link(t, nc.vector.tensor_tensor(chosen[:, s + 1, :], chosen[:, s, :], both[:, s, :], ALU.add))
                    nc.vector.nop().then_inc(both_ready, 1)
                    assert links[0] == FIRST_LINKS, links[0]

                def enter(t, first):
                    links[0] = FIRST_LINKS
                    dve.wait_ge(filled[RANKS], t + 1)
                    link(t, nc.vector.scalar_tensor_tensor(pos[:, :, :], iota, float(REGION * P), psum[RANKS][:, 0:LSUB * NE].rearrange("p (s e) -> p s e", s=LSUB),
                                                           ALU.mult, ALU.add))
                    for k in range(2):
                        link(t, nc.vector.tensor_tensor(picked[k][:, :, :], picked[k][:, :, :], pos[:, :, :], ALU.mult))
                        link(t, nc.vector.tensor_reduce(row_f[:, k, :], picked[k][:, :, :], AX.X, ALU.add))
                    if not first:
                        dve.wait_ge(entries_stored, 16 * 2 * LSUB * t)
                    nc.vector.tensor_copy(row_i[:, :, :], row_f[:, :, :])
                    for k in range(2):
                        nc.vector.tensor_copy(entry[:, :, k, 0], tok_ids[:, bass.ds(LSUB * t, LSUB)])
                    dve.wait_ge(expo_ready, t + 1)
                    link(t, nc.vector.tensor_scalar(total[:, :], expo[:, :], 1.0, None, ALU.add))
                    link(t, nc.vector.reciprocal(entry[:, :, 0, 1], total[:, :]))
                    nc.vector.tensor_tensor(entry[:, :, 1, 1], expo[:, :], entry[:, :, 0, 1], ALU.mult).then_inc(entries_ready, 1)
                    assert links[0] == LINKS, links[0]

                def body(t, n, b, has_next, first):
                    dve.wait_ge(filled[XA], t + 1)
                    batches = LTILE // SEQ
                    own = adapter_scale[:, bass.ds(batches * t, batches)]
                    nc.vector.tensor_tensor(xa[:, :].rearrange("p (b c) -> p b c", b=batches), psum[XA][:, :].rearrange("p (b c) -> p b c", b=batches),
                                            own.rearrange("p (b c) -> p b c", c=1).to_broadcast([P, batches, SEQ]), ALU.mult).then_inc(drained[XA], 1)
                    dve.wait_ge(xa_high, t + 1)
                    nc.vector.tensor_tensor(xa_lo[:, :], xa[:, :], xa_hi[:, :].bitcast(F32), ALU.subtract).then_inc(xa_done, 1)
                    for s in range(LSUB):
                        if has_next:
                            transpose(t + 1, 1 - b, s)
                    choose(t, b)
                    enter(t, first and b == 0)

                for s in range(LSUB):
                    transpose(0, 0, s)
                steps(dve, body)

                places = [0]

                def then(ins):
                    places[0] += 1
                    ins.then_inc(place_step, 1)
                    dve.wait_ge(place_step, places[0])

                def prefix(a, other, n):
                    d = 1
                    while d < n:
                        nc.vector.tensor_copy(other[:, 0:d, :], a[:, 0:d, :])
                        then(nc.vector.tensor_tensor(other[:, d:n, :], a[:, d:n, :], a[:, 0:n - d, :], ALU.add))
                        a, other, d = other, a, 2 * d
                    return a

                dve.wait_ge(z_stored[0], 16 * LNT // 2)
                dve.wait_ge(counted, 1)
                then(nc.vector.tensor_scalar(count, psum[XA][:, 0:NE], 1.0, None, ALU.max))
                then(nc.vector.tensor_scalar(blocks_from, small[:, 24:24 + MAX_BLOCKS], float(P), None, ALU.mult))
                then(nc.vector.tensor_tensor(full_blocks, view(count, 0, [[1, NE], [0, MAX_BLOCKS]]),
                                             view(blocks_from, 0, [[0, NE], [1, MAX_BLOCKS]]), ALU.is_gt))
                then(nc.vector.tensor_reduce(n_blocks, full_blocks, AX.X, ALU.add))
                then(nc.vector.tensor_copy(ends[0], n_blocks))
                tall = lambda t: t.rearrange("p (e a) -> p e a", a=1)
                end = prefix(tall(ends[0]), tall(ends[1]), NE).rearrange("p e a -> p (e a)")
                then(nc.vector.tensor_tensor(past_end, view(small[:, :], 24, [[1, COLS], [0, NE - 1]]),
                                             view(end, 0, [[0, COLS], [1, NE - 1]]), ALU.is_ge))
                then(nc.vector.tensor_tensor(past_blocks, past_end, view(n_blocks, 0, [[0, COLS], [1, NE - 1]]), ALU.mult))
                nc.vector.tensor_reduce(expert_f, past_end, AX.X, ALU.add)
                then(nc.vector.tensor_reduce(start_f, past_blocks, AX.X, ALU.add))
                then(nc.vector.tensor_tensor(column, small[:, 24:24 + COLS], start_f, ALU.subtract))
                then(nc.vector.tensor_scalar(column, column, float(MAX_BLOCKS), None, ALU.min))
                then(nc.vector.scalar_tensor_tensor(column, expert_f, float(REGION), column, ALU.mult, ALU.add))
                for c in range(CHUNKS):
                    ins = nc.vector.tensor_scalar(chosen_at[:, c, :], column, small[:, 2 + c:3 + c], None, ALU.is_equal)
                then(nc.vector.tensor_copy(ctl_f[:, 0:COLS], expert_f))
                for first in range(SLOTS, NE, SLOTS):
                    then(nc.vector.tensor_scalar(wrapped, expert_f, float(first), float(SLOTS), ALU.is_ge, ALU.mult))
                    then(nc.vector.tensor_tensor(ctl_f[:, 0:COLS], ctl_f[:, 0:COLS], wrapped, ALU.subtract))
                nc.vector.tensor_scalar(ctl_f[:, COLS:2 * COLS], expert_f, float(LOADS), float(LOADS), ALU.mult, ALU.add)
                then(nc.vector.tensor_copy(ctl_f[:, 2 * COLS:2 * COLS + NE], end))
                nc.vector.tensor_copy(ctl, ctl_f).then_inc(ctl_ready, 1)


def experts(nc, alloc, sem, psum, ident, small, idle, slots, weights_loaded, load_expert, table_dram, z_dram, out,
            ctl, chosen_at, ctl_ready):
    with ExitStack() as scope:
        sb = alloc(scope)
        columns = sb("columns", [P, CHUNKS, P, 2])
        row_of, share_of = sb("row_of", [P, COLS], I32), sb("share_of", [P, COLS])
        z_now = [sb(f"z_now{b}", [P, D]) for b in range(2)]
        gather_at = [sb(f"gather_at{b}", [P, 1], I32) for b in range(2)]
        scatter_at = [sb(f"scatter_at{b}", [P, 1], I32) for b in range(2)]
        zt_hi, zt_lo = sb("zt_hi", [P, DK, P], F32R), sb("zt_lo", [P, DK, P], F32R)
        silu_g, hid = sb("silu_g", [P, FD]), sb("hid", [P, FP])
        ht_hi, ht_lo = sb("ht_hi", [P, FC, P], F32R), sb("ht_lo", [P, FC, P], F32R)
        result = [sb(f"result{b}", [P, D]) for b in range(2)]

        columns_loaded, sorted_filled, table_ready, hid_set = (sem(n) for n in ("columns_loaded", "sorted_filled", "table_ready", "hid_set"))
        ZT, GATE, UP, HT, OUT, SORTED = 0, 1, 2, 3, [4, 5], 7
        filled = [sem(f"ex_filled{i}") for i in range(6)]
        drained = [sem(f"ex_drained{i}") for i in range(6)]
        z_loaded = [sem(f"ex_z_loaded{b}") for b in range(2)]
        zt_high, ht_high = sem("zt_high"), sem("ht_high")
        gather_set, scatter_set, added = sem("gather_set"), sem("scatter_set"), sem("added")

        with nc.Block() as block:
            @block.sync
            def _(sp):
                full = table_dram[0:(CHUNKS - 1) * P * P, :].rearrange("(c q p) w -> q c (p w)", q=P, p=P)
                sp.dma_start(columns[:, 0:CHUNKS - 1, :, :].rearrange("q c p w -> q c (p w)"), full).then_inc(columns_loaded, 16)
                sp.dma_start(columns[0:REST, CHUNKS - 1, :, :].rearrange("q p w -> q (p w)"),
                             table_dram[(CHUNKS - 1) * P * P:, :].rearrange("(q p) w -> q (p w)", p=P)).then_inc(columns_loaded, 16)
                sp.wait_ge(ctl_ready, 1)
                for e in range(SLOTS, NE):
                    end = 2 * COLS + e - SLOTS
                    blocks = sp.value_load(ctl[0:1, end:end + 1], min_val=1, max_val=BLOCKS)
                    sp.wait_ge(filled[HT], blocks + 1)
                    load_expert(sp, e, True)

            @block.gpsimd
            def _(pool):
                nc.gpsimd.memset(hid[:, :], 0.0).then_inc(hid_set, 1)
                pool.wait_ge(table_ready, 1)
                places = [0]

                def alone():
                    at = places[0]
                    places[0] += 1
                    nc.gpsimd.tensor_tensor(idle[:, at:at + 1], small[:, 0:1], small[:, 0:1], ALU.add)


                def gather(j, b):
                    nc.gpsimd.tensor_copy(gather_at[b][:, :], row_of[:, bass.ds(j, 1)]).then_inc(gather_set, 1)
                    pool.wait_ge(gather_set, j + 1)
                    alone()
                    nc.gpsimd.indirect_dma_start(z_now[b][:, :], None, z_dram,
                                                 bass.IndirectOffsetOnAxis(ap=gather_at[b][:, 0:1], axis=0)).then_inc(z_loaded[b], 16)

                def set_scatter(j, b):
                    nc.gpsimd.tensor_copy(scatter_at[b][:, :], row_of[:, bass.ds(j, 1)]).then_inc(scatter_set, 1)

                def scatter(j, n, b, first):
                    if not first:
                        pool.wait_ge(added, 16 * j)
                        alone()
                    pool.wait_ge(scatter_set, j + 1)
                    pool.wait_ge(drained[OUT[b]], n + 2)
                    alone()
                    nc.gpsimd.indirect_dma_start(out, bass.IndirectOffsetOnAxis(ap=scatter_at[b][:, 0:1], axis=0),
                                                 result[b][:, :], None, compute_op=ALU.add).then_inc(added, 16)

                def body(j, n, b, more, first):
                    set_scatter(j - 1, 1 - b)
                    if more:
                        pool.wait_ge(filled[ZT], j + 1)
                        alone()
                        gather(j + 2, b)
                    scatter(j - 1, n - 1 + b, 1 - b, first)

                gather(0, 0)
                gather(1, 1)
                pool.wait_ge(filled[ZT], 1)
                gather(2, 0)
                body(1, 0, 1, True, True)
                body(2, 1, 0, True, False)
                with pool.Fori(1, BLOCKS // 2) as k:
                    body(2 * k + 1, k, 1, True, False)
                    body(2 * k + 2, k + 1, 0, True, False)
                set_scatter(BLOCKS - 1, 0)
                scatter(BLOCKS - 1, BLOCKS // 2, 0, False)
                pool.wait_ge(added, 16 * BLOCKS)
                for b in range(2):
                    pool.wait_ge(z_loaded[b], 16 * ((COLS - b + 1) // 2))

            @block.tensor
            def _(pe):
                pe.wait_ge(columns_loaded, 32)
                for w in range(2):
                    for c in range(CHUNKS):
                        rows = P if c < CHUNKS - 1 else REST
                        ins = nc.tensor.matmul(psum[SORTED][:, w * COLS:(w + 1) * COLS], columns[0:rows, c, :, w], chosen_at[0:rows, c, :],
                                               start=(c == 0), stop=(c == CHUNKS - 1))
                ins.then_inc(sorted_filled, 1)
                pe.wait_ge(hid_set, 1)

                def transpose_z(j, n, b):
                    pe.wait_ge(z_loaded[b], 16 * (n + 1))
                    pe.wait_ge(drained[ZT], j + 1)
                    for k in range(DK):
                        ins = nc.tensor.transpose(psum[ZT][:, k * P:(k + 1) * P], z_now[b][:, k * P:(k + 1) * P], ident[:, :])
                    ins.then_inc(filled[ZT], 1)

                def gate_up(j, slot):
                    pe.wait_ge(drained[ZT], j + 2)
                    for bank, high, low in ((GATE, GH, GL), (UP, UH, UL)):
                        pe.wait_ge(drained[bank], j + 1)
                        for k in range(DK):
                            w_high = slots[:, bass.ds(slot, 1), high + k * FD:high + (k + 1) * FD].rearrange("p a n -> p (a n)")
                            w_low = slots[:, bass.ds(slot, 1), low + k * FD:low + (k + 1) * FD].rearrange("p a n -> p (a n)")
                            nc.tensor.matmul(psum[bank][:, 0:FD], zt_hi[:, k, :], w_high, start=(k == 0), stop=False)
                            nc.tensor.matmul(psum[bank][:, 0:FD], zt_hi[:, k, :], w_low, start=False, stop=False)
                            ins = nc.tensor.matmul(psum[bank][:, 0:FD], zt_lo[:, k, :], w_high, start=False, stop=(k == DK - 1))
                        ins.then_inc(filled[bank], 1)

                def transpose_h(j):
                    pe.wait_ge(drained[UP], j + 2)
                    pe.wait_ge(drained[HT], j + 1)
                    for f in range(FC):
                        ins = nc.tensor.transpose(psum[HT][:, f * P:(f + 1) * P], hid[:, f * P:(f + 1) * P], ident[:, :])
                    ins.then_inc(filled[HT], 1)

                def down(j, n, b, slot):
                    pe.wait_ge(drained[HT], j + 2)
                    pe.wait_ge(drained[OUT[b]], n + 1)
                    for f in range(FC):
                        w_high = slots[:, bass.ds(slot, 1), DH_ + f * D:DH_ + (f + 1) * D].rearrange("p a n -> p (a n)")
                        w_low = slots[:, bass.ds(slot, 1), DL_ + f * D:DL_ + (f + 1) * D].rearrange("p a n -> p (a n)")
                        nc.tensor.matmul(psum[OUT[b]][:, :], ht_hi[:, f, :], w_high, start=(f == 0), stop=False)
                        nc.tensor.matmul(psum[OUT[b]][:, :], ht_hi[:, f, :], w_low, start=False, stop=False)
                        ins = nc.tensor.matmul(psum[OUT[b]][:, :], ht_lo[:, f, :], w_high, start=False, stop=(f == FC - 1))
                    ins.then_inc(filled[OUT[b]], 1)

                def slot_of(j):
                    pe.wait_ge(ctl_ready, 1)
                    return pe.value_load(ctl[0:1, bass.ds(j, 1)], min_val=0, max_val=SLOTS - 1)

                def wait_weights(j):
                    pe.wait_ge(ctl_ready, 1)
                    loaded = pe.value_load(ctl[0:1, bass.ds(j + COLS, 1)], min_val=LOADS, max_val=LOADS * NE)
                    pe.wait_ge(weights_loaded, loaded)

                def body(j, n, b):
                    transpose_h(j - 1)
                    now = slot_of(j)
                    wait_weights(j)
                    gate_up(j, now)
                    transpose_z(j + 1, n + b, 1 - b)
                    down(j - 1, n - 1 + b, 1 - b, slot_of(j - 1))

                transpose_z(0, 0, 0)
                first = slot_of(0)
                wait_weights(0)
                gate_up(0, first)
                transpose_z(1, 0, 1)
                with pe.Fori(0, BLOCKS // 2) as k:
                    body(2 * k + 1, k, 1)
                    body(2 * k + 2, k + 1, 0)
                transpose_h(BLOCKS - 1)
                down(BLOCKS - 1, BLOCKS // 2, 0, slot_of(BLOCKS - 1))

            @block.scalar
            def _(act):
                def high_h(j):
                    act.wait_ge(filled[HT], j + 1)
                    nc.scalar.activation(ht_hi[:, :, :].rearrange("p f n -> p (f n)"), psum[HT][:, 0:FP], ACT.Copy).then_inc(ht_high, 1)

                def gate(j):
                    act.wait_ge(filled[GATE], j + 1)
                    act.wait_ge(drained[UP], j + 1)
                    nc.scalar.activation(silu_g[:, :], psum[GATE][:, 0:FD], ACT.Silu).then_inc(drained[GATE], 1)

                def high_z(j):
                    act.wait_ge(filled[ZT], j + 1)
                    nc.scalar.activation(zt_hi[:, :, :].rearrange("p k n -> p (k n)"), psum[ZT][:, :], ACT.Copy).then_inc(zt_high, 1)

                high_z(0)
                gate(0)
                high_z(1)
                with act.Fori(1, BLOCKS) as j:
                    high_h(j - 1)
                    gate(j)
                    high_z(j + 1)
                high_h(BLOCKS - 1)

            @block.vector
            def _(dve):
                for i in range(6):
                    nc.vector.nop().then_inc(drained[i], 1)
                dve.wait_ge(sorted_filled, 1)
                nc.vector.tensor_copy(share_of[:, :], psum[SORTED][:, COLS:2 * COLS])
                nc.vector.tensor_copy(row_of[:, :], psum[SORTED][:, 0:COLS]).then_inc(table_ready, 1)
                dve.wait_ge(table_ready, 1)

                def low_z(j):
                    dve.wait_ge(zt_high, j + 1)
                    nc.vector.tensor_tensor(zt_lo[:, :, :].rearrange("p k n -> p (k n)"), psum[ZT][:, :],
                                            zt_hi[:, :, :].rearrange("p k n -> p (k n)").bitcast(F32), ALU.subtract).then_inc(drained[ZT], 1)

                def low_h(j):
                    dve.wait_ge(ht_high, j + 1)
                    nc.vector.tensor_tensor(ht_lo[:, :, :].rearrange("p f n -> p (f n)"), psum[HT][:, 0:FP],
                                            ht_hi[:, :, :].rearrange("p f n -> p (f n)").bitcast(F32), ALU.subtract).then_inc(drained[HT], 1)

                def multiply(j):
                    dve.wait_ge(drained[GATE], j + 2)
                    dve.wait_ge(filled[UP], j + 1)
                    nc.vector.tensor_tensor(hid[:, 0:FD], silu_g[:, :], psum[UP][:, 0:FD], ALU.mult).then_inc(drained[UP], 1)

                def weigh(j, n, b, first):
                    dve.wait_ge(filled[OUT[b]], n + 1)
                    if not first:
                        dve.wait_ge(added, 16 * (j - 1))
                    nc.vector.tensor_tensor(result[b][:, :], psum[OUT[b]][:, :], share_of[:, bass.ds(j, 1)].to_broadcast([P, D]),
                                            ALU.mult).then_inc(drained[OUT[b]], 1)

                def body(j, n, b, first):
                    low_h(j - 1)
                    multiply(j)
                    low_z(j + 1)
                    weigh(j - 1, n - 1 + b, 1 - b, first)

                low_z(0)
                multiply(0)
                low_z(1)
                body(1, 0, 1, True)
                body(2, 1, 0, True)
                with dve.Fori(1, BLOCKS // 2) as k:
                    body(2 * k + 1, k, 1, False)
                    body(2 * k + 2, k + 1, 0, False)
                low_h(BLOCKS - 1)
                weigh(BLOCKS - 1, BLOCKS // 2, 0, False)


NAMES = {"x": "x", "cond": "itok_B_1_198", "adapter": "itok_B_0_6", "cond_w": "L0_cond_weights",
         "gate_cp": "L0_ffn_gate_cp", "up_cp": "L0_ffn_up_cp", "down_cp": "L0_ffn_down_cp",
         "W": "L1_cond_W", "A": "L1_cond_A", "Bm": "L1_cond_Bm", "scalings": "L1_cond_scalings",
         "router_w": "L1_ffn_gate_w", "gate_proj": "L1_ffn_gate_proj", "up_proj": "L1_ffn_up_proj", "down_proj": "L1_ffn_down_proj"}


def kernel(**inputs):
    import concourse.bacc as bacc
    from concourse.bass_utils import run_bass_kernel_spmd

    nc = bacc.Bacc("TRN2", target_bir_lowering=False, num_devices=1)
    arrays = {name: np.ascontiguousarray(inputs[key]) for name, key in NAMES.items()}
    arrays.update(spline_constants())
    arrays.update(index_constants())
    io = {name: nc.dram_tensor(f"in_{name}", a.shape, mybir.dt.from_np(a.dtype), kind="ExternalInput").ap()
          for name, a in arrays.items()}
    io["out"] = nc.dram_tensor("out", [TOKP, D], F32, kind="ExternalOutput").ap()
    build(nc, io)
    result = run_bass_kernel_spmd(nc, [{f"in_{name}": a for name, a in arrays.items()}], core_ids=[0])
    return result.results[0]["out"][0:TOK].reshape(BATCH, SEQ, D)
```
